# Optimizing a Trainium2 kernel written in Bass

```python
import numpy as np
import jax
import jax.numpy as jnp

def _softmax(x, axis=-1):
    return jax.nn.softmax(x, axis=axis)

def _gelu(x):
    return jax.nn.gelu(x, approximate=True)

def _silu(x):
    return jax.nn.silu(x)

def _sigmoid(x):
    return jax.nn.sigmoid(x)

def _layernorm(x, axis=-1, eps=1e-05):
    m = jnp.mean(x, axis=axis, keepdims=True)
    v = jnp.var(x, axis=axis, keepdims=True)
    return (x - m) / jnp.sqrt(v + eps)

def _scatter_add(tgt, idx, src, axis=0):
    return tgt.at[idx].add(src)

def _segment_sum(src, seg, n):
    return jax.ops.segment_sum(src, seg, n)
kernel_name = 'mk_macaron_d2_jaxref_r8_9ca971'

def setup_inputs(seed: int=0):
    np.random.seed(seed)
    _w = jnp.asarray

    def _L0_attn_setup():
        import jax, jax.numpy as jnp
        import numpy as np
        DM = 128
        NH = 16
        key = jax.random.key(seed)
        ks = jax.random.split(key, 9)
        B, S = (8, 128)
        sc = 1.0 / np.sqrt(DM)
        return {'x': jax.random.normal(ks[0], (B, S, DM), jnp.float32), 'Wq': jax.random.normal(ks[1], (DM, DM), jnp.float32) * sc, 'bq': jax.random.normal(ks[2], (DM,), jnp.float32) * 0.02, 'Wk': jax.random.normal(ks[3], (DM, DM), jnp.float32) * sc, 'bk': jax.random.normal(ks[4], (DM,), jnp.float32) * 0.02, 'Wv': jax.random.normal(ks[5], (DM, DM), jnp.float32) * sc, 'bv': jax.random.normal(ks[6], (DM,), jnp.float32) * 0.02, 'Wo': jax.random.normal(ks[7], (DM, DM), jnp.float32) * sc, 'bo': jax.random.normal(ks[8], (DM,), jnp.float32) * 0.02}
    _L0_attn_in = _L0_attn_setup()

    def _L0_ffn_setup():
        import jax, jax.numpy as jnp
        import numpy as np
        B, S, H = (2, 256, 128)
        I = 64
        E_R, E_Z = (32, 8)
        E_T = E_R + E_Z
        K = 6
        SCALE = 2.5
        W_INIT = 0.02
        key = jax.random.key(seed)
        k0, k1, k2, k3 = jax.random.split(key, 4)
        return {'hidden_states': jax.random.normal(k0, (B, S, H), jnp.float32), 'classifier_weight': jax.random.normal(k1, (E_T, H), jnp.float32) * W_INIT, 'e_score_correction_bias': jnp.zeros((E_T,), jnp.float32), 'gate_up_proj': jax.random.normal(k2, (E_T, 2 * I, H), jnp.float32) * W_INIT, 'down_proj': jax.random.normal(k3, (E_R, H, I), jnp.float32) * W_INIT}
    _L0_ffn_in = _L0_ffn_setup()

    def _L1_attn_setup():
        import jax, jax.numpy as jnp
        import numpy as np
        import math
        DIM_EMB = 128
        DIM_QK = 128
        DIM_V = 128
        NORM_FACT = 1.0 / math.sqrt(DIM_EMB)
        key = jax.random.key(seed)
        k0, k1, k2, k3 = jax.random.split(key, 4)
        x = jax.random.normal(k0, (4, 512, DIM_EMB), dtype=jnp.float32)
        s = 1.0 / math.sqrt(DIM_EMB)
        Wq = jax.random.uniform(k1, (DIM_QK, DIM_EMB), jnp.float32, -s, s)
        Wk = jax.random.uniform(k2, (DIM_QK, DIM_EMB), jnp.float32, -s, s)
        Wv = jax.random.uniform(k3, (DIM_V, DIM_EMB), jnp.float32, -s, s)
        return {'x': x, 'Wq': Wq, 'Wk': Wk, 'Wv': Wv}
    _L1_attn_in = _L1_attn_setup()

    def _L1_ffn_setup():
        import jax, jax.numpy as jnp
        import numpy as np
        DIM = 128
        HIDDEN = 384
        SCALE = 1.0 / 127.0

        def _dequant(w_int, dtype):
            return w_int.astype(dtype) * jnp.asarray(SCALE, dtype)
        key = jax.random.key(seed)
        k_x, k_g, k_u, k_d = jax.random.split(key, 4)
        x = jax.random.normal(k_x, (4, 256, DIM), dtype=jnp.float32)
        w_gate = jax.random.randint(k_g, (HIDDEN, DIM), -127, 128, dtype=jnp.int32)
        w_up = jax.random.randint(k_u, (HIDDEN, DIM), -127, 128, dtype=jnp.int32)
        w_down = jax.random.randint(k_d, (DIM, HIDDEN), -127, 128, dtype=jnp.int32)
        return {'x': x, 'w_gate': w_gate, 'w_up': w_up, 'w_down': w_down}
    _L1_ffn_in = _L1_ffn_setup()
    _d = {'L0_attn_x': _L0_attn_in['x'], 'L0_attn_Wq': _L0_attn_in['Wq'], 'L0_attn_bq': _L0_attn_in['bq'], 'L0_attn_Wk': _L0_attn_in['Wk'], 'L0_attn_bk': _L0_attn_in['bk'], 'L0_attn_Wv': _L0_attn_in['Wv'], 'L0_attn_bv': _L0_attn_in['bv'], 'L0_attn_Wo': _L0_attn_in['Wo'], 'L0_attn_bo': _L0_attn_in['bo'], 'L0_ffn_classifier_weight': _L0_ffn_in['classifier_weight'], 'L0_ffn_e_score_correction_bias': _L0_ffn_in['e_score_correction_bias'], 'L0_ffn_gate_up_proj': _L0_ffn_in['gate_up_proj'], 'L0_ffn_down_proj': _L0_ffn_in['down_proj'], 'L1_attn_Wq': _L1_attn_in['Wq'], 'L1_attn_Wk': _L1_attn_in['Wk'], 'L1_attn_Wv': _L1_attn_in['Wv'], 'L1_ffn_w_gate': _L1_ffn_in['w_gate'], 'L1_ffn_w_up': _L1_ffn_in['w_up'], 'L1_ffn_w_down': _L1_ffn_in['w_down']}
    _x0 = _d['L0_attn_x']
    _d['L0_attn_x'] = jax.random.normal(jax.random.fold_in(jax.random.key(seed), 1), (16, 512, 128), dtype=_x0.dtype)
    del _x0
    return _d

def reference(L0_attn_x, L0_attn_Wq, L0_attn_bq, L0_attn_Wk, L0_attn_bk, L0_attn_Wv, L0_attn_bv, L0_attn_Wo, L0_attn_bo, L0_ffn_classifier_weight, L0_ffn_e_score_correction_bias, L0_ffn_gate_up_proj, L0_ffn_down_proj, L1_attn_Wq, L1_attn_Wk, L1_attn_Wv, L1_ffn_w_gate, L1_ffn_w_up, L1_ffn_w_down):

    def _L0_attn_ref(x, Wq, bq, Wk, bk, Wv, bv, Wo, bo):
        import jax, jax.numpy as jnp
        import numpy as np
        DM = 128
        NH = 16
        B, S, dm = x.shape
        H = NH
        dk = dm // H
        Q = (x @ Wq.T + bq).reshape(B, S, H, dk)
        K = (x @ Wk.T + bk).reshape(B, S, H, dk)
        V = (x @ Wv.T + bv).reshape(B, S, H, dk)
        scores = jnp.einsum('bqhd,bkhd->hbqk', Q, K)
        attn = jax.nn.softmax(scores, axis=1)
        heads = jnp.einsum('hbqk,bkhd->bqhd', attn, V).reshape(B, S, dm)
        return heads @ Wo.T + bo

    def _L0_ffn_ref(hidden_states, classifier_weight, e_score_correction_bias, gate_up_proj, down_proj):
        import jax, jax.numpy as jnp
        import numpy as np
        B, S, H = (2, 256, 128)
        I = 64
        E_R, E_Z = (32, 8)
        E_T = E_R + E_Z
        K = 6
        SCALE = 2.5
        W_INIT = 0.02
        orig_shape = hidden_states.shape
        x = hidden_states.reshape(-1, H).astype(jnp.float32)
        T = x.shape[0]
        logits = x @ classifier_weight.T
        scores = jax.nn.softmax(logits, axis=-1)
        _, topk_idx = jax.lax.top_k(scores + e_score_correction_bias[None, :], K)
        topk_w = jnp.take_along_axis(scores, topk_idx, axis=1) * SCALE
        w_full = jnp.zeros((T, E_T), jnp.float32).at[jnp.arange(T)[:, None], topk_idx].add(topk_w)
        zero_w = w_full[:, E_R:].sum(axis=-1, keepdims=True)
        out0 = x * zero_w
        routed_w = w_full[:, :E_R].T

        def body(out, xs):
            Wgu, Wd, we = xs
            gate, up = jnp.split(x @ Wgu.T, 2, axis=-1)
            y = jax.nn.silu(gate) * up @ Wd.T
            return (out + we[:, None] * y, None)
        out, _ = jax.lax.scan(body, out0, (gate_up_proj[:E_R], down_proj, routed_w))
        return out.reshape(orig_shape).astype(hidden_states.dtype)

    def _L1_attn_ref(x, Wq, Wk, Wv):
        import jax, jax.numpy as jnp
        import numpy as np
        import math
        DIM_EMB = 128
        DIM_QK = 128
        DIM_V = 128
        NORM_FACT = 1.0 / math.sqrt(DIM_EMB)
        q = jnp.einsum('bne,de->bnd', x, Wq)
        k = jnp.einsum('bne,de->bnd', x, Wk)
        v = jnp.einsum('bne,de->bnd', x, Wv)
        logits = jnp.einsum('bnd,bmd->bnm', q, k)
        score = jax.nn.softmax(logits, axis=-1) * NORM_FACT
        att = jnp.einsum('bnm,bmv->bnv', score, v)
        return att

    def _L1_ffn_ref(x, w_gate, w_up, w_down):
        import jax, jax.numpy as jnp
        import numpy as np
        DIM = 128
        HIDDEN = 384
        SCALE = 1.0 / 127.0

        def _dequant(w_int, dtype):
            return w_int.astype(dtype) * jnp.asarray(SCALE, dtype)
        wg = _dequant(w_gate, x.dtype)
        wu = _dequant(w_up, x.dtype)
        wd = _dequant(w_down, x.dtype)
        gate = jnp.einsum('bsd,hd->bsh', x, wg)
        up = jnp.einsum('bsd,hd->bsh', x, wu)
        h = jax.nn.silu(gate) * up
        return jnp.einsum('bsh,dh->bsd', h, wd)
    x = L0_attn_x
    x = x + 0.5 * _L0_ffn_ref(_layernorm(x, axis=-1), L0_ffn_classifier_weight, L0_ffn_e_score_correction_bias, L0_ffn_gate_up_proj, L0_ffn_down_proj)
    x = x + _L0_attn_ref(_layernorm(x, axis=-1), L0_attn_Wq, L0_attn_bq, L0_attn_Wk, L0_attn_bk, L0_attn_Wv, L0_attn_bv, L0_attn_Wo, L0_attn_bo)
    x = x + 0.5 * _L0_ffn_ref(_layernorm(x, axis=-1), L0_ffn_classifier_weight, L0_ffn_e_score_correction_bias, L0_ffn_gate_up_proj, L0_ffn_down_proj)
    x = x + 0.5 * _L1_ffn_ref(_layernorm(x, axis=-1), L1_ffn_w_gate, L1_ffn_w_up, L1_ffn_w_down)
    x = x + _L1_attn_ref(_layernorm(x, axis=-1), L1_attn_Wq, L1_attn_Wk, L1_attn_Wv)
    x = x + 0.5 * _L1_ffn_ref(_layernorm(x, axis=-1), L1_ffn_w_gate, L1_ffn_w_up, L1_ffn_w_down)
    return x

_drawn_inputs = setup_inputs


def setup_inputs(seed=0):
    import zlib

    import numpy as np

    out = dict(_drawn_inputs(seed))
    spreads = {'L0_ffn_e_score_correction_bias': (0.0, 0.688)}
    factors = {'L0_attn_bo': 8.0,
     'L0_ffn_classifier_weight': 8.0,
     'L0_ffn_gate_up_proj': 8.0,
     'L0_ffn_down_proj': 8.0,
     'L1_attn_Wq': 64.0,
     'L1_attn_Wk': 64.0,
     'L1_attn_Wv': 64.0}
    for name, (base, spread) in spreads.items():
        noise = np.random.default_rng([zlib.crc32(name.encode()), seed]).standard_normal(out[name].shape)
        drawn = base * np.exp(spread * noise) if base else spread * noise
        out[name] = jnp.asarray(drawn.astype(out[name].dtype))
    for name, factor in factors.items():
        out[name] = (out[name] * factor).astype(out[name].dtype)
    return out
```

```python
from contextlib import ExitStack

import numpy as np

import concourse.bass as bass
from concourse import mybir

F32 = mybir.dt.float32
F32R = mybir.dt.float32r
BF16 = mybir.dt.bfloat16
I32 = mybir.dt.int32
ALU = mybir.AluOpType
ACT = mybir.ActivationFunctionType
AX = mybir.AxisListType

P = 128
BATCH, SEQ = 16, 512
TOKENS = BATCH * SEQ
TILE = 512
TILES = TOKENS // TILE
CH = TILE // P
EPS = 1e-5

ROUTED, ZERO, TOPK = 32, 8, 6
EXPERTS = ROUTED + ZERO
INNER = 64
PAIRS = ROUTED // 2
ROUTE_SCALE = 2.5 * 0.5
HIDDEN = 384
HCH = HIDDEN // P
DEQUANT = 1.0 / 127.0
SENTINEL = -3.0e38

HEADS, DK = 16, 8
TERMS = 8
STACK = TERMS * DK
NORM = 1.0 / float(np.sqrt(128.0))


def wait(eng, sem, value):
    if isinstance(value, int) and value <= 0:
        return
    eng.wait_ge(sem, value)


def wait_first(eng, sem, value):
    if isinstance(value, int):
        return wait(eng, sem, value)
    value = eng.snap(value)
    eng.wait_ge(sem, 1)
    eng.wait_ge(sem, value)


class Chain:

    def __init__(self, eng, sem, per):
        self.eng, self.sem, self.per, self.at = eng, sem, per, 0

    def tile(self, t):
        self.base, self.at = t * self.per, 0

    def link(self, ins):
        self.at += 1
        ins.then_inc(self.sem, 1)
        self.eng.wait_ge(self.sem, self.base + self.at)

    def end(self):
        assert self.at == self.per, self.at


def column(ap, t, width=TILE):
    if isinstance(t, int):
        return ap[:, t * width:(t + 1) * width]
    return ap[:, bass.ds(t * width, width)]


def chunks(ap):
    return ap.rearrange("p (c n) -> p c n", c=CH)


def over(ap, n):
    return ap.unsqueeze(2).broadcast_to([ap.shape[0], ap.shape[1], n])


class Memory:

    def __init__(self, nc, ctx, prefix):
        self.nc, self.ctx, self.prefix, self.semaphores = nc, ctx, prefix, []

    def sb(self, name, shape, dtype):
        return self.ctx.enter_context(self.nc.sbuf_tensor(self.prefix + name, shape, dtype))

    def ps(self, name, shape=(P, 512), dtype=F32):
        return self.ctx.enter_context(self.nc.psum_tensor(self.prefix + name, list(shape), dtype))

    def sem(self, name):
        semaphore = self.ctx.enter_context(self.nc.semaphore(self.prefix + name))
        self.semaphores.append(semaphore)
        return semaphore

    def sems(self, names):
        return [self.sem(name) for name in names.split()]

    def block(self):
        self.ctx.callback(self.clear)
        return self.ctx.enter_context(self.nc.Block())

    def clear(self):
        with self.nc.Block() as clearing:
            @clearing.gpsimd
            def _(pool):
                for semaphore in self.semaphores:
                    pool.sem_clear(semaphore)


def over_tiles(eng, body):
    body(0, 0)
    body(1, 1)
    with eng.Fori(1, TILES // 2 - 1) as i:
        body(i * 2, 0)
        body(i * 2 + 1, 1)
    body(TILES - 2, 0)
    body(TILES - 1, 1)


def is_last(t):
    return isinstance(t, int) and t == TILES - 1


def is_first(t):
    return isinstance(t, int) and t == 0


class Kept:

    def __init__(self, m):
        def parts(name, width):
            return (m.sb(name + "_high", [P, width], F32R), m.sb(name + "_low", [P, width], F32R))

        self.xT = m.sb("xT", [P, TOKENS], F32)
        self.wg, self.wu = parts("wg", PAIRS * P), parts("wu", PAIRS * P)
        self.wd = parts("wd", PAIRS * P)
        self.ffn = parts("ffn", 3 * HIDDEN)
        self.proj = parts("proj", PROJECTIONS * P)
        self.wc = m.sb("wc", [P, EXPERTS], F32)
        self.bias = m.sb("bias", [P, CH, EXPERTS], F32)
        self.sel = m.sb("sel", [3 * ROUTED, PAIRS * P], BF16)
        self.ident = m.sb("ident", [P, P], F32)
        self.identb = m.sb("identb", [P, P], BF16)
        self.biases = m.sb("biases", [P, 4], F32)
        self.minus_half = m.sb("minus_half", [P, CH], F32)
        self.eps = m.sb("eps", [P, CH], F32)
        self.wv_full = m.sb("wv_full", [P, 2 * P], F32)
        self.bv_row = m.sb("bv_row", [P, P], F32)
        self.x_dram = m.nc.dram_tensor("x_kept", (P, TOKENS), F32).ap()
        self.heads_dram = m.nc.dram_tensor("heads_kept", (P, TOKENS), F32).ap()
        self.thirds_dram = [m.nc.dram_tensor(f"thirds_{x}", (3, P, CH, BATCH, P), BF16).ap()
                            for x in "qk"]

    def ffn_part(self, n):
        return [part[:, n * HIDDEN:(n + 1) * HIDDEN] for part in self.ffn]

    def proj_part(self, n):
        return [part[:, n * P:(n + 1) * P] for part in self.proj]


PROJECTIONS = 7


def load_block(nc, k, ins):
    with ExitStack() as ctx:
        m = Memory(nc, ctx, "ld_")
        raw = [m.sb(f"raw{i}", [P, PAIRS * P], F32) for i in range(2)]
        ints = m.sb("ints", [P, 3 * HIDDEN], I32)
        loaded = m.sems("loaded0 loaded1")
        ints_loaded, dequantised, const_loaded, x_loaded, high_done, low_done, half_set = m.sems(
            "ints_loaded dequantised const_loaded x_loaded high_done low_done half_set")
        todo = [(ins["wg"], k.wg), (ins["wu"], k.wu), (ins["wd"], k.wd), (ins["proj"], k.proj),
                (None, k.ffn)]
        consts = [("wc", k.wc), ("sel", k.sel), ("ident", k.ident), ("identb", k.identb),
                  ("biases", k.biases), ("wv_full", k.wv_full)]
        block = m.block()

        @block.sync
        def _(sync):
            sync.dma_start(ints[:, :], ins["ffn"]).then_inc(ints_loaded, 16)
            for n, (src, parts) in enumerate(todo[:-1]):
                if n >= 2:
                    sync.wait_ge(low_done, n - 1)
                sync.dma_start(raw[n % 2][:, 0:parts[0].shape[1]],
                               src).then_inc(loaded[n % 2], 16)

        @block.scalar
        def _(act):
            act.dma_start(k.xT[:, :], ins["xT"]).then_inc(x_loaded, 16)
            for c in range(CH):
                act.dma_start(k.bias[:, c, :],
                              ins["bias"].partition_broadcast(P)).then_inc(const_loaded, 16)
            act.dma_start(k.bv_row[:, :], ins["bv"].partition_broadcast(P)).then_inc(const_loaded,
                                                                                     16)
            for name, tensor in consts:
                act.dma_start(tensor[:, :], ins[name]).then_inc(const_loaded, 16)
            for n, (src, (high, _)) in enumerate(todo):
                if src is None:
                    act.wait_ge(dequantised, 1)
                else:
                    act.wait_ge(loaded[n % 2], 16 * (n // 2 + 1))
                nc.scalar.activation(high[:, :], raw[n % 2][:, 0:high.shape[1]],
                                     ACT.Copy).then_inc(high_done, 1)
            act.wait_ge(const_loaded, 16 * (CH + 1 + len(consts)))
            act.wait_ge(x_loaded, 16)

        @block.vector
        def _(dve):
            nc.vector.memset(k.minus_half[:, :], -0.5).then_inc(half_set, 1)
            nc.vector.memset(k.eps[:, :], EPS).then_inc(half_set, 1)
            for n, (src, (high, low)) in enumerate(todo):
                if src is None:
                    dve.wait_ge(ints_loaded, 16)
                    dve.wait_ge(low_done, n - 1)
                    nc.vector.tensor_scalar(raw[n % 2][:, 0:3 * HIDDEN], ints[:, :], DEQUANT, None,
                                            ALU.mult).then_inc(dequantised, 1)
                dve.wait_ge(high_done, n + 1)
                nc.vector.tensor_tensor(low[:, :], raw[n % 2][:, 0:high.shape[1]], high[:, :],
                                        ALU.subtract).then_inc(low_done, 1)


def three_passes(nc, out, w, x, start=True, stop=True):
    (wh, wl), (xh, xl) = w, x
    nc.tensor.matmul(out, wl, xh, start=start, stop=False, skip_group_check=True)
    nc.tensor.matmul(out, wh, xl, start=False, stop=False, skip_group_check=True)
    return nc.tensor.matmul(out, wh, xh, start=False, stop=stop, skip_group_check=True)



class Norm:

    def __init__(self, nc, k, m, bank):
        self.nc, self.k, self.bank = nc, k, bank
        self.xs = m.sb("xs", [P, TILE], F32)
        self.stats = m.sb("stats", [P, CH, 6], F32)
        self.mv = m.sb("mv", [P, CH, 2], F32)
        self.var = m.sb("var", [P, CH], F32)
        self.rstd = m.sb("rstd", [P, CH], F32)
        self.rows = [m.sb(f"rows{i}", [P, TILE], F32) for i in range(2)]
        self.full = m.sb("full", [P, TILE], F32)
        self.high = [m.sb(f"high{i}", [P, TILE], F32R) for i in range(2)]
        self.low = [m.sb(f"low{i}", [P, TILE], F32R) for i in range(2)]
        (self.x_copied, self.x_turned, self.stats_done, self.aggregated, self.var_done,
         self.rstd_done, self.normed, self.n_turned, self.n_copied, self.n_high,
         self.n_low) = m.sems("x_copied x_turned stats_done aggregated var_done rstd_done "
                              "normed n_turned n_copied n_high n_low")

    def copy_in(self, act, t):
        wait(act, self.x_turned, t)
        self.nc.scalar.activation(self.xs[:, :], column(self.k.xT, t),
                                  ACT.Copy).then_inc(self.x_copied, 1)

    def turn(self, pe, t):
        pe.wait_ge(self.x_copied, t + 1)
        wait(pe, self.n_copied, t)
        wait(pe, self.n_high, t)
        for c in range(CH):
            part = self.nc.tensor.transpose(self.bank[:, c * P:(c + 1) * P],
                                            self.xs[:, c * P:(c + 1) * P], self.k.ident[:, :])
        part.then_inc(self.x_turned, 1)

    def moments(self, dve, t):
        dve.wait_ge(self.x_turned, t + 1)
        wait(dve, self.aggregated, t)
        for c in range(CH):
            part = self.nc.vector.bn_stats(self.stats[:, c, :], self.bank[:, c * P:(c + 1) * P])
        part.then_inc(self.stats_done, 1)
        dve.wait_ge(self.stats_done, 1)
        dve.wait_ge(self.stats_done, t + 1)
        for c in range(CH):
            part = self.nc.vector.bn_aggr(self.mv[:, c, :], self.stats[:, c, :])
        part.then_inc(self.aggregated, 1)

    def deviation(self, pool, t):
        pool.wait_ge(self.aggregated, t + 1)
        self.nc.gpsimd.tensor_tensor(self.var[:, :], self.mv[:, :, 1], self.k.eps[:, :],
                                     ALU.add).then_inc(self.var_done, 1)
        pool.wait_ge(self.var_done, t + 1)
        self.nc.gpsimd.tensor_tensor(self.rstd[:, :], self.var[:, :], self.k.minus_half[:, :],
                                     ALU.pow).then_inc(self.rstd_done, 1)

    def norm_rows(self, dve, t, parity):
        dve.wait_ge(self.rstd_done, t + 1)
        wait(dve, self.n_turned, t - 1)
        for c in range(CH):
            part = self.nc.vector.tensor_scalar(
                self.rows[parity][:, c * P:(c + 1) * P], self.bank[:, c * P:(c + 1) * P],
                self.mv[:, c, 0:1], self.rstd[:, c:c + 1], ALU.subtract, ALU.mult)
        part.then_inc(self.normed, 1)

    def turn_back(self, pe, t, parity):
        pe.wait_ge(self.normed, t + 1)
        for c in range(CH):
            part = self.nc.tensor.transpose(self.bank[:, c * P:(c + 1) * P],
                                            self.rows[parity][:, c * P:(c + 1) * P],
                                            self.k.ident[:, :])
        part.then_inc(self.n_turned, 1)

    def cut_high(self, act, t, parity):
        act.wait_ge(self.n_turned, t + 1)
        wait(act, self.n_low, t)
        self.nc.scalar.activation(self.full[:, :], self.bank[:, :],
                                  ACT.Copy).then_inc(self.n_copied, 1)
        self.nc.scalar.activation(self.high[parity][:, :], self.bank[:, :],
                                  ACT.Copy).then_inc(self.n_high, 1)

    def cut_low(self, dve, t, parity):
        dve.wait_ge(self.n_copied, t + 1)
        dve.wait_ge(self.n_high, t + 1)
        self.nc.vector.tensor_tensor(self.low[parity][:, :], self.full[:, :],
                                     self.high[parity][:, :], ALU.subtract).then_inc(self.n_low, 1)


class Router:

    LINKS = 12

    def __init__(self, nc, k, m, norm):
        self.nc, self.k, self.norm, self.bank = nc, k, norm, norm.bank
        self.top = m.sb("top", [P, CH], F32)
        self.z = m.sb("z", [P, CH, EXPERTS], F32)
        self.e = m.sb("e", [P, CH, EXPERTS], F32)
        self.total = m.sb("total", [P, CH], F32)
        self.inverse = m.sb("inverse", [P, CH], F32)
        self.score = m.sb("score", [P, CH, EXPERTS], F32)
        self.biased = m.sb("biased", [P, CH, EXPERTS + 2], F32)
        self.best = m.sb("best", [P, CH, 8], F32)
        self.marked = m.sb("marked", [P, CH, EXPERTS + 2], F32)
        self.mask = m.sb("mask", [P, CH, EXPERTS], F32)
        self.weight = m.sb("weight", [P, CH, EXPERTS], F32)
        self.rest = m.sb("rest", [P, CH, ROUTED], F32)
        self.rest2 = m.sb("rest2", [P, CH, ROUTED], F32)
        self.thirds = m.sb("thirds", [P, CH, 3 * ROUTED], BF16)
        self.zero_weight = m.sb("zero_weight", [P, CH], F32)
        self.diagonal = [m.sb(f"diagonal{i}", [P, CH, P], F32) for i in range(2)]
        self.turned = [m.sb(f"turned{i}", [3 * ROUTED, TILE], BF16) for i in range(2)]
        (self.sentinels, self.logits_done, self.shifted, self.e_done, self.thirds_done,
         self.w_turned, self.w_copied, self.diagonal_done,
         self.biased_done, self.best_done, self.own) = m.sems("sentinels logits_done shifted e_done thirds_done w_turned w_copied "
                            "diagonal_done biased_done best_done route_own")

    def chain(self, dve):
        self.steps = Chain(dve, self.own, self.LINKS)

    def logits(self, pe, t):
        norm = self.norm
        pe.wait_ge(norm.n_copied, t + 1)
        pe.wait_ge(norm.n_high, t + 1)
        for c in range(CH):
            part = self.nc.tensor.matmul(self.bank[:, c * EXPERTS:(c + 1) * EXPERTS],
                                         norm.full[:, c * P:(c + 1) * P], self.k.wc[:, :],
                                         start=True, stop=True)
        part.then_inc(self.logits_done, 1)

    def shift(self, dve, t):
        logits = self.bank[:, 0:CH * EXPERTS].rearrange("p (c n) -> p c n", c=CH)
        self.steps.tile(t)
        dve.wait_ge(self.logits_done, t + 1)
        self.steps.link(self.nc.vector.tensor_reduce(self.top[:, :], logits, AX.X, ALU.max))
        wait(dve, self.e_done, t)
        self.nc.vector.tensor_tensor(self.z[:, :, :], logits, over(self.top[:, :], EXPERTS),
                                     ALU.subtract).then_inc(self.shifted, 1)

    def exponentials(self, act, t):
        act.wait_ge(self.shifted, t + 1)
        wait(act, self.thirds_done, t)
        self.nc.scalar.activation(self.e[:, :, :], self.z[:, :, :],
                                  ACT.Exp).then_inc(self.e_done, 1)

    def choose(self, dve, t):
        vector, link = self.nc.vector, self.steps.link
        real = self.biased[:, :, 0:EXPERTS]
        dve.wait_ge(self.e_done, t + 1)
        link(vector.tensor_reduce(self.total[:, :], self.e[:, :, :], AX.X, ALU.add))
        link(vector.reciprocal(self.inverse[:, :], self.total[:, :]))
        link(vector.tensor_tensor(self.score[:, :, :], self.e[:, :, :],
                                  over(self.inverse[:, :], EXPERTS), ALU.mult))
        vector.tensor_tensor(real, self.score[:, :, :], self.k.bias[:, :, :],
                             ALU.add).then_inc(self.biased_done, 1)
        dve.wait_ge(self.biased_done, 1)
        dve.wait_ge(self.biased_done, t + 1)
        for c in range(CH):
            part = vector.max(self.best[:, c, :], self.biased[:, c, 0:EXPERTS])
        link(part)
        vector.memset(self.best[:, :, TOPK:8], SENTINEL).then_inc(self.best_done, 1)
        dve.wait_ge(self.best_done, 1)
        dve.wait_ge(self.best_done, t + 1)
        for c in range(CH):
            part = vector.match_replace(self.marked[:, c, :], self.best[:, c, :],
                                        self.biased[:, c, :], -SENTINEL)
        link(part)
        link(vector.tensor_tensor(self.mask[:, :, :], self.marked[:, :, 0:EXPERTS], real,
                                  ALU.not_equal))
        link(vector.scalar_tensor_tensor(self.weight[:, :, :], self.mask[:, :, :], ROUTE_SCALE,
                                         self.score[:, :, :], ALU.mult, ALU.mult))

    def cut(self, dve, t):
        vector, link = self.nc.vector, self.steps.link
        routed = self.weight[:, :, 0:ROUTED]
        third = [self.thirds[:, :, i * ROUTED:(i + 1) * ROUTED] for i in range(3)]
        wait(dve, self.w_turned, t)
        wait(dve, self.diagonal_done, t)
        vector.tensor_reduce(self.zero_weight[:, :], self.weight[:, :, ROUTED:EXPERTS], AX.X,
                             ALU.add)
        link(vector.tensor_copy(third[0], routed))
        link(vector.tensor_tensor(self.rest[:, :, :], routed, third[0], ALU.subtract))
        link(vector.tensor_copy(third[1], self.rest[:, :, :]))
        link(vector.tensor_tensor(self.rest2[:, :, :], self.rest[:, :, :], third[1],
                                  ALU.subtract))
        vector.tensor_copy(third[2], self.rest2[:, :, :]).then_inc(self.thirds_done, 1)
        self.steps.end()

    def diagonals(self, pool, t, parity):
        pool.wait_ge(self.thirds_done, t + 1)
        for c in range(CH):
            part = self.nc.gpsimd.tensor_tensor(
                self.diagonal[parity][:, c, :], self.k.ident[:, :],
                self.zero_weight[:, c:c + 1].broadcast_to([P, P]), ALU.mult)
        part.then_inc(self.diagonal_done, 1)

    def turn(self, pe, t):
        bank = self.bank[:, :].bitcast(BF16)
        pe.wait_ge(self.thirds_done, t + 1)
        for c in range(CH):
            part = self.nc.tensor.transpose(bank[0:3 * ROUTED, c * P:(c + 1) * P],
                                            self.thirds[:, c, :], self.k.identb[:, :])
        part.then_inc(self.w_turned, 1)

    def copy_turned(self, act, t, parity):
        act.wait_ge(self.w_turned, t + 1)
        self.nc.scalar.activation(self.turned[parity][:, :],
                                  self.bank[:, :].bitcast(BF16)[0:3 * ROUTED, 0:TILE],
                                  ACT.Copy).then_inc(self.w_copied, 1)


def gated_block(nc, k, prefix, units, w_gate, w_up, w_down, routed):
    LAG = 2
    hold = 4 if routed else 3
    with ExitStack() as ctx:
        m = Memory(nc, ctx, prefix)
        gate = [m.ps(f"gate{i}") for i in range(2)]
        up = [m.ps(f"up{i}") for i in range(2)]
        y, bank = m.ps("y"), m.ps("bank")
        norm = Norm(nc, k, m, bank)
        gated = [m.sb(f"gated{i}", [P, TILE], F32) for i in range(2)]
        h = [m.sb(f"h{i}", [P, TILE], F32) for i in range(2)]
        h_high = [m.sb(f"h_high{i}", [P, TILE], F32R) for i in range(hold)]
        h_low = [m.sb(f"h_low{i}", [P, TILE], F32R) for i in range(hold)]
        (gate_done, up_done, silu_done, h_done, high_done, low_done, down_done, y_done,
         y_added) = m.sems("gate_done up_done silu_done h_done high_done low_done down_done "
                           "y_done y_added")
        if routed:
            share = [m.ps(f"share{i}") for i in range(2)]
            product = m.sb("product", [P, TILE], F32)
            product_done = m.sem("product_done")
            router = Router(nc, k, m, norm)
            at = dict(copy=0, turn=1, moments=2, deviation=2, rows=3, back=4, high=5, low=6,
                      logits=7, shift=8, exp=9, choose=10, cut=11, diagonals=11, w_turn=13,
                      w_copy=13)
        else:
            at = dict(copy=0, turn=0, moments=0, deviation=0, rows=0, back=1, high=1, low=1)
        block = m.block()

        @block.scalar
        def _(act):
            def high(n, u, slot):
                act.wait_ge(h_done, n + 1)
                wait(act, down_done, n - hold + 1)
                nc.scalar.activation(h_high[u % hold][:, :], h[slot][:, :],
                                     ACT.Copy).then_inc(high_done, 1)

            def prepare(s, t, parity):
                if s == "copy":
                    norm.copy_in(act, t)
                elif s == "high":
                    wait(act, up_done, units * (t - 1))
                    if routed:
                        wait(act, router.logits_done, t)
                    norm.cut_high(act, t, parity)
                elif s == "exp":
                    router.exponentials(act, t)
                elif s == "w_copy":
                    router.copy_turned(act, t, parity)

            steps = [s for s in ("copy", "high", "exp", "w_copy") if s in at]
            for s in steps:
                prepare(s, 0, 0)

            def tile(t, parity):
                for u in range(units):
                    n = t * units + u
                    slot = (parity * units + u) % 2
                    act.wait_ge(gate_done, n + 1)
                    wait(act, h_done, n - 1)
                    nc.scalar.activation(gated[slot][:, :], gate[slot][:, :],
                                         ACT.Silu).then_inc(silu_done, 1)
                    if u:
                        high(n - 1, u - 1, 1 - slot)
                    for s in steps:
                        if at[s] == u and not is_last(t):
                            prepare(s, t + 1, 1 - parity)
                high(n, u, slot)

            over_tiles(act, tile)

        @block.gpsimd
        def _(pool):
            def prepare(t, parity, s):
                if s == "deviation":
                    norm.deviation(pool, t)
                elif s == "diagonals":
                    wait(pool, y_done, t - 1)
                    router.diagonals(pool, t, parity)

            steps = [s for s in ("deviation", "diagonals") if s in at]
            for s in steps:
                prepare(0, 0, s)

            def tile(t, parity):
                for u in range(units):
                    n = t * units + u
                    slot = (parity * units + u) % 2
                    for s in steps:
                        if at[s] == u and not is_last(t):
                            prepare(t + 1, 1 - parity, s)
                    pool.wait_ge(high_done, n + 1)
                    nc.gpsimd.tensor_tensor(h_low[u % hold][:, :], h[slot][:, :],
                                            h_high[u % hold][:, :],
                                            ALU.subtract).then_inc(low_done, 1)

            over_tiles(pool, tile)

        @block.vector
        def _(dve):
            if routed:
                router.chain(dve)
                nc.vector.memset(router.biased[:, :, EXPERTS:EXPERTS + 2],
                                 SENTINEL).then_inc(router.sentinels, 1)
                dve.wait_ge(router.sentinels, 1)

            def prepare(s, t, parity):
                if s == "moments":
                    norm.moments(dve, t)
                elif s == "rows":
                    if routed:
                        wait(dve, y_done, t - 1)
                    norm.norm_rows(dve, t, parity)
                elif s == "low":
                    norm.cut_low(dve, t, parity)
                elif s == "shift":
                    router.shift(dve, t)
                elif s == "choose":
                    router.choose(dve, t)
                elif s == "cut":
                    router.cut(dve, t)

            steps = [s for s in ("moments", "rows", "low", "shift", "choose", "cut") if s in at]
            for s in steps:
                prepare(s, 0, 0)

            def add(t):
                if routed:
                    dve.wait_ge(y_done, t + 1)
                else:
                    dve.wait_ge(down_done, (t + 1) * units)
                nc.vector.scalar_tensor_tensor(column(k.xT, t), y[:, :], 1.0 if routed else 0.5,
                                               column(k.xT, t), ALU.mult,
                                               ALU.add).then_inc(y_added, 1)

            def tile(t, parity):
                for u in range(units):
                    n = t * units + u
                    slot = (parity * units + u) % 2
                    dve.wait_ge(silu_done, n + 1)
                    dve.wait_ge(up_done, n + 1)
                    if routed:
                        wait(dve, h_done, n)
                        nc.vector.tensor_tensor(product[:, :], gated[slot][:, :], up[slot][:, :],
                                                ALU.mult).then_inc(product_done, 1)
                        dve.wait_ge(product_done, n + 1)
                        wait(dve, low_done, n - 1)
                        nc.vector.tensor_tensor(h[slot][:, :], product[:, :], share[slot][:, :],
                                                ALU.mult).then_inc(h_done, 1)
                    else:
                        wait(dve, low_done, n - 1)
                        nc.vector.tensor_tensor(h[slot][:, :], gated[slot][:, :], up[slot][:, :],
                                                ALU.mult).then_inc(h_done, 1)
                    if u == LAG - 1 and not is_first(t):
                        add(t - 1)
                    for s in steps:
                        if at[s] == u and not is_last(t):
                            prepare(s, t + 1, 1 - parity)

            over_tiles(dve, tile)
            add(TILES - 1)

        @block.tensor
        def _(pe):
            def prepare(s, t, parity):
                if s == "turn":
                    if routed:
                        wait(pe, router.w_copied, t)
                    norm.turn(pe, t)
                elif s == "back":
                    norm.turn_back(pe, t, parity)
                elif s == "logits":
                    router.logits(pe, t)
                elif s == "w_turn":
                    router.turn(pe, t)

            def rows_of(w, u):
                return w[0][:, u * P:(u + 1) * P], w[1][:, u * P:(u + 1) * P]

            def down(t, u, parity):
                n = t * units + u
                if u == 0:
                    wait(pe, y_added, t)
                pe.wait_ge(high_done, n + 1)
                pe.wait_ge(low_done, n + 1)
                last = u == units - 1
                ins = three_passes(nc, y[:, :], rows_of(w_down, u),
                                   (h_high[u % hold][:, :], h_low[u % hold][:, :]),
                                   start=(u == 0), stop=(last and not routed))
                ins.then_inc(down_done, 1)
                if last:
                    if routed:
                        pe.wait_ge(router.diagonal_done, t + 1)
                        for c in range(CH):
                            ins = nc.tensor.matmul(y[:, c * P:(c + 1) * P],
                                                   norm.rows[parity][:, c * P:(c + 1) * P],
                                                   router.diagonal[parity][:, c, :],
                                                   start=False, stop=True, skip_group_check=True)
                        ins.then_inc(y_done, 1)

            steps = [s for s in ("turn", "back", "logits", "w_turn") if s in at]
            for s in steps:
                prepare(s, 0, 0)

            def tile(t, parity):
                x = (norm.high[parity][:, :], norm.low[parity][:, :])
                pe.wait_ge(norm.n_low, t + 1)
                pe.wait_ge(norm.n_high, t + 1)
                if routed:
                    pe.wait_ge(router.w_copied, t + 1)
                for u in range(units):
                    n = t * units + u
                    slot = (parity * units + u) % 2
                    wait(pe, silu_done, n - 1)
                    three_passes(nc, gate[slot][:, :], rows_of(w_gate, u),
                                 x).then_inc(gate_done, 1)
                    wait(pe, h_done, n - 1)
                    if routed:
                        nc.tensor.matmul(share[slot][:, :], k.sel[:, u * P:(u + 1) * P],
                                         router.turned[parity][:, :], start=True, stop=True)
                    three_passes(nc, up[slot][:, :], rows_of(w_up, u), x).then_inc(up_done, 1)
                    if u >= LAG:
                        down(t, u - LAG, parity)
                    elif not is_first(t):
                        down(t - 1, units - LAG + u, 1 - parity)
                    for s in steps:
                        if at[s] == u and not is_last(t):
                            prepare(s, t + 1, 1 - parity)

            over_tiles(pe, tile)
            for u in range(units - LAG, units):
                down(TILES - 1, u, (TILES - 1) % 2)


THIRDS_Q = ((0, 3), (1, 3), (2, 2))
PIECES = SEQ // P
HALF = P // 2
UNITS = 2 * PIECES
STEPS = HEADS * PIECES


def head_projection(nc, k, prefix):
    with ExitStack() as ctx:
        m = Memory(nc, ctx, prefix)
        norm = Norm(nc, k, m, m.ps("bank"))
        product = [[m.ps(f"{x}{i}") for i in range(2)] for x in "qk"]
        v_bank = m.ps("v")
        biased = [m.sb(f"biased{x}", [P, TILE], F32) for x in "qk"]
        rest = [m.sb(f"rest{x}", [P, TILE], F32) for x in "qk"]
        thirds = [[m.sb(f"thirds{x}{i}", [P, 3, TILE], BF16) for i in range(2)] for x in "qk"]
        x_saved, v_done, v_added = m.sems("x_saved v_done v_added")
        qk_done, full_done, first_done, rest_done, second_done, third_done = [
            [m.sem(f"{name}_{x}") for x in "qk"] for name in
            ("qk_done", "full_done", "first_done", "rest_done", "second_done", "third_done")]
        stored = [[m.sem(f"stored_{x}{i}") for i in range(2)] for x in "qk"]
        block = m.block()

        @block.sync
        def _(sync):
            sync.dma_start(k.x_dram, k.xT[:, :]).then_inc(x_saved, 16)

            def tile(t, parity):
                for x in range(2):
                    wait_first(sync, third_done[x], t + 1)
                    for n in range(3):
                        out = k.thirds_dram[x][n]
                        at = out[:, :, t, :] if isinstance(t, int) else out[:, :, bass.ds(t, 1), :]
                        sync.dma_start(at, thirds[x][parity][:, n, :].rearrange(
                            "p (c q) -> p c q", c=PIECES)).then_inc(stored[x][parity], 16)

            over_tiles(sync, tile)
            for x in range(2):
                for parity in range(2):
                    sync.wait_ge(stored[x][parity], 16 * 3 * TILES // 2)

        @block.scalar
        def _(act):
            def tile(t, parity):
                if not is_last(t):
                    norm.copy_in(act, t + 1)
                for x in range(2):
                    act.wait_ge(qk_done[x], t + 1)
                    wait(act, rest_done[x], t)
                    nc.scalar.activation(biased[x][:, :], product[x][parity][:, :], ACT.Identity,
                                         bias=k.biases[:, x:x + 1]).then_inc(full_done[x], 1)
                    if isinstance(t, int):
                        wait(act, stored[x][parity], 48 * (t // 2))
                    else:
                        act.wait_ge(stored[x][parity], (t - parity) * 24)
                    nc.scalar.activation(thirds[x][parity][:, 0, :], product[x][parity][:, :],
                                         ACT.Identity,
                                         bias=k.biases[:, x:x + 1]).then_inc(first_done[x], 1)
                if not is_last(t):
                    wait(act, v_done, t + 1)
                    norm.cut_high(act, t + 1, 1 - parity)

            norm.copy_in(act, 0)
            norm.cut_high(act, 0, 0)
            over_tiles(act, tile)

        @block.gpsimd
        def _(pool):
            def tile(t, parity):
                if not is_last(t):
                    norm.deviation(pool, t + 1)
                for x in range(2):
                    pool.wait_ge(second_done[x], t + 1)
                    nc.gpsimd.tensor_tensor(thirds[x][parity][:, 2, :], rest[x][:, :],
                                            thirds[x][parity][:, 1, :],
                                            ALU.subtract).then_inc(third_done[x], 1)

            norm.deviation(pool, 0)
            over_tiles(pool, tile)

        @block.vector
        def _(dve):
            def tile(t, parity):
                for x in range(2):
                    dve.wait_ge(full_done[x], t + 1)
                    dve.wait_ge(first_done[x], t + 1)
                    wait(dve, third_done[x], t)
                    nc.vector.tensor_tensor(rest[x][:, :], biased[x][:, :],
                                            thirds[x][parity][:, 0, :],
                                            ALU.subtract).then_inc(rest_done[x], 1)
                    dve.wait_ge(rest_done[x], t + 1)
                    nc.vector.tensor_copy(thirds[x][parity][:, 1, :],
                                          rest[x][:, :]).then_inc(second_done[x], 1)
                if not is_last(t):
                    norm.moments(dve, t + 1)
                dve.wait_ge(v_done, t + 1)
                dve.wait_ge(x_saved, 16)
                dve.wait_ge(norm.x_copied, t + 1)
                nc.vector.tensor_tensor(chunks(column(k.xT, t)), chunks(v_bank[:, :]),
                                        k.bv_row[:, :].unsqueeze(1).broadcast_to([P, CH, P]),
                                        ALU.add).then_inc(v_added, 1)
                if not is_last(t):
                    norm.norm_rows(dve, t + 1, 1 - parity)
                    norm.cut_low(dve, t + 1, 1 - parity)

            norm.moments(dve, 0)
            norm.norm_rows(dve, 0, 0)
            norm.cut_low(dve, 0, 0)
            over_tiles(dve, tile)

        @block.tensor
        def _(pe):
            def tile(t, parity):
                pe.wait_ge(norm.n_copied, t + 1)
                pe.wait_ge(norm.n_high, t + 1)
                pe.wait_ge(norm.n_low, t + 1)
                wait(pe, v_added, t)
                for c in range(CH):
                    part = nc.tensor.matmul(v_bank[:, c * P:(c + 1) * P],
                                            norm.full[:, c * P:(c + 1) * P], k.wv_full[:, 0:P],
                                            start=True, stop=True)
                part.then_inc(v_done, 1)
                for x in range(2):
                    wait(pe, first_done[x], t - 1)
                    wait(pe, full_done[x], t - 1)
                    three_passes(nc, product[x][parity][:, :], k.proj_part(x),
                                 (norm.high[parity][:, :], norm.low[parity][:, :])
                                 ).then_inc(qk_done[x], 1)
                if not is_last(t):
                    norm.turn(pe, t + 1)
                    norm.turn_back(pe, t + 1, 1 - parity)

            norm.turn(pe, 0)
            norm.turn_back(pe, 0, 0)
            over_tiles(pe, tile)


def batch_attention(nc, k, prefix):
    BUFS = 4
    LAG = 3
    with ExitStack() as ctx:
        m = Memory(nc, ctx, prefix)
        score = [m.ps(f"score{i}", (P, BATCH * HALF)) for i in range(2)]
        heads_bank = m.ps("heads")
        keys = m.sb("keys", [STACK, PIECES, BATCH * P], BF16)
        queries = m.sb("queries", [STACK, 2, BATCH * P], BF16)
        e = [m.sb(f"e{i}", [P, BATCH, P], F32) for i in range(BUFS)]
        top = [m.sb(f"top{i}", [P, HALF], F32R) for i in range(2)]
        total = m.sb("total", [P, P], F32)
        inverse = [m.sb(f"inverse{i}", [P, P], F32) for i in range(2)]
        values = m.sb("values", [P, PIECES, BATCH, 32], F32)
        heads_out = [m.sb(f"heads_out{i}", [P, TILE], F32) for i in range(2)]
        minus = m.sb("minus", [P, P], F32R)
        (minus_set, scored, top_done, shifted, e_done, summed, inverse_done, normed, v_copied,
         weighted, copied) = m.sems("minus_set scored top_done shifted e_done summed "
                                    "inverse_done normed v_copied weighted copied")
        keys_loaded = [m.sem(f"keys_loaded{i}") for i in range(PIECES)]
        queries_loaded = [m.sem(f"queries_loaded{i}") for i in range(2)]
        stored = [m.sem(f"stored{i}") for i in range(2)]
        v = k.xT[:, :].rearrange("p (b c n) -> p b c n", b=BATCH, c=PIECES)
        block = m.block()

        def rows(head):
            return slice(head * DK, (head + 1) * DK) if isinstance(head, int) else \
                bass.ds(head * DK, DK)

        @block.sync
        def _(sync):
            def load_keys(head, c):
                first = 0
                for count in (3, 3, 2):
                    for n in range(count):
                        sync.dma_start(keys[first:first + DK, c, :],
                                       k.thirds_dram[1][n, rows(head), c, :, :].rearrange(
                                           "d b q -> d (b q)")).then_inc(keys_loaded[c], 16)
                        first += DK

            def load_queries(head, c):
                first = 0
                for n, count in THIRDS_Q:
                    for _ in range(count):
                        sync.dma_start(queries[first:first + DK, c % 2, :],
                                       k.thirds_dram[0][n, rows(head), c, :, :].rearrange(
                                           "d b q -> d (b q)")).then_inc(queries_loaded[c % 2], 16)
                        first += DK

            def store(head, c):
                step = head * PIECES + c
                wait_first(sync, copied, step + 1)
                out = k.heads_dram[rows(head), :].rearrange("d (j g c q) -> d g j c q",
                                                            g=4, c=PIECES, q=P)
                for g in range(4):
                    sync.dma_start(out[:, g, :, c, :],
                                   heads_out[c % 2][32 * g:32 * g + DK, :].rearrange(
                                       "d (j q) -> d j q", j=4)).then_inc(stored[c % 2], 16)

            def head_steps(head, first, last):
                for c in range(PIECES):
                    step = head * PIECES + c
                    if c == PIECES - 1 and not last:
                        for piece in range(PIECES):
                            wait_first(sync, scored, step * UNITS + 2 * piece + 2)
                            load_keys(head + 1, piece)
                    if not (last and c >= PIECES - 2):
                        wait_first(sync, scored, (step + 1) * UNITS)
                        load_queries(head + (c + 2) // PIECES, (c + 2) % PIECES)
                    if c:
                        store(head, c - 1)
                    elif not first:
                        store(head - 1, PIECES - 1)

            for c in range(PIECES):
                load_keys(0, c)
                if c < 2:
                    load_queries(0, c)
            head_steps(0, True, False)
            with sync.Fori(1, HEADS - 1) as head:
                head_steps(head, False, False)
            head_steps(HEADS - 1, False, True)
            store(HEADS - 1, PIECES - 1)
            for parity in range(2):
                sync.wait_ge(stored[parity], 16 * 4 * STEPS // 2)

        def over_steps(eng, body):
            body(0, 0, 0)
            body(1, 1, 0)
            with eng.Fori(1, STEPS // 2 - 1) as i:
                body(i * 2, 0, i // 2)
                body(i * 2 + 1, 1, i // 2)
            body(STEPS - 2, 0, HEADS - 1)
            body(STEPS - 1, 1, HEADS - 1)

        @block.tensor
        def _(pe):
            def scores(n, slot, c, half, parity):
                wait(pe, e_done, n - 1)
                for b in range(BATCH):
                    part = nc.tensor.matmul(
                        score[slot][:, b * HALF:(b + 1) * HALF], keys[:, c, b * P:(b + 1) * P],
                        queries[:, parity, b * P + half * HALF:b * P + (half + 1) * HALF],
                        start=(b % 8 == 0), stop=False, skip_group_check=True)
                part.then_inc(scored, 1)

            def shift(n, slot):
                pe.wait_ge(top_done, n + 1)
                for bank in range(2):
                    part = nc.tensor.matmul(
                        score[slot][:, bank * 512:(bank + 1) * 512], minus[:, :],
                        top[slot][:, :].unsqueeze(1).broadcast_to([P, 8, HALF]),
                        start=False, stop=True, skip_group_check=True)
                part.then_inc(shifted, 1)

            def values_of(pair, c, step, head):
                pe.wait_ge(normed, pair + 1)
                pe.wait_ge(v_copied, head * PIECES + c + 1)
                if c == 0:
                    wait(pe, copied, step)
                for b in range(BATCH):
                    g, j = b % 4, b // 4
                    part = nc.tensor.matmul(
                        heads_bank[32 * g:32 * g + 32, j * P:(j + 1) * P], values[:, c, b, :],
                        e[c][:, b, :], start=(c == 0 and j == 0), stop=(c == PIECES - 1),
                        skip_group_check=True)
                part.then_inc(weighted, 1)

            def step(s, parity, head):
                if isinstance(s, int):
                    pe.wait_ge(queries_loaded[parity], 16 * TERMS * (s // 2 + 1))
                else:
                    pe.wait_ge(queries_loaded[parity], (s - parity + 2) * (8 * TERMS))
                for u in range(UNITS):
                    c, half = u // 2, u % 2
                    n = s * UNITS + u
                    if half == 0 and parity == 0:
                        pe.wait_ge(keys_loaded[c], (head + 1) * (16 * TERMS))
                    scores(n, u % 2, c, half, parity)
                    if not (isinstance(n, int) and n == 0):
                        shift(n - 1, 1 - u % 2)
                    if half:
                        if c == LAG:
                            values_of(s * PIECES, 0, s, head)
                        elif not (isinstance(s, int) and s == 0):
                            before = head if parity else (
                                (s - 1) // PIECES if isinstance(s, int) else
                                (s - 1) // PIECES)
                            values_of(s * PIECES + c - LAG, c + PIECES - LAG, s - 1, before)

            pe.wait_ge(minus_set, 1)
            over_steps(pe, step)
            shift(STEPS * UNITS - 1, 1)
            for c in range(PIECES - LAG, PIECES):
                values_of((STEPS - 1) * PIECES + c, c, STEPS - 1, HEADS - 1)

        @block.vector
        def _(dve):
            def largest(n, slot):
                dve.wait_ge(scored, n + 1)
                wait(dve, shifted, n - 1)
                nc.vector.tensor_reduce(
                    top[slot][:, :], score[slot][:, :].rearrange("p (b q) -> p q b", b=BATCH),
                    AX.X, ALU.max).then_inc(top_done, 1)

            def add_up(pair, slot):
                dve.wait_ge(e_done, (pair + 1) * 2)
                wait(dve, inverse_done, pair)
                nc.vector.tensor_reduce(total[:, :], e[slot][:, :, :].rearrange("p b q -> p q b"),
                                        AX.X, ALU.add).then_inc(summed, 1)

            def invert(pair, slot):
                dve.wait_ge(summed, pair + 1)
                wait(dve, normed, pair - 1)
                nc.vector.reciprocal(inverse[slot % 2][:, :],
                                     total[:, :]).then_inc(inverse_done, 1)

            def step(s, parity, head):
                for c in range(PIECES):
                    pair = s * PIECES + c
                    started = not (isinstance(pair, int) and pair == 0)
                    largest(pair * 2, 0)
                    if started:
                        add_up(pair - 1, (c - 1) % PIECES)
                    largest(pair * 2 + 1, 1)
                    if started:
                        invert(pair - 1, (c - 1) % PIECES)

            nc.vector.tensor_scalar(minus[:, :], k.ident[:, :], -1.0, None,
                                    ALU.mult).then_inc(minus_set, 1)
            over_steps(dve, step)
            add_up(STEPS * PIECES - 1, PIECES - 1)
            invert(STEPS * PIECES - 1, PIECES - 1)

        @block.scalar
        def _(act):
            def copy_heads(s, parity):
                act.wait_ge(weighted, (s + 1) * PIECES)
                if isinstance(s, int):
                    wait(act, stored[parity], 64 * (s // 2))
                else:
                    act.wait_ge(stored[parity], (s - parity) * 32)
                nc.scalar.activation(heads_out[parity][:, :], heads_bank[:, :],
                                     ACT.Copy).then_inc(copied, 1)

            def step(s, parity, head):
                for u in range(UNITS):
                    c, half = u // 2, u % 2
                    n = s * UNITS + u
                    act.wait_ge(shifted, n + 1)
                    wait(act, weighted, s * PIECES + c - BUFS + 1)
                    nc.scalar.activation(
                        e[c][:, :, half * HALF:(half + 1) * HALF],
                        score[u % 2][:, :].rearrange("p (b q) -> p b q", b=BATCH),
                        ACT.Exp).then_inc(e_done, 1)
                    if u == UNITS - 2 and not (isinstance(s, int) and s == 0):
                        copy_heads(s - 1, 1 - parity)

            over_steps(act, step)
            copy_heads(STEPS - 1, 1)

        @block.gpsimd
        def _(pool):
            def head_steps(head):
                for c in range(PIECES):
                    for piece in range(PIECES):
                        pair = (head * PIECES + c) * PIECES + piece
                        if c == 0:
                            wait(pool, weighted, pair - PIECES + 1)
                            at = rows(head)
                            nc.gpsimd.tensor_copy(
                                values[:, piece, :, :].rearrange("p b (r d) -> p b r d", d=DK),
                                v[:, :, piece, at].unsqueeze(2).broadcast_to(
                                    [P, BATCH, 4, DK])).then_inc(v_copied, 1)
                        pool.wait_ge(inverse_done, pair + 1)
                        nc.gpsimd.tensor_tensor(
                            e[piece][:, :, :], e[piece][:, :, :],
                            inverse[piece % 2][:, :].unsqueeze(1).broadcast_to([P, BATCH, P]),
                            ALU.mult).then_inc(normed, 1)

            head_steps(0)
            with pool.Fori(1, HEADS) as head:
                head_steps(head)


def head_output(nc, k, prefix):
    with ExitStack() as ctx:
        m = Memory(nc, ctx, prefix)
        heads = [m.sb(f"heads{i}", [P, TILE], F32) for i in range(2)]
        high = [m.sb(f"high{i}", [P, TILE], F32R) for i in range(2)]
        low = [m.sb(f"low{i}", [P, TILE], F32R) for i in range(2)]
        x = [m.sb(f"x{i}", [P, TILE], F32) for i in range(2)]
        y = [m.ps(f"y{i}") for i in range(2)]
        high_done, low_done, y_done, added = m.sems("high_done low_done y_done added")
        heads_loaded, x_loaded = [[m.sem(f"{n}_loaded{i}") for i in range(2)]
                                  for n in ("heads", "x")]
        block = m.block()

        @block.sync
        def _(sync):
            def tile(t, parity):
                wait_first(sync, low_done, t - 1)
                sync.dma_start(heads[parity][:, :],
                               column(k.heads_dram, t)).then_inc(heads_loaded[parity], 16)
                wait_first(sync, added, t - 1)
                sync.dma_start(x[parity][:, :],
                               column(k.x_dram, t)).then_inc(x_loaded[parity], 16)

            over_tiles(sync, tile)

        def loaded(eng, sem, t, parity):
            if isinstance(t, int):
                eng.wait_ge(sem[parity], 16 * (t // 2 + 1))
            else:
                eng.wait_ge(sem[parity], (t - parity + 2) * 8)

        @block.scalar
        def _(act):
            def tile(t, parity):
                loaded(act, heads_loaded, t, parity)
                wait(act, y_done, t - 1)
                nc.scalar.activation(high[parity][:, :], heads[parity][:, :],
                                     ACT.Copy).then_inc(high_done, 1)

            over_tiles(act, tile)

        @block.vector
        def _(dve):
            def add(t, parity):
                dve.wait_ge(y_done, t + 1)
                loaded(dve, x_loaded, t, parity)
                nc.vector.scalar_tensor_tensor(column(k.xT, t), y[parity][:, :], k.biases[:, 3:4],
                                               x[parity][:, :], ALU.add,
                                               ALU.add).then_inc(added, 1)

            def tile(t, parity):
                dve.wait_ge(high_done, t + 1)
                wait(dve, y_done, t - 1)
                nc.vector.tensor_tensor(low[parity][:, :], heads[parity][:, :], high[parity][:, :],
                                        ALU.subtract).then_inc(low_done, 1)
                if not is_first(t):
                    add(t - 1, 1 - parity)

            over_tiles(dve, tile)
            add(TILES - 1, 1)

        @block.tensor
        def _(pe):
            def tile(t, parity):
                pe.wait_ge(low_done, t + 1)
                pe.wait_ge(high_done, t + 1)
                wait(pe, added, t - 1)
                three_passes(nc, y[parity][:, :], k.proj_part(3),
                             (high[parity][:, :], low[parity][:, :])).then_inc(y_done, 1)

            over_tiles(pe, tile)


def sequence_attention(nc, k, prefix):
    with ExitStack() as ctx:
        m = Memory(nc, ctx, prefix)
        norm = Norm(nc, k, m, m.ps("bank"))
        project = [m.ps(f"project{i}") for i in range(2)]
        score = [m.ps(f"score{i}") for i in range(2)]
        turned_bank = [m.ps(f"turned_bank{i}") for i in range(2)]
        y = m.ps("y")
        full = [m.sb(f"full_{x}", [P, TILE], F32) for x in "qk"]
        high = [[m.sb(f"high_{x}{i}", [P, TILE], F32R) for i in range(2)] for x in "qk"]
        low = [[m.sb(f"low_{x}{i}", [P, TILE], F32R) for i in range(2)] for x in "qk"]
        v = [m.sb(f"v{i}", [P, TILE], F32) for i in range(2)]
        top = [m.sb(f"top{i}", [P, 1], F32) for i in range(2)]
        e = [m.sb(f"e{i}", [P, SEQ], F32) for i in range(2)]
        total = [m.sb(f"total{i}", [P, 1], F32) for i in range(2)]
        inverse = [m.sb(f"inverse{i}", [P, 1], F32) for i in range(2)]
        weight = [m.sb(f"weight{i}", [P, SEQ], F32) for i in range(2)]
        turned = [m.sb(f"turned{i}", [P, SEQ], F32) for i in range(2)]
        (v_done, v_copied, scored, top_done, e_done, inverse_done, scaled, w_turned, w_copied,
         weighted, added) = m.sems("v_done v_copied scored top_done e_done inverse_done scaled "
                                   "w_turned w_copied weighted added")
        qk_done, full_done, high_done, low_done = [
            [m.sem(f"{name}_{x}") for x in "qk"] for name in
            ("qk_done", "full_done", "high_done", "low_done")]
        block = m.block()

        @block.scalar
        def _(act):
            def cut(t, parity):
                for x in range(2):
                    act.wait_ge(qk_done[x], t + 1)
                    wait(act, low_done[x], t)
                    nc.scalar.activation(full[x][:, :], project[x][:, :],
                                         ACT.Copy).then_inc(full_done[x], 1)
                    wait(act, scored, (t - 1) * PIECES)
                    nc.scalar.activation(high[x][parity][:, :], project[x][:, :],
                                         ACT.Copy).then_inc(high_done[x], 1)
                act.wait_ge(v_done, t + 1)
                wait(act, weighted, (t - 1) * PIECES)
                nc.scalar.activation(v[parity][:, :], project[0][:, :],
                                     ACT.Copy).then_inc(v_copied, 1)

            def copy_turned(n, slot):
                act.wait_ge(w_turned, n + 1)
                wait(act, weighted, n - 1)
                nc.scalar.activation(turned[slot][:, :], turned_bank[slot][:, :],
                                     ACT.Copy).then_inc(w_copied, 1)

            def tile(t, parity):
                for c in range(PIECES):
                    n, slot = t * PIECES + c, c % 2
                    act.wait_ge(top_done, n + 1)
                    wait(act, inverse_done, n - 1)
                    wait(act, scaled, n - 1)
                    nc.scalar.activation(e[slot][:, :], score[slot][:, :], ACT.Exp,
                                         bias=top[slot][:, 0:1],
                                         accum_out=total[slot][:, 0:1]).then_inc(e_done, 1)
                    if c or not is_first(t):
                        copy_turned(n - 1, 1 - slot)
                    if not is_last(t):
                        if c == 0:
                            norm.copy_in(act, t + 1)
                        elif c == 1:
                            wait(act, v_done, t + 1)
                            norm.cut_high(act, t + 1, 1 - parity)
                        elif c == 3:
                            cut(t + 1, 1 - parity)

            norm.copy_in(act, 0)
            norm.cut_high(act, 0, 0)
            cut(0, 0)
            over_tiles(act, tile)
            copy_turned(TILES * PIECES - 1, 1)

        @block.gpsimd
        def _(pool):
            def cut(t, parity):
                for x in range(2):
                    pool.wait_ge(full_done[x], t + 1)
                    pool.wait_ge(high_done[x], t + 1)
                    nc.gpsimd.tensor_tensor(low[x][parity][:, :], full[x][:, :],
                                            high[x][parity][:, :],
                                            ALU.subtract).then_inc(low_done[x], 1)

            def tile(t, parity):
                if not is_last(t):
                    norm.deviation(pool, t + 1)
                    cut(t + 1, 1 - parity)

            norm.deviation(pool, 0)
            cut(0, 0)
            over_tiles(pool, tile)

        @block.vector
        def _(dve):
            def largest(n, slot):
                dve.wait_ge(scored, n + 1)
                wait(dve, e_done, n - 1)
                nc.vector.tensor_reduce(top[slot][:, 0:1], score[slot][:, :], AX.X, ALU.max,
                                        negate=True).then_inc(top_done, 1)

            def scale(n, slot):
                dve.wait_ge(e_done, n + 1)
                nc.vector.reciprocal(inverse[slot][:, 0:1],
                                     total[slot][:, 0:1]).then_inc(inverse_done, 1)
                dve.wait_ge(inverse_done, n + 1)
                wait(dve, w_turned, n - 1)
                nc.vector.tensor_scalar(weight[slot][:, :], e[slot][:, :], inverse[slot][:, 0:1],
                                        NORM, ALU.mult, ALU.mult).then_inc(scaled, 1)

            def add(t):
                dve.wait_ge(weighted, (t + 1) * PIECES)
                nc.vector.tensor_tensor(column(k.xT, t), y[:, :], column(k.xT, t),
                                        ALU.add).then_inc(added, 1)

            def tile(t, parity):
                for c in range(PIECES):
                    n, slot = t * PIECES + c, c % 2
                    largest(n, slot)
                    if c or not is_first(t):
                        scale(n - 1, 1 - slot)
                    if c == 1 and not is_first(t):
                        add(t - 1)
                    if not is_last(t):
                        if c == 0:
                            norm.moments(dve, t + 1)
                        elif c == 1:
                            norm.norm_rows(dve, t + 1, 1 - parity)
                        elif c == 2:
                            norm.cut_low(dve, t + 1, 1 - parity)

            norm.moments(dve, 0)
            norm.norm_rows(dve, 0, 0)
            norm.cut_low(dve, 0, 0)
            over_tiles(dve, tile)
            scale(TILES * PIECES - 1, 1)
            add(TILES - 1)

        @block.tensor
        def _(pe):
            def projections(t, parity):
                pe.wait_ge(norm.n_copied, t + 1)
                pe.wait_ge(norm.n_high, t + 1)
                pe.wait_ge(norm.n_low, t + 1)
                for x in range(2):
                    if x == 0:
                        wait(pe, v_copied, t)
                    else:
                        wait(pe, high_done[x], t)
                    three_passes(nc, project[x][:, :], k.proj_part(4 + x),
                                 (norm.high[parity][:, :], norm.low[parity][:, :])
                                 ).then_inc(qk_done[x], 1)
                pe.wait_ge(high_done[0], t + 1)
                pe.wait_ge(full_done[0], t + 1)
                for c in range(CH):
                    part = nc.tensor.matmul(project[0][:, c * P:(c + 1) * P],
                                            norm.full[:, c * P:(c + 1) * P],
                                            k.wv_full[:, P:2 * P], start=True, stop=True)
                part.then_inc(v_done, 1)

            def scores(n, c, parity):
                wait(pe, e_done, n - 1)
                (qh, ql), (kh, kl) = [(high[x][parity], low[x][parity]) for x in range(2)]
                three_passes(nc, score[c % 2][:, :],
                             (qh[:, c * P:(c + 1) * P], ql[:, c * P:(c + 1) * P]),
                             (kh[:, :], kl[:, :])).then_inc(scored, 1)

            def turn_weights(n, slot):
                pe.wait_ge(scaled, n + 1)
                wait(pe, w_copied, n - 1)
                for c in range(PIECES):
                    part = nc.tensor.transpose(turned_bank[slot][:, c * P:(c + 1) * P],
                                               weight[slot][:, c * P:(c + 1) * P], k.ident[:, :])
                part.then_inc(w_turned, 1)

            def weigh(t, c, parity):
                pe.wait_ge(w_copied, t * PIECES + c + 1)
                if c == 0:
                    pe.wait_ge(v_copied, t + 1)
                    wait(pe, added, t)
                for piece in range(PIECES):
                    part = nc.tensor.matmul(y[:, c * P:(c + 1) * P],
                                            v[parity][:, piece * P:(piece + 1) * P],
                                            turned[c % 2][:, piece * P:(piece + 1) * P],
                                            start=(piece == 0), stop=(piece == PIECES - 1))
                part.then_inc(weighted, 1)

            def tile(t, parity):
                for x in range(2):
                    pe.wait_ge(high_done[x], t + 1)
                    pe.wait_ge(low_done[x], t + 1)
                for c in range(PIECES):
                    n = t * PIECES + c
                    scores(n, c, parity)
                    if c >= 1 or not is_first(t):
                        turn_weights(n - 1, (c - 1) % 2)
                    if c >= 2:
                        weigh(t, c - 2, parity)
                    elif not is_first(t):
                        weigh(t - 1, c + 2, 1 - parity)
                    if not is_last(t):
                        if c == 0:
                            norm.turn(pe, t + 1)
                        elif c == 1:
                            norm.turn_back(pe, t + 1, 1 - parity)
                        elif c == 3:
                            projections(t + 1, 1 - parity)

            norm.turn(pe, 0)
            norm.turn_back(pe, 0, 0)
            projections(0, 0)
            over_tiles(pe, tile)
            turn_weights(TILES * PIECES - 1, 1)
            weigh(TILES - 1, 2, 1)
            weigh(TILES - 1, 3, 1)


def program(nc, ins, out, phases):
    with ExitStack() as ctx:
        m = Memory(nc, ctx, "")
        k = Kept(m)
        load_block(nc, k, ins)
        for n, phase in enumerate(phases):
            if phase == "moe":
                gated_block(nc, k, f"b{n}_", PAIRS, k.wg, k.wu, k.wd, True)
            elif phase == "ffn":
                gated_block(nc, k, f"b{n}_", HCH, k.ffn_part(0), k.ffn_part(1), k.ffn_part(2),
                            False)
            elif phase == "heads":
                head_projection(nc, k, f"b{n}_")
                batch_attention(nc, k, f"b{n}c_")
                head_output(nc, k, f"b{n}d_")
            elif phase == "attention":
                sequence_attention(nc, k, f"b{n}_")
        store_block(nc, k, out)


def store_block(nc, k, out):
    with ExitStack() as ctx:
        stored = Memory(nc, ctx, "st_").sem("stored")
        block = ctx.enter_context(nc.Block())

        @block.sync
        def _(sync):
            sync.dma_start(out, k.xT[:, :]).then_inc(stored, 16)
            sync.wait_ge(stored, 16)


_PROJECTIONS = ["L0_attn_Wq", "L0_attn_Wk", "L0_attn_Wv", "L0_attn_Wo",
                "L1_attn_Wq", "L1_attn_Wk", "L1_attn_Wv"]
PHASES = ("moe", "heads", "moe", "ffn", "attention", "ffn")


def kernel(**inputs):
    import ml_dtypes
    import concourse.bacc as bacc
    from concourse.bass_utils import run_bass_kernel_spmd

    given = {name: np.asarray(value) for name, value in inputs.items()}
    gate_up, down = given["L0_ffn_gate_up_proj"], given["L0_ffn_down_proj"]

    def pairs(w):
        return w.transpose(2, 0, 1).reshape(P, ROUTED * INNER)

    def by_chunk(w):
        return w.T.reshape(HCH, P, P).transpose(1, 0, 2).reshape(P, HIDDEN)

    third_row, column_ = np.arange(3 * ROUTED)[:, None], np.arange(ROUTED * INNER)[None, :]
    arrays = {
        "xT": given["L0_attn_x"].reshape(TOKENS, P).T,
        "wg": pairs(gate_up[:ROUTED, :INNER]),
        "wu": pairs(gate_up[:ROUTED, INNER:]),
        "wd": down.transpose(0, 2, 1).reshape(PAIRS, P, P).transpose(1, 0, 2).reshape(P, -1),
        "wc": given["L0_ffn_classifier_weight"].T,
        "bias": given["L0_ffn_e_score_correction_bias"],
        "proj": np.concatenate([given[name].T for name in _PROJECTIONS], axis=1),
        "ffn": np.concatenate([given["L1_ffn_w_gate"].T, given["L1_ffn_w_up"].T,
                               by_chunk(given["L1_ffn_w_down"])], axis=1),
        "biases": np.stack([given[f"L0_attn_b{x}"] for x in "qkvo"], axis=1),
        "wv_full": np.concatenate([given["L0_attn_Wv"].T, given["L1_attn_Wv"].T], axis=1),
        "bv": given["L0_attn_bv"],
        "sel": (third_row % ROUTED == column_ // INNER).astype(ml_dtypes.bfloat16),
        "ident": np.eye(P, dtype=np.float32),
        "identb": np.eye(P, dtype=ml_dtypes.bfloat16),
    }
    arrays = {name: np.ascontiguousarray(a) for name, a in arrays.items()}

    nc = bacc.Bacc("TRN2", target_bir_lowering=False, num_devices=1)
    ins = {name: nc.dram_tensor("in_" + name, a.shape, mybir.dt.from_np(a.dtype),
                                kind="ExternalInput").ap() for name, a in arrays.items()}
    out = nc.dram_tensor("out_xT", (P, TOKENS), F32, kind="ExternalOutput").ap()
    program(nc, ins, out, PHASES)
    run = run_bass_kernel_spmd(nc, [{"in_" + name: a for name, a in arrays.items()}],
                               core_ids=[0])
    return run.results[0]["out_xT"].T.reshape(BATCH, SEQ, P)
```

```python
from contextlib import ExitStack

import numpy as np

import concourse.bass as bass
from concourse import mybir

F32 = mybir.dt.float32
F32R = mybir.dt.float32r
BF16 = mybir.dt.bfloat16
I32 = mybir.dt.int32
ALU = mybir.AluOpType
ACT = mybir.ActivationFunctionType
AX = mybir.AxisListType

P = 128
BATCH, SEQ = 16, 512
TOKENS = BATCH * SEQ
TILE = 512
TILES = TOKENS // TILE
CH = TILE // P
EPS = 1e-5

ROUTED, ZERO, TOPK = 32, 8, 6
EXPERTS = ROUTED + ZERO
INNER = 64
PAIRS = ROUTED // 2
ROUTE_SCALE = 2.5 * 0.5
HIDDEN = 384
HCH = HIDDEN // P
DEQUANT = 1.0 / 127.0
SENTINEL = -3.0e38

HEADS, DK = 16, 8
TERMS = 8
STACK = TERMS * DK
NORM = 1.0 / float(np.sqrt(128.0))


def wait(eng, sem, value):
    if isinstance(value, int) and value <= 0:
        return
    eng.wait_ge(sem, value)


def wait_first(eng, sem, value):
    if isinstance(value, int):
        return wait(eng, sem, value)
    value = eng.snap(value)
    eng.wait_ge(sem, 1)
    eng.wait_ge(sem, value)


class Chain:

    def __init__(self, eng, sem, per):
        self.eng, self.sem, self.per, self.at = eng, sem, per, 0

    def tile(self, t):
        self.base, self.at = t * self.per, 0

    def link(self, ins):
        self.at += 1
        ins.then_inc(self.sem, 1)
        self.eng.wait_ge(self.sem, self.base + self.at)

    def end(self):
        assert self.at == self.per, self.at


def column(ap, t, width=TILE):
    if isinstance(t, int):
        return ap[:, t * width:(t + 1) * width]
    return ap[:, bass.ds(t * width, width)]


def chunks(ap):
    return ap.rearrange("p (c n) -> p c n", c=CH)


def over(ap, n):
    return ap.unsqueeze(2).broadcast_to([ap.shape[0], ap.shape[1], n])


class Memory:

    def __init__(self, nc, ctx, prefix):
        self.nc, self.ctx, self.prefix, self.semaphores = nc, ctx, prefix, []

    def sb(self, name, shape, dtype):
        return self.ctx.enter_context(self.nc.sbuf_tensor(self.prefix + name, shape, dtype))

    def ps(self, name, shape=(P, 512), dtype=F32):
        return self.ctx.enter_context(self.nc.psum_tensor(self.prefix + name, list(shape), dtype))

    def sem(self, name):
        semaphore = self.ctx.enter_context(self.nc.semaphore(self.prefix + name))
        self.semaphores.append(semaphore)
        return semaphore

    def sems(self, names):
        return [self.sem(name) for name in names.split()]

    def block(self):
        self.ctx.callback(self.clear)
        return self.ctx.enter_context(self.nc.Block())

    def clear(self):
        with self.nc.Block() as clearing:
            @clearing.gpsimd
            def _(pool):
                for semaphore in self.semaphores:
                    pool.sem_clear(semaphore)


def over_tiles(eng, body):
    body(0, 0)
    body(1, 1)
    with eng.Fori(1, TILES // 2 - 1) as i:
        body(i * 2, 0)
        body(i * 2 + 1, 1)
    body(TILES - 2, 0)
    body(TILES - 1, 1)


def is_last(t):
    return isinstance(t, int) and t == TILES - 1


def is_first(t):
    return isinstance(t, int) and t == 0


class Kept:

    def __init__(self, m):
        def parts(name, width):
            return (m.sb(name + "_high", [P, width], F32R), m.sb(name + "_low", [P, width], F32R))

        self.xT = m.sb("xT", [P, TOKENS], F32)
        self.wg, self.wu = parts("wg", PAIRS * P), parts("wu", PAIRS * P)
        self.wd = parts("wd", PAIRS * P)
        self.ffn = parts("ffn", 3 * HIDDEN)
        self.proj = parts("proj", PROJECTIONS * P)
        self.wc = m.sb("wc", [P, EXPERTS], F32)
        self.bias = m.sb("bias", [P, CH, EXPERTS], F32)
        self.sel = m.sb("sel", [3 * ROUTED, PAIRS * P], BF16)
        self.ident = m.sb("ident", [P, P], F32)
        self.identb = m.sb("identb", [P, P], BF16)
        self.biases = m.sb("biases", [P, 4], F32)
        self.minus_half = m.sb("minus_half", [P, CH], F32)
        self.eps = m.sb("eps", [P, CH], F32)
        self.wv_full = m.sb("wv_full", [P, 2 * P], F32)
        self.bv_row = m.sb("bv_row", [P, P], F32)
        self.x_dram = m.nc.dram_tensor("x_kept", (P, TOKENS), F32).ap()
        self.heads_dram = m.nc.dram_tensor("heads_kept", (P, TOKENS), F32).ap()
        self.thirds_dram = [m.nc.dram_tensor(f"thirds_{x}", (3, P, CH, BATCH, P), BF16).ap()
                            for x in "qk"]

    def ffn_part(self, n):
        return [part[:, n * HIDDEN:(n + 1) * HIDDEN] for part in self.ffn]

    def proj_part(self, n):
        return [part[:, n * P:(n + 1) * P] for part in self.proj]


PROJECTIONS = 7


def load_block(nc, k, ins):
    with ExitStack() as ctx:
        m = Memory(nc, ctx, "ld_")
        raw = [m.sb(f"raw{i}", [P, PAIRS * P], F32) for i in range(2)]
        ints = m.sb("ints", [P, 3 * HIDDEN], I32)
        loaded = m.sems("loaded0 loaded1")
        ints_loaded, dequantised, const_loaded, x_loaded, high_done, low_done, half_set = m.sems(
            "ints_loaded dequantised const_loaded x_loaded high_done low_done half_set")
        todo = [(ins["wg"], k.wg), (ins["wu"], k.wu), (ins["wd"], k.wd), (ins["proj"], k.proj),
                (None, k.ffn)]
        consts = [("wc", k.wc), ("sel", k.sel), ("ident", k.ident), ("identb", k.identb),
                  ("biases", k.biases), ("wv_full", k.wv_full)]
        block = m.block()

        @block.sync
        def _(sync):
            sync.dma_start(ints[:, :], ins["ffn"]).then_inc(ints_loaded, 16)
            for n, (src, parts) in enumerate(todo[:-1]):
                if n >= 2:
                    sync.wait_ge(low_done, n - 1)
                sync.dma_start(raw[n % 2][:, 0:parts[0].shape[1]],
                               src).then_inc(loaded[n % 2], 16)

        @block.scalar
        def _(act):
            act.dma_start(k.xT[:, :], ins["xT"]).then_inc(x_loaded, 16)
            for c in range(CH):
                act.dma_start(k.bias[:, c, :],
                              ins["bias"].partition_broadcast(P)).then_inc(const_loaded, 16)
            act.dma_start(k.bv_row[:, :], ins["bv"].partition_broadcast(P)).then_inc(const_loaded,
                                                                                     16)
            for name, tensor in consts:
                act.dma_start(tensor[:, :], ins[name]).then_inc(const_loaded, 16)
            for n, (src, (high, _)) in enumerate(todo):
                if src is None:
                    act.wait_ge(dequantised, 1)
                else:
                    act.wait_ge(loaded[n % 2], 16 * (n // 2 + 1))
                nc.scalar.activation(high[:, :], raw[n % 2][:, 0:high.shape[1]],
                                     ACT.Copy).then_inc(high_done, 1)
            act.wait_ge(const_loaded, 16 * (CH + 1 + len(consts)))
            act.wait_ge(x_loaded, 16)

        @block.vector
        def _(dve):
            nc.vector.memset(k.minus_half[:, :], -0.5).then_inc(half_set, 1)
            nc.vector.memset(k.eps[:, :], EPS).then_inc(half_set, 1)
            for n, (src, (high, low)) in enumerate(todo):
                if src is None:
                    dve.wait_ge(ints_loaded, 16)
                    dve.wait_ge(low_done, n - 1)
                    nc.vector.tensor_scalar(raw[n % 2][:, 0:3 * HIDDEN], ints[:, :], DEQUANT, None,
                                            ALU.mult).then_inc(dequantised, 1)
                dve.wait_ge(high_done, n + 1)
                nc.vector.tensor_tensor(low[:, :], raw[n % 2][:, 0:high.shape[1]], high[:, :],
                                        ALU.subtract).then_inc(low_done, 1)


def three_passes(nc, out, w, x, start=True, stop=True):
    (wh, wl), (xh, xl) = w, x
    nc.tensor.matmul(out, wl, xh, start=start, stop=False, skip_group_check=True)
    nc.tensor.matmul(out, wh, xl, start=False, stop=False, skip_group_check=True)
    return nc.tensor.matmul(out, wh, xh, start=False, stop=stop, skip_group_check=True)



class Norm:

    def __init__(self, nc, k, m, bank):
        self.nc, self.k, self.bank = nc, k, bank
        self.xs = m.sb("xs", [P, TILE], F32)
        self.stats = m.sb("stats", [P, CH, 6], F32)
        self.mv = m.sb("mv", [P, CH, 2], F32)
        self.var = m.sb("var", [P, CH], F32)
        self.rstd = m.sb("rstd", [P, CH], F32)
        self.rows = [m.sb(f"rows{i}", [P, TILE], F32) for i in range(2)]
        self.full = m.sb("full", [P, TILE], F32)
        self.high = [m.sb(f"high{i}", [P, TILE], F32R) for i in range(2)]
        self.low = [m.sb(f"low{i}", [P, TILE], F32R) for i in range(2)]
        (self.x_copied, self.x_turned, self.stats_done, self.aggregated, self.var_done,
         self.rstd_done, self.normed, self.n_turned, self.n_copied, self.n_high,
         self.n_low) = m.sems("x_copied x_turned stats_done aggregated var_done rstd_done "
                              "normed n_turned n_copied n_high n_low")

    def copy_in(self, act, t):
        wait(act, self.x_turned, t)
        self.nc.scalar.activation(self.xs[:, :], column(self.k.xT, t),
                                  ACT.Copy).then_inc(self.x_copied, 1)

    def turn(self, pe, t):
        pe.wait_ge(self.x_copied, t + 1)
        wait(pe, self.n_copied, t)
        wait(pe, self.n_high, t)
        for c in range(CH):
            part = self.nc.tensor.transpose(self.bank[:, c * P:(c + 1) * P],
                                            self.xs[:, c * P:(c + 1) * P], self.k.ident[:, :])
        part.then_inc(self.x_turned, 1)

    def moments(self, dve, t):
        dve.wait_ge(self.x_turned, t + 1)
        wait(dve, self.aggregated, t)
        for c in range(CH):
            part = self.nc.vector.bn_stats(self.stats[:, c, :], self.bank[:, c * P:(c + 1) * P])
        part.then_inc(self.stats_done, 1)

    def aggregate(self, dve, t):
        dve.wait_ge(self.stats_done, 1)
        dve.wait_ge(self.stats_done, t + 1)
        for c in range(CH):
            part = self.nc.vector.bn_aggr(self.mv[:, c, :], self.stats[:, c, :])
        part.then_inc(self.aggregated, 1)

    def deviation(self, pool, t):
        pool.wait_ge(self.aggregated, t + 1)
        self.nc.gpsimd.tensor_tensor(self.var[:, :], self.mv[:, :, 1], self.k.eps[:, :],
                                     ALU.add).then_inc(self.var_done, 1)
        pool.wait_ge(self.var_done, t + 1)
        self.nc.gpsimd.tensor_tensor(self.rstd[:, :], self.var[:, :], self.k.minus_half[:, :],
                                     ALU.pow).then_inc(self.rstd_done, 1)

    def norm_rows(self, dve, t, parity, which=range(CH)):
        dve.wait_ge(self.rstd_done, t + 1)
        wait(dve, self.n_turned, t - 1)
        for c in which:
            part = self.nc.vector.tensor_scalar(
                self.rows[parity][:, c * P:(c + 1) * P], self.bank[:, c * P:(c + 1) * P],
                self.mv[:, c, 0:1], self.rstd[:, c:c + 1], ALU.subtract, ALU.mult)
        if CH - 1 in which:
            part.then_inc(self.normed, 1)

    def turn_back(self, pe, t, parity):
        pe.wait_ge(self.normed, t + 1)
        for c in range(CH):
            part = self.nc.tensor.transpose(self.bank[:, c * P:(c + 1) * P],
                                            self.rows[parity][:, c * P:(c + 1) * P],
                                            self.k.ident[:, :])
        part.then_inc(self.n_turned, 1)

    def cut_high(self, act, t, parity):
        act.wait_ge(self.n_turned, t + 1)
        wait(act, self.n_low, t)
        self.nc.scalar.activation(self.full[:, :], self.bank[:, :],
                                  ACT.Copy).then_inc(self.n_copied, 1)
        self.nc.scalar.activation(self.high[parity][:, :], self.bank[:, :],
                                  ACT.Copy).then_inc(self.n_high, 1)

    def cut_low(self, dve, t, parity):
        dve.wait_ge(self.n_copied, t + 1)
        dve.wait_ge(self.n_high, t + 1)
        self.nc.vector.tensor_tensor(self.low[parity][:, :], self.full[:, :],
                                     self.high[parity][:, :], ALU.subtract).then_inc(self.n_low, 1)


class Router:

    LINKS = 12

    def __init__(self, nc, k, m, norm):
        self.nc, self.k, self.norm, self.bank = nc, k, norm, norm.bank
        self.top = m.sb("top", [P, CH], F32)
        self.z = m.sb("z", [P, CH, EXPERTS], F32)
        self.e = m.sb("e", [P, CH, EXPERTS], F32)
        self.total = m.sb("total", [P, CH], F32)
        self.inverse = m.sb("inverse", [P, CH], F32)
        self.score = m.sb("score", [P, CH, EXPERTS], F32)
        self.biased = m.sb("biased", [P, CH, EXPERTS + 2], F32)
        self.best = m.sb("best", [P, CH, 8], F32)
        self.marked = m.sb("marked", [P, CH, EXPERTS + 2], F32)
        self.mask = m.sb("mask", [P, CH, EXPERTS], F32)
        self.weight = m.sb("weight", [P, CH, EXPERTS], F32)
        self.rest = m.sb("rest", [P, CH, ROUTED], F32)
        self.rest2 = m.sb("rest2", [P, CH, ROUTED], F32)
        self.thirds = m.sb("thirds", [P, CH, 3 * ROUTED], BF16)
        self.zero_weight = m.sb("zero_weight", [P, CH], F32)
        self.diagonal = [m.sb(f"diagonal{i}", [P, CH, P], F32) for i in range(2)]
        self.turned = [m.sb(f"turned{i}", [3 * ROUTED, TILE], BF16) for i in range(2)]
        (self.sentinels, self.logits_done, self.shifted, self.e_done, self.thirds_done,
         self.w_turned, self.w_copied, self.diagonal_done,
         self.biased_done, self.best_done, self.own) = m.sems("sentinels logits_done shifted e_done thirds_done w_turned w_copied "
                            "diagonal_done biased_done best_done route_own")

    def chain(self, dve):
        self.steps = Chain(dve, self.own, self.LINKS)

    def logits(self, pe, t):
        norm = self.norm
        pe.wait_ge(norm.n_copied, t + 1)
        pe.wait_ge(norm.n_high, t + 1)
        for c in range(CH):
            part = self.nc.tensor.matmul(self.bank[:, c * EXPERTS:(c + 1) * EXPERTS],
                                         norm.full[:, c * P:(c + 1) * P], self.k.wc[:, :],
                                         start=True, stop=True)
        part.then_inc(self.logits_done, 1)

    def shift(self, dve, t):
        logits = self.bank[:, 0:CH * EXPERTS].rearrange("p (c n) -> p c n", c=CH)
        self.steps.tile(t)
        dve.wait_ge(self.logits_done, t + 1)
        self.steps.link(self.nc.vector.tensor_reduce(self.top[:, :], logits, AX.X, ALU.max))
        wait(dve, self.e_done, t)
        self.nc.vector.tensor_tensor(self.z[:, :, :], logits, over(self.top[:, :], EXPERTS),
                                     ALU.subtract).then_inc(self.shifted, 1)

    def exponentials(self, act, t):
        act.wait_ge(self.shifted, t + 1)
        wait(act, self.thirds_done, t)
        self.nc.scalar.activation(self.e[:, :, :], self.z[:, :, :],
                                  ACT.Exp).then_inc(self.e_done, 1)

    def choose(self, dve, t):
        vector, link = self.nc.vector, self.steps.link
        real = self.biased[:, :, 0:EXPERTS]
        dve.wait_ge(self.e_done, t + 1)
        link(vector.tensor_reduce(self.total[:, :], self.e[:, :, :], AX.X, ALU.add))
        link(vector.reciprocal(self.inverse[:, :], self.total[:, :]))
        link(vector.tensor_tensor(self.score[:, :, :], self.e[:, :, :],
                                  over(self.inverse[:, :], EXPERTS), ALU.mult))
        vector.tensor_tensor(real, self.score[:, :, :], self.k.bias[:, :, :],
                             ALU.add).then_inc(self.biased_done, 1)

    def search(self, dve, t):
        vector, link = self.nc.vector, self.steps.link
        dve.wait_ge(self.biased_done, 1)
        dve.wait_ge(self.biased_done, t + 1)
        for c in range(CH):
            part = vector.max(self.best[:, c, :], self.biased[:, c, 0:EXPERTS])
        link(part)
        vector.memset(self.best[:, :, TOPK:8], SENTINEL).then_inc(self.best_done, 1)

    def mark(self, dve, t):
        vector, link = self.nc.vector, self.steps.link
        real = self.biased[:, :, 0:EXPERTS]
        dve.wait_ge(self.best_done, 1)
        dve.wait_ge(self.best_done, t + 1)
        for c in range(CH):
            part = vector.match_replace(self.marked[:, c, :], self.best[:, c, :],
                                        self.biased[:, c, :], -SENTINEL)
        link(part)
        link(vector.tensor_tensor(self.mask[:, :, :], self.marked[:, :, 0:EXPERTS], real,
                                  ALU.not_equal))
        link(vector.scalar_tensor_tensor(self.weight[:, :, :], self.mask[:, :, :], ROUTE_SCALE,
                                         self.score[:, :, :], ALU.mult, ALU.mult))

    def cut(self, dve, t):
        vector, link = self.nc.vector, self.steps.link
        routed = self.weight[:, :, 0:ROUTED]
        third = [self.thirds[:, :, i * ROUTED:(i + 1) * ROUTED] for i in range(3)]
        wait(dve, self.w_turned, t)
        wait(dve, self.diagonal_done, t)
        vector.tensor_reduce(self.zero_weight[:, :], self.weight[:, :, ROUTED:EXPERTS], AX.X,
                             ALU.add)
        link(vector.tensor_copy(third[0], routed))

    def cut_rest(self, dve, t):
        vector, link = self.nc.vector, self.steps.link
        routed = self.weight[:, :, 0:ROUTED]
        third = [self.thirds[:, :, i * ROUTED:(i + 1) * ROUTED] for i in range(3)]
        link(vector.tensor_tensor(self.rest[:, :, :], routed, third[0], ALU.subtract))
        link(vector.tensor_copy(third[1], self.rest[:, :, :]))
        link(vector.tensor_tensor(self.rest2[:, :, :], self.rest[:, :, :], third[1],
                                  ALU.subtract))
        vector.tensor_copy(third[2], self.rest2[:, :, :]).then_inc(self.thirds_done, 1)
        self.steps.end()

    def diagonals(self, pool, t, parity):
        pool.wait_ge(self.thirds_done, t + 1)
        for c in range(CH):
            part = self.nc.gpsimd.tensor_tensor(
                self.diagonal[parity][:, c, :], self.k.ident[:, :],
                self.zero_weight[:, c:c + 1].broadcast_to([P, P]), ALU.mult)
        part.then_inc(self.diagonal_done, 1)

    def turn(self, pe, t):
        bank = self.bank[:, :].bitcast(BF16)
        pe.wait_ge(self.thirds_done, t + 1)
        for c in range(CH):
            part = self.nc.tensor.transpose(bank[0:3 * ROUTED, c * P:(c + 1) * P],
                                            self.thirds[:, c, :], self.k.identb[:, :])
        part.then_inc(self.w_turned, 1)

    def copy_turned(self, act, t, parity):
        act.wait_ge(self.w_turned, t + 1)
        self.nc.scalar.activation(self.turned[parity][:, :],
                                  self.bank[:, :].bitcast(BF16)[0:3 * ROUTED, 0:TILE],
                                  ACT.Copy).then_inc(self.w_copied, 1)


def gated_block(nc, k, prefix, units, w_gate, w_up, w_down, routed):
    LAG = 2
    hold = 4 if routed else 3
    with ExitStack() as ctx:
        m = Memory(nc, ctx, prefix)
        gate = [m.ps(f"gate{i}") for i in range(2)]
        up = [m.ps(f"up{i}") for i in range(2)]
        y, bank = m.ps("y"), m.ps("bank")
        norm = Norm(nc, k, m, bank)
        gated = [m.sb(f"gated{i}", [P, TILE], F32) for i in range(2)]
        h = [m.sb(f"h{i}", [P, TILE], F32) for i in range(2)]
        h_high = [m.sb(f"h_high{i}", [P, TILE], F32R) for i in range(hold)]
        h_low = [m.sb(f"h_low{i}", [P, TILE], F32R) for i in range(hold)]
        (gate_done, up_done, silu_done, h_done, high_done, low_done, down_done, y_done,
         y_added) = m.sems("gate_done up_done silu_done h_done high_done low_done down_done "
                           "y_done y_added")
        if routed:
            share = [m.ps(f"share{i}") for i in range(2)]
            product = m.sb("product", [P, TILE], F32)
            product_done = m.sem("product_done")
            router = Router(nc, k, m, norm)
            at = dict(copy=0, turn=1, moments=2, aggregate=3, deviation=3, rows_a=4, rows_b=5,
                      back=6, high=7, low=8, logits=8, shift=9, exp=9, choose=10, search=11,
                      mark=12, cut=13, cut_rest=13, diagonals=14, w_turn=14, w_copy=15)
        else:
            at = dict(copy=0, turn=0, moments=0, aggregate=0, deviation=0, rows_a=0, rows_b=0,
                      back=1, high=1, low=1)
        block = m.block()

        @block.scalar
        def _(act):
            def high(n, u, slot):
                act.wait_ge(h_done, n + 1)
                wait(act, down_done, n - hold + 1)
                nc.scalar.activation(h_high[u % hold][:, :], h[slot][:, :],
                                     ACT.Copy).then_inc(high_done, 1)

            def prepare(s, t, parity):
                if s == "copy":
                    norm.copy_in(act, t)
                elif s == "high":
                    wait(act, up_done, units * (t - 1))
                    if routed:
                        wait(act, router.logits_done, t)
                    norm.cut_high(act, t, parity)
                elif s == "exp":
                    router.exponentials(act, t)
                elif s == "w_copy":
                    router.copy_turned(act, t, parity)

            steps = [s for s in ("copy", "high", "exp", "w_copy") if s in at]
            for s in steps:
                prepare(s, 0, 0)

            def tile(t, parity):
                for u in range(units):
                    n = t * units + u
                    slot = (parity * units + u) % 2
                    act.wait_ge(gate_done, n + 1)
                    wait(act, h_done, n - 1)
                    nc.scalar.activation(gated[slot][:, :], gate[slot][:, :],
                                         ACT.Silu).then_inc(silu_done, 1)
                    if u:
                        high(n - 1, u - 1, 1 - slot)
                    for s in steps:
                        if at[s] == u and not is_last(t):
                            prepare(s, t + 1, 1 - parity)
                high(n, u, slot)

            over_tiles(act, tile)

        @block.gpsimd
        def _(pool):
            def prepare(t, parity, s):
                if s == "deviation":
                    norm.deviation(pool, t)
                elif s == "diagonals":
                    wait(pool, y_done, t - 1)
                    router.diagonals(pool, t, parity)

            steps = [s for s in ("deviation", "diagonals") if s in at]
            for s in steps:
                prepare(0, 0, s)

            def tile(t, parity):
                for u in range(units):
                    n = t * units + u
                    slot = (parity * units + u) % 2
                    for s in steps:
                        if at[s] == u and not is_last(t):
                            prepare(t + 1, 1 - parity, s)
                    pool.wait_ge(high_done, n + 1)
                    nc.gpsimd.tensor_tensor(h_low[u % hold][:, :], h[slot][:, :],
                                            h_high[u % hold][:, :],
                                            ALU.subtract).then_inc(low_done, 1)

            over_tiles(pool, tile)

        @block.vector
        def _(dve):
            if routed:
                router.chain(dve)
                nc.vector.memset(router.biased[:, :, EXPERTS:EXPERTS + 2],
                                 SENTINEL).then_inc(router.sentinels, 1)
                dve.wait_ge(router.sentinels, 1)

            def prepare(s, t, parity):
                if s == "moments":
                    norm.moments(dve, t)
                elif s == "aggregate":
                    norm.aggregate(dve, t)
                elif s == "rows_a":
                    if routed:
                        wait(dve, y_done, t - 1)
                    norm.norm_rows(dve, t, parity, range(CH // 2))
                elif s == "rows_b":
                    norm.norm_rows(dve, t, parity, range(CH // 2, CH))
                elif s == "low":
                    norm.cut_low(dve, t, parity)
                elif s == "shift":
                    router.shift(dve, t)
                elif s == "choose":
                    router.choose(dve, t)
                elif s == "search":
                    router.search(dve, t)
                elif s == "mark":
                    router.mark(dve, t)
                elif s == "cut":
                    router.cut(dve, t)
                elif s == "cut_rest":
                    router.cut_rest(dve, t)

            steps = [s for s in ("moments", "aggregate", "rows_a", "rows_b", "low", "shift",
                                 "choose", "search", "mark", "cut", "cut_rest") if s in at]
            for s in steps:
                prepare(s, 0, 0)

            def add(t):
                if routed:
                    dve.wait_ge(y_done, t + 1)
                else:
                    dve.wait_ge(down_done, (t + 1) * units)
                nc.vector.scalar_tensor_tensor(column(k.xT, t), y[:, :], 1.0 if routed else 0.5,
                                               column(k.xT, t), ALU.mult,
                                               ALU.add).then_inc(y_added, 1)

            def tile(t, parity):
                for u in range(units):
                    n = t * units + u
                    slot = (parity * units + u) % 2
                    dve.wait_ge(silu_done, n + 1)
                    dve.wait_ge(up_done, n + 1)
                    if routed:
                        wait(dve, h_done, n)
                        nc.vector.tensor_tensor(product[:, :], gated[slot][:, :], up[slot][:, :],
                                                ALU.mult).then_inc(product_done, 1)
                        dve.wait_ge(product_done, n + 1)
                        wait(dve, low_done, n - 1)
                        nc.vector.tensor_tensor(h[slot][:, :], product[:, :], share[slot][:, :],
                                                ALU.mult).then_inc(h_done, 1)
                    else:
                        wait(dve, low_done, n - 1)
                        nc.vector.tensor_tensor(h[slot][:, :], gated[slot][:, :], up[slot][:, :],
                                                ALU.mult).then_inc(h_done, 1)
                    if u == LAG - 1 and not is_first(t):
                        add(t - 1)
                    for s in steps:
                        if at[s] == u and not is_last(t):
                            prepare(s, t + 1, 1 - parity)

            over_tiles(dve, tile)
            add(TILES - 1)

        @block.tensor
        def _(pe):
            def prepare(s, t, parity):
                if s == "turn":
                    if routed:
                        wait(pe, router.w_copied, t)
                    norm.turn(pe, t)
                elif s == "back":
                    norm.turn_back(pe, t, parity)
                elif s == "logits":
                    router.logits(pe, t)
                elif s == "w_turn":
                    router.turn(pe, t)

            def rows_of(w, u):
                return w[0][:, u * P:(u + 1) * P], w[1][:, u * P:(u + 1) * P]

            def down(t, u, parity):
                n = t * units + u
                if u == 0:
                    wait(pe, y_added, t)
                pe.wait_ge(high_done, n + 1)
                pe.wait_ge(low_done, n + 1)
                last = u == units - 1
                ins = three_passes(nc, y[:, :], rows_of(w_down, u),
                                   (h_high[u % hold][:, :], h_low[u % hold][:, :]),
                                   start=(u == 0), stop=(last and not routed))
                ins.then_inc(down_done, 1)
                if last:
                    if routed:
                        pe.wait_ge(router.diagonal_done, t + 1)
                        for c in range(CH):
                            ins = nc.tensor.matmul(y[:, c * P:(c + 1) * P],
                                                   norm.rows[parity][:, c * P:(c + 1) * P],
                                                   router.diagonal[parity][:, c, :],
                                                   start=False, stop=True, skip_group_check=True)
                        ins.then_inc(y_done, 1)

            steps = [s for s in ("turn", "back", "logits", "w_turn") if s in at]
            for s in steps:
                prepare(s, 0, 0)

            def tile(t, parity):
                x = (norm.high[parity][:, :], norm.low[parity][:, :])
                pe.wait_ge(norm.n_low, t + 1)
                pe.wait_ge(norm.n_high, t + 1)
                for u in range(units):
                    n = t * units + u
                    slot = (parity * units + u) % 2
                    wait(pe, silu_done, n - 1)
                    three_passes(nc, gate[slot][:, :], rows_of(w_gate, u),
                                 x).then_inc(gate_done, 1)
                    wait(pe, h_done, n - 1)
                    done = three_passes(nc, up[slot][:, :], rows_of(w_up, u), x)
                    if routed:
                        if u == 0:
                            pe.wait_ge(router.w_copied, t + 1)
                        done = nc.tensor.matmul(share[slot][:, :], k.sel[:, u * P:(u + 1) * P],
                                                router.turned[parity][:, :],
                                                start=True, stop=True)
                    done.then_inc(up_done, 1)
                    if u >= LAG:
                        down(t, u - LAG, parity)
                    elif not is_first(t):
                        down(t - 1, units - LAG + u, 1 - parity)
                    for s in steps:
                        if at[s] == u and not is_last(t):
                            prepare(s, t + 1, 1 - parity)

            over_tiles(pe, tile)
            for u in range(units - LAG, units):
                down(TILES - 1, u, (TILES - 1) % 2)


THIRDS_Q = ((0, 3), (1, 3), (2, 2))
PIECES = SEQ // P
HALF = P // 2
UNITS = 2 * PIECES
STEPS = HEADS * PIECES


def head_projection(nc, k, prefix):
    with ExitStack() as ctx:
        m = Memory(nc, ctx, prefix)
        norm = Norm(nc, k, m, m.ps("bank"))
        product = [[m.ps(f"{x}{i}") for i in range(2)] for x in "qk"]
        v_bank = m.ps("v")
        biased = [m.sb(f"biased{x}", [P, TILE], F32) for x in "qk"]
        rest = [m.sb(f"rest{x}", [P, TILE], F32) for x in "qk"]
        thirds = [[m.sb(f"thirds{x}{i}", [P, 3, TILE], BF16) for i in range(2)] for x in "qk"]
        x_saved, v_done, v_added = m.sems("x_saved v_done v_added")
        qk_done, full_done, first_done, rest_done, second_done, third_done = [
            [m.sem(f"{name}_{x}") for x in "qk"] for name in
            ("qk_done", "full_done", "first_done", "rest_done", "second_done", "third_done")]
        stored = [[m.sem(f"stored_{x}{i}") for i in range(2)] for x in "qk"]
        block = m.block()

        @block.sync
        def _(sync):
            sync.dma_start(k.x_dram, k.xT[:, :]).then_inc(x_saved, 16)

            def tile(t, parity):
                for x in range(2):
                    wait_first(sync, third_done[x], t + 1)
                    for n in range(3):
                        out = k.thirds_dram[x][n]
                        at = out[:, :, t, :] if isinstance(t, int) else out[:, :, bass.ds(t, 1), :]
                        sync.dma_start(at, thirds[x][parity][:, n, :].rearrange(
                            "p (c q) -> p c q", c=PIECES)).then_inc(stored[x][parity], 16)

            over_tiles(sync, tile)
            for x in range(2):
                for parity in range(2):
                    sync.wait_ge(stored[x][parity], 16 * 3 * TILES // 2)

        @block.scalar
        def _(act):
            def tile(t, parity):
                if not is_last(t):
                    norm.copy_in(act, t + 1)
                for x in range(2):
                    act.wait_ge(qk_done[x], t + 1)
                    wait(act, rest_done[x], t)
                    nc.scalar.activation(biased[x][:, :], product[x][parity][:, :], ACT.Identity,
                                         bias=k.biases[:, x:x + 1]).then_inc(full_done[x], 1)
                    if isinstance(t, int):
                        wait(act, stored[x][parity], 48 * (t // 2))
                    else:
                        act.wait_ge(stored[x][parity], (t - parity) * 24)
                    nc.scalar.activation(thirds[x][parity][:, 0, :], product[x][parity][:, :],
                                         ACT.Identity,
                                         bias=k.biases[:, x:x + 1]).then_inc(first_done[x], 1)
                if not is_last(t):
                    wait(act, v_done, t + 1)
                    norm.cut_high(act, t + 1, 1 - parity)

            norm.copy_in(act, 0)
            norm.cut_high(act, 0, 0)
            over_tiles(act, tile)

        @block.gpsimd
        def _(pool):
            def tile(t, parity):
                if not is_last(t):
                    norm.deviation(pool, t + 1)
                for x in range(2):
                    pool.wait_ge(second_done[x], t + 1)
                    nc.gpsimd.tensor_tensor(thirds[x][parity][:, 2, :], rest[x][:, :],
                                            thirds[x][parity][:, 1, :],
                                            ALU.subtract).then_inc(third_done[x], 1)

            norm.deviation(pool, 0)
            over_tiles(pool, tile)

        @block.vector
        def _(dve):
            def tile(t, parity):
                for x in range(2):
                    dve.wait_ge(full_done[x], t + 1)
                    dve.wait_ge(first_done[x], t + 1)
                    wait(dve, third_done[x], t)
                    nc.vector.tensor_tensor(rest[x][:, :], biased[x][:, :],
                                            thirds[x][parity][:, 0, :],
                                            ALU.subtract).then_inc(rest_done[x], 1)
                    dve.wait_ge(rest_done[x], t + 1)
                    nc.vector.tensor_copy(thirds[x][parity][:, 1, :],
                                          rest[x][:, :]).then_inc(second_done[x], 1)
                if not is_last(t):
                    norm.moments(dve, t + 1)
                    norm.aggregate(dve, t + 1)
                dve.wait_ge(v_done, t + 1)
                dve.wait_ge(x_saved, 16)
                dve.wait_ge(norm.x_copied, t + 1)
                nc.vector.tensor_tensor(chunks(column(k.xT, t)), chunks(v_bank[:, :]),
                                        k.bv_row[:, :].unsqueeze(1).broadcast_to([P, CH, P]),
                                        ALU.add).then_inc(v_added, 1)
                if not is_last(t):
                    norm.norm_rows(dve, t + 1, 1 - parity)
                    norm.cut_low(dve, t + 1, 1 - parity)

            norm.moments(dve, 0)
            norm.aggregate(dve, 0)
            norm.norm_rows(dve, 0, 0)
            norm.cut_low(dve, 0, 0)
            over_tiles(dve, tile)

        @block.tensor
        def _(pe):
            def tile(t, parity):
                pe.wait_ge(norm.n_copied, t + 1)
                pe.wait_ge(norm.n_high, t + 1)
                pe.wait_ge(norm.n_low, t + 1)
                wait(pe, v_added, t)
                for c in range(CH):
                    part = nc.tensor.matmul(v_bank[:, c * P:(c + 1) * P],
                                            norm.full[:, c * P:(c + 1) * P], k.wv_full[:, 0:P],
                                            start=True, stop=True)
                part.then_inc(v_done, 1)
                for x in range(2):
                    wait(pe, first_done[x], t - 1)
                    wait(pe, full_done[x], t - 1)
                    three_passes(nc, product[x][parity][:, :], k.proj_part(x),
                                 (norm.high[parity][:, :], norm.low[parity][:, :])
                                 ).then_inc(qk_done[x], 1)
                if not is_last(t):
                    norm.turn(pe, t + 1)
                    norm.turn_back(pe, t + 1, 1 - parity)

            norm.turn(pe, 0)
            norm.turn_back(pe, 0, 0)
            over_tiles(pe, tile)


def batch_attention(nc, k, prefix):
    BUFS = 4
    LAG = 3
    with ExitStack() as ctx:
        m = Memory(nc, ctx, prefix)
        score = [m.ps(f"score{i}", (P, BATCH * HALF)) for i in range(3)]
        heads_bank = m.ps("heads")
        keys = m.sb("keys", [STACK, PIECES, BATCH * P], BF16)
        queries = m.sb("queries", [STACK, 3, BATCH * P], BF16)
        e = [m.sb(f"e{i}", [P, BATCH, P], F32) for i in range(BUFS)]
        top = [m.sb(f"top{i}", [P, HALF], F32R) for i in range(2)]
        total = [m.sb(f"total{i}", [P, P], F32) for i in range(2)]
        log = m.sb("log", [P, P], F32)
        inverse = [m.sb(f"inverse{i}", [P, P], F32) for i in range(2)]
        values = m.sb("values", [P, PIECES, BATCH, 32], F32)
        heads_out = m.sb("heads_out", [P, 3, TILE], F32)
        minus = m.sb("minus", [P, P], F32R)
        (zeroed, minus_set, queries_loaded, stored, scored, top_done, shifted, e_done, summed, log_done, inverse_done, normed, v_copied,
         weighted, copied) = m.sems("zeroed minus_set queries_loaded stored scored top_done shifted e_done summed "
                                    "log_done inverse_done normed v_copied weighted copied")
        keys_loaded = [m.sem(f"keys_loaded{i}") for i in range(PIECES)]
        v = k.xT[:, :].rearrange("p (b c n) -> p b c n", b=BATCH, c=PIECES)
        block = m.block()

        def rows(head):
            return slice(head * DK, (head + 1) * DK) if isinstance(head, int) else \
                bass.ds(head * DK, DK)

        @block.sync
        def _(sync):
            def load_keys(head, c):
                first = 0
                for count in (3, 3, 2):
                    for n in range(count):
                        sync.dma_start(keys[first:first + DK, c, :],
                                       k.thirds_dram[1][n, rows(head), c, :, :].rearrange(
                                           "d b q -> d (b q)")).then_inc(keys_loaded[c], 16)
                        first += DK

            def place(tensor, rows_, step):
                if isinstance(step, int):
                    return tensor[rows_, step % 3, :]
                return tensor[rows_, bass.ds(step % 3, 1), :].squeeze(1)

            def load_queries(step, head, c):
                wait_first(sync, queries_loaded, step * (16 * TERMS))
                first = 0
                for n, count in THIRDS_Q:
                    for _ in range(count):
                        sync.dma_start(place(queries, slice(first, first + DK), step),
                                       k.thirds_dram[0][n, rows(head), c, :, :].rearrange(
                                           "d b q -> d (b q)")).then_inc(queries_loaded, 16)
                        first += DK

            def store(step, head, c):
                wait_first(sync, copied, step + 1)
                wait_first(sync, stored, step * 64)
                out = k.heads_dram[rows(head), :].rearrange("d (j g c q) -> d g j c q",
                                                            g=4, c=PIECES, q=P)
                for g in range(4):
                    sync.dma_start(out[:, g, :, c, :],
                                   place(heads_out, slice(32 * g, 32 * g + DK), step).rearrange(
                                       "d (j q) -> d j q", j=4)).then_inc(stored, 16)

            def head_steps(head, first, last):
                for c in range(PIECES):
                    step = head * PIECES + c
                    if c == PIECES - 1 and not last:
                        for piece in range(PIECES):
                            wait_first(sync, scored, step * UNITS + 2 * piece + 2)
                            load_keys(head + 1, piece)
                    if not (last and c >= PIECES - 2):
                        wait_first(sync, scored, step * UNITS)
                        load_queries(step + 2, head + (c + 2) // PIECES, (c + 2) % PIECES)
                    if c:
                        store(step - 1, head, c - 1)
                    elif not first:
                        store(step - 1, head - 1, PIECES - 1)

            for c in range(PIECES):
                load_keys(0, c)
                if c < 2:
                    load_queries(c, 0, c)
            head_steps(0, True, False)
            with sync.Fori(1, HEADS - 1) as head:
                head_steps(head, False, False)
            head_steps(HEADS - 1, False, True)
            store(STEPS - 1, HEADS - 1, PIECES - 1)
            sync.wait_ge(stored, 16 * 4 * STEPS)

        def over_steps(eng, body):
            for r in range(3):
                body(r, r)
            with eng.Fori(1, STEPS // 3) as i:
                for r in range(3):
                    body(i * 3 + r, r)
            body(STEPS - 1, 0)

        def begins(s):
            return isinstance(s, int) and s == 0

        def ends(s):
            return isinstance(s, int) and s == STEPS - 1

        @block.tensor
        def _(pe):
            def scores(n, r, u):
                c, half, slot = u // 2, u % 2, (2 * r + u) % 3
                wait(pe, e_done, n - 2)
                for b in range(BATCH):
                    part = nc.tensor.matmul(
                        score[slot][:, b * HALF:(b + 1) * HALF], keys[:, c, b * P:(b + 1) * P],
                        queries[:, r, b * P + half * HALF:b * P + (half + 1) * HALF],
                        start=(b % 8 == 0), stop=False, skip_group_check=True)
                part.then_inc(scored, 1)

            def shift(n, slot, half):
                pe.wait_ge(top_done, n + 1)
                for bank in range(2):
                    part = nc.tensor.matmul(
                        score[slot][:, bank * 512:(bank + 1) * 512], minus[:, :],
                        top[half][:, :].unsqueeze(1).broadcast_to([P, 8, HALF]),
                        start=False, stop=True, skip_group_check=True)
                part.then_inc(shifted, 1)

            def values_of(pair, c, step, head):
                pe.wait_ge(normed, pair + 1)
                pe.wait_ge(v_copied, head * PIECES + c + 1)
                if c == 0:
                    wait(pe, copied, step)
                for b in range(BATCH):
                    g, j = b % 4, b // 4
                    part = nc.tensor.matmul(
                        heads_bank[32 * g:32 * g + 32, j * P:(j + 1) * P], values[:, c, b, :],
                        e[c][:, b, :], start=(c == 0 and j == 0), stop=(c == PIECES - 1),
                        skip_group_check=True)
                part.then_inc(weighted, 1)

            def score_unit(s, r, u):
                if u % 2 == 0:
                    pe.wait_ge(queries_loaded, (s + 1) * (16 * TERMS))
                    pe.wait_ge(keys_loaded[u // 2], (s // PIECES + 1) * (16 * TERMS))
                scores(s * UNITS + u, r, u)

            def step(s, r):
                for c in range(PIECES):
                    for u in (2 * c, 2 * c + 1):
                        shift(s * UNITS + u, (2 * r + u) % 3, u % 2)
                    for u in (2 * c + 2, 2 * c + 3):
                        if u < UNITS:
                            score_unit(s, r, u)
                        elif not ends(s):
                            score_unit(s + 1, (r + 1) % 3, u - UNITS)
                    if c == LAG:
                        values_of(s * PIECES, 0, s, s // PIECES)
                    elif not begins(s):
                        values_of(s * PIECES + c - LAG, c + PIECES - LAG, s - 1,
                                  (s - 1) // PIECES)

            pe.wait_ge(minus_set, 1)
            for u in range(2):
                score_unit(0, 0, u)
            over_steps(pe, step)
            for c in range(PIECES - LAG, PIECES):
                values_of((STEPS - 1) * PIECES + c, c, STEPS - 1, HEADS - 1)

        @block.vector
        def _(dve):
            def largest(n, slot, half):
                dve.wait_ge(scored, n + 1)
                wait(dve, shifted, n - 1)
                nc.vector.tensor_reduce(
                    top[half][:, :], score[slot][:, :].rearrange("p (b q) -> p q b", b=BATCH),
                    AX.X, ALU.max).then_inc(top_done, 1)

            def add_up(pair, slot):
                dve.wait_ge(e_done, (pair + 1) * 2)
                wait(dve, log_done, pair - 1)
                nc.vector.tensor_reduce(total[slot % 2][:, :], e[slot][:, :, :].rearrange("p b q -> p q b"),
                                        AX.X, ALU.add).then_inc(summed, 1)

            def step(s, r):
                for c in range(PIECES):
                    pair = s * PIECES + c
                    for u in (2 * c, 2 * c + 1):
                        largest(s * UNITS + u, (2 * r + u) % 3, u % 2)
                    if c or not begins(s):
                        add_up(pair - 1, (c - 1) % PIECES)

            nc.vector.tensor_scalar(minus[:, :], k.ident[:, :], -1.0, None,
                                    ALU.mult).then_inc(minus_set, 1)
            over_steps(dve, step)
            add_up(STEPS * PIECES - 1, PIECES - 1)

        @block.scalar
        def _(act):
            def copy_heads(s, r):
                act.wait_ge(weighted, (s + 1) * PIECES)
                wait(act, stored, (s - 2) * 64)
                nc.scalar.activation(heads_out[:, r, :], heads_bank[:, :],
                                     ACT.Copy).then_inc(copied, 1)

            def invert(pair, slot):
                act.wait_ge(summed, pair + 1)
                wait(act, inverse_done, pair)
                nc.scalar.activation(log[:, :], total[slot % 2][:, :], ACT.Ln).then_inc(log_done, 1)
                act.wait_ge(log_done, pair + 1)
                wait(act, normed, pair - 1)
                nc.scalar.activation(inverse[slot % 2][:, :], log[:, :], ACT.Exp,
                                     scale=-1.0).then_inc(inverse_done, 1)

            def step(s, r):
                for u in range(UNITS):
                    c, half, slot = u // 2, u % 2, (2 * r + u) % 3
                    act.wait_ge(shifted, s * UNITS + u + 1)
                    wait(act, weighted, s * PIECES + c - BUFS + 1)
                    nc.scalar.activation(
                        e[c][:, :, half * HALF:(half + 1) * HALF],
                        score[slot][:, :].rearrange("p (b q) -> p b q", b=BATCH),
                        ACT.Exp).then_inc(e_done, 1)
                    if half and (c or not begins(s)):
                        invert(s * PIECES + c - 1, (c - 1) % PIECES)
                    if u == UNITS - 1 and not begins(s):
                        copy_heads(s - 1, (r - 1) % 3)

            nc.scalar.preload_act_table_set("natural_log_exp_and_others")
            over_steps(act, step)
            invert(STEPS * PIECES - 1, PIECES - 1)
            copy_heads(STEPS - 1, 0)

        @block.gpsimd
        def _(pool):
            def head_steps(head):
                for c in range(PIECES):
                    for piece in range(PIECES):
                        pair = (head * PIECES + c) * PIECES + piece
                        if c == 0:
                            wait(pool, weighted, pair - PIECES + 1)
                            at = rows(head)
                            nc.gpsimd.tensor_copy(values[:, piece, :, 0:DK],
                                                  v[:, :, piece, at]).then_inc(v_copied, 1)
                        pool.wait_ge(inverse_done, pair + 1)
                        nc.gpsimd.tensor_tensor(
                            e[piece][:, :, :], e[piece][:, :, :],
                            inverse[piece % 2][:, :].unsqueeze(1).broadcast_to([P, BATCH, P]),
                            ALU.mult).then_inc(normed, 1)

            nc.gpsimd.memset(values[:, :, :, :], 0.0).then_inc(zeroed, 1)
            pool.wait_ge(zeroed, 1)
            head_steps(0)
            with pool.Fori(1, HEADS) as head:
                head_steps(head)


def head_output(nc, k, prefix):
    with ExitStack() as ctx:
        m = Memory(nc, ctx, prefix)
        heads = [m.sb(f"heads{i}", [P, TILE], F32) for i in range(2)]
        high = [m.sb(f"high{i}", [P, TILE], F32R) for i in range(2)]
        low = [m.sb(f"low{i}", [P, TILE], F32R) for i in range(2)]
        x = [m.sb(f"x{i}", [P, TILE], F32) for i in range(2)]
        y = [m.ps(f"y{i}") for i in range(2)]
        high_done, low_done, y_done, added = m.sems("high_done low_done y_done added")
        heads_loaded, x_loaded = [[m.sem(f"{n}_loaded{i}") for i in range(2)]
                                  for n in ("heads", "x")]
        block = m.block()

        @block.sync
        def _(sync):
            def tile(t, parity):
                wait_first(sync, low_done, t - 1)
                sync.dma_start(heads[parity][:, :],
                               column(k.heads_dram, t)).then_inc(heads_loaded[parity], 16)
                wait_first(sync, added, t - 1)
                sync.dma_start(x[parity][:, :],
                               column(k.x_dram, t)).then_inc(x_loaded[parity], 16)

            over_tiles(sync, tile)

        def loaded(eng, sem, t, parity):
            if isinstance(t, int):
                eng.wait_ge(sem[parity], 16 * (t // 2 + 1))
            else:
                eng.wait_ge(sem[parity], (t - parity + 2) * 8)

        @block.scalar
        def _(act):
            def tile(t, parity):
                loaded(act, heads_loaded, t, parity)
                wait(act, y_done, t - 1)
                nc.scalar.activation(high[parity][:, :], heads[parity][:, :],
                                     ACT.Copy).then_inc(high_done, 1)

            over_tiles(act, tile)

        @block.vector
        def _(dve):
            def add(t, parity):
                dve.wait_ge(y_done, t + 1)
                loaded(dve, x_loaded, t, parity)
                nc.vector.scalar_tensor_tensor(column(k.xT, t), y[parity][:, :], k.biases[:, 3:4],
                                               x[parity][:, :], ALU.add,
                                               ALU.add).then_inc(added, 1)

            def tile(t, parity):
                dve.wait_ge(high_done, t + 1)
                wait(dve, y_done, t - 1)
                nc.vector.tensor_tensor(low[parity][:, :], heads[parity][:, :], high[parity][:, :],
                                        ALU.subtract).then_inc(low_done, 1)
                if not is_first(t):
                    add(t - 1, 1 - parity)

            over_tiles(dve, tile)
            add(TILES - 1, 1)

        @block.tensor
        def _(pe):
            def tile(t, parity):
                pe.wait_ge(low_done, t + 1)
                pe.wait_ge(high_done, t + 1)
                wait(pe, added, t - 1)
                three_passes(nc, y[parity][:, :], k.proj_part(3),
                             (high[parity][:, :], low[parity][:, :])).then_inc(y_done, 1)

            over_tiles(pe, tile)


def sequence_attention(nc, k, prefix):
    with ExitStack() as ctx:
        m = Memory(nc, ctx, prefix)
        norm = Norm(nc, k, m, m.ps("bank"))
        project = [m.ps(f"project{i}") for i in range(2)]
        score = [m.ps(f"score{i}") for i in range(2)]
        turned_bank = [m.ps(f"turned_bank{i}") for i in range(2)]
        y = m.ps("y")
        full = [m.sb(f"full_{x}", [P, TILE], F32) for x in "qk"]
        high = [[m.sb(f"high_{x}{i}", [P, TILE], F32R) for i in range(2)] for x in "qk"]
        low = [[m.sb(f"low_{x}{i}", [P, TILE], F32R) for i in range(2)] for x in "qk"]
        v = [m.sb(f"v{i}", [P, TILE], F32) for i in range(2)]
        top = [m.sb(f"top{i}", [P, 1], F32) for i in range(2)]
        e = [m.sb(f"e{i}", [P, SEQ], F32) for i in range(2)]
        total = [m.sb(f"total{i}", [P, 1], F32) for i in range(2)]
        inverse = [m.sb(f"inverse{i}", [P, 1], F32) for i in range(2)]
        weight = [m.sb(f"weight{i}", [P, SEQ], F32) for i in range(2)]
        turned = [m.sb(f"turned{i}", [P, SEQ], F32) for i in range(2)]
        (v_done, v_copied, scored, top_done, e_done, inverse_done, scaled, w_turned, w_copied,
         weighted, added) = m.sems("v_done v_copied scored top_done e_done inverse_done scaled "
                                   "w_turned w_copied weighted added")
        qk_done, full_done, high_done, low_done = [
            [m.sem(f"{name}_{x}") for x in "qk"] for name in
            ("qk_done", "full_done", "high_done", "low_done")]
        block = m.block()

        def has_second_next(t):
            return not isinstance(t, int) or t < TILES - 2

        @block.scalar
        def _(act):
            def cut(t, parity):
                for x in range(2):
                    act.wait_ge(qk_done[x], t + 1)
                    wait(act, low_done[x], t)
                    nc.scalar.activation(full[x][:, :], project[x][:, :],
                                         ACT.Copy).then_inc(full_done[x], 1)
                    wait(act, scored, (t - 1) * PIECES)
                    nc.scalar.activation(high[x][parity][:, :], project[x][:, :],
                                         ACT.Copy).then_inc(high_done[x], 1)

            def copy_v(t, parity):
                act.wait_ge(v_done, t + 1)
                wait(act, weighted, (t - 1) * PIECES)
                nc.scalar.activation(v[parity][:, :], project[0][:, :],
                                     ACT.Copy).then_inc(v_copied, 1)

            def copy_turned(n, slot):
                act.wait_ge(w_turned, n + 1)
                wait(act, weighted, n - 1)
                nc.scalar.activation(turned[slot][:, :], turned_bank[slot][:, :],
                                     ACT.Copy).then_inc(w_copied, 1)

            def tile(t, parity):
                for c in range(PIECES):
                    n, slot = t * PIECES + c, c % 2
                    act.wait_ge(top_done, n + 1)
                    wait(act, inverse_done, n - 1)
                    wait(act, scaled, n - 1)
                    nc.scalar.activation(e[slot][:, :], score[slot][:, :], ACT.Exp,
                                         bias=top[slot][:, 0:1],
                                         accum_out=total[slot][:, 0:1]).then_inc(e_done, 1)
                    if c >= 2 or not is_first(t):
                        copy_turned(n - 2, slot)
                    if not is_last(t):
                        if c == 1:
                            wait(act, v_done, t + 1)
                            norm.cut_high(act, t + 1, 1 - parity)
                        elif c == 2:
                            cut(t + 1, 1 - parity)
                        elif c == 3:
                            copy_v(t + 1, 1 - parity)
                    if c == 1 and has_second_next(t):
                        norm.copy_in(act, t + 2)

            norm.copy_in(act, 0)
            norm.cut_high(act, 0, 0)
            cut(0, 0)
            copy_v(0, 0)
            norm.copy_in(act, 1)
            over_tiles(act, tile)
            copy_turned(TILES * PIECES - 2, 0)
            copy_turned(TILES * PIECES - 1, 1)

        @block.gpsimd
        def _(pool):
            def cut(t, parity):
                for x in range(2):
                    pool.wait_ge(full_done[x], t + 1)
                    pool.wait_ge(high_done[x], t + 1)
                    nc.gpsimd.tensor_tensor(low[x][parity][:, :], full[x][:, :],
                                            high[x][parity][:, :],
                                            ALU.subtract).then_inc(low_done[x], 1)

            def tile(t, parity):
                if not is_last(t):
                    cut(t + 1, 1 - parity)
                if has_second_next(t):
                    norm.deviation(pool, t + 2)

            norm.deviation(pool, 0)
            cut(0, 0)
            norm.deviation(pool, 1)
            over_tiles(pool, tile)

        @block.vector
        def _(dve):
            def largest(n, slot):
                dve.wait_ge(scored, n + 1)
                wait(dve, e_done, n - 1)
                nc.vector.tensor_reduce(top[slot][:, 0:1], score[slot][:, :], AX.X, ALU.max,
                                        negate=True).then_inc(top_done, 1)

            def scale(n, slot):
                dve.wait_ge(e_done, n + 1)
                nc.vector.reciprocal(inverse[slot][:, 0:1],
                                     total[slot][:, 0:1]).then_inc(inverse_done, 1)
                dve.wait_ge(inverse_done, n + 1)
                wait(dve, w_turned, n - 1)
                nc.vector.tensor_scalar(weight[slot][:, :], e[slot][:, :], inverse[slot][:, 0:1],
                                        NORM, ALU.mult, ALU.mult).then_inc(scaled, 1)

            def add(t):
                dve.wait_ge(weighted, (t + 1) * PIECES)
                nc.vector.tensor_tensor(column(k.xT, t), y[:, :], column(k.xT, t),
                                        ALU.add).then_inc(added, 1)

            def tile(t, parity):
                for c in range(PIECES):
                    n, slot = t * PIECES + c, c % 2
                    largest(n, slot)
                    if c or not is_first(t):
                        scale(n - 1, 1 - slot)
                    if c == 2 and not is_first(t):
                        add(t - 1)
                    if not is_last(t):
                        if c == 0:
                            norm.norm_rows(dve, t + 1, 1 - parity)
                        elif c == 1:
                            norm.cut_low(dve, t + 1, 1 - parity)
                    if c == 3 and has_second_next(t):
                        norm.moments(dve, t + 2)
                        norm.aggregate(dve, t + 2)

            norm.moments(dve, 0)
            norm.aggregate(dve, 0)
            norm.norm_rows(dve, 0, 0)
            norm.cut_low(dve, 0, 0)
            norm.moments(dve, 1)
            norm.aggregate(dve, 1)
            over_tiles(dve, tile)
            scale(TILES * PIECES - 1, 1)
            add(TILES - 1)

        @block.tensor
        def _(pe):
            def projections(t, parity):
                pe.wait_ge(norm.n_copied, t + 1)
                pe.wait_ge(norm.n_high, t + 1)
                pe.wait_ge(norm.n_low, t + 1)
                for x in range(2):
                    if x == 0:
                        wait(pe, v_copied, t)
                    else:
                        wait(pe, high_done[x], t)
                    three_passes(nc, project[x][:, :], k.proj_part(4 + x),
                                 (norm.high[parity][:, :], norm.low[parity][:, :])
                                 ).then_inc(qk_done[x], 1)

            def project_v(t):
                pe.wait_ge(high_done[0], t + 1)
                pe.wait_ge(full_done[0], t + 1)
                for c in range(CH):
                    part = nc.tensor.matmul(project[0][:, c * P:(c + 1) * P],
                                            norm.full[:, c * P:(c + 1) * P],
                                            k.wv_full[:, P:2 * P], start=True, stop=True)
                part.then_inc(v_done, 1)

            def scores(n, c, parity):
                wait(pe, e_done, n - 1)
                (qh, ql), (kh, kl) = [(high[x][parity], low[x][parity]) for x in range(2)]
                three_passes(nc, score[c % 2][:, :],
                             (qh[:, c * P:(c + 1) * P], ql[:, c * P:(c + 1) * P]),
                             (kh[:, :], kl[:, :])).then_inc(scored, 1)

            def turn_weights(n, slot):
                pe.wait_ge(scaled, n + 1)
                wait(pe, w_copied, n - 1)
                for c in range(PIECES):
                    part = nc.tensor.transpose(turned_bank[slot][:, c * P:(c + 1) * P],
                                               weight[slot][:, c * P:(c + 1) * P], k.ident[:, :])
                part.then_inc(w_turned, 1)

            def weigh(t, c, parity):
                pe.wait_ge(w_copied, t * PIECES + c + 1)
                if c == 0:
                    pe.wait_ge(v_copied, t + 1)
                    wait(pe, added, t)
                for piece in range(PIECES):
                    part = nc.tensor.matmul(y[:, c * P:(c + 1) * P],
                                            v[parity][:, piece * P:(piece + 1) * P],
                                            turned[c % 2][:, piece * P:(piece + 1) * P],
                                            start=(piece == 0), stop=(piece == PIECES - 1))
                part.then_inc(weighted, 1)

            def tile(t, parity):
                for x in range(2):
                    pe.wait_ge(high_done[x], t + 1)
                    pe.wait_ge(low_done[x], t + 1)
                for c in range(PIECES):
                    n = t * PIECES + c
                    scores(n, c, parity)
                    if c == 3 and has_second_next(t):
                        norm.turn(pe, t + 2)
                    if c >= 2 or not is_first(t):
                        turn_weights(n - 2, c % 2)
                    if c >= 3:
                        weigh(t, c - 3, parity)
                    elif not is_first(t):
                        weigh(t - 1, c + 1, 1 - parity)
                    if not is_last(t):
                        if c == 1:
                            norm.turn_back(pe, t + 1, 1 - parity)
                        elif c == 2:
                            projections(t + 1, 1 - parity)
                        elif c == 3:
                            project_v(t + 1)

            norm.turn(pe, 0)
            norm.turn_back(pe, 0, 0)
            projections(0, 0)
            project_v(0)
            norm.turn(pe, 1)
            over_tiles(pe, tile)
            turn_weights(TILES * PIECES - 2, 0)
            weigh(TILES - 1, 1, 1)
            turn_weights(TILES * PIECES - 1, 1)
            weigh(TILES - 1, 2, 1)
            weigh(TILES - 1, 3, 1)


def program(nc, ins, out, phases):
    with ExitStack() as ctx:
        m = Memory(nc, ctx, "")
        k = Kept(m)
        load_block(nc, k, ins)
        for n, phase in enumerate(phases):
            if phase == "moe":
                gated_block(nc, k, f"b{n}_", PAIRS, k.wg, k.wu, k.wd, True)
            elif phase == "ffn":
                gated_block(nc, k, f"b{n}_", HCH, k.ffn_part(0), k.ffn_part(1), k.ffn_part(2),
                            False)
            elif phase == "heads":
                head_projection(nc, k, f"b{n}_")
                batch_attention(nc, k, f"b{n}c_")
                head_output(nc, k, f"b{n}d_")
            elif phase == "attention":
                sequence_attention(nc, k, f"b{n}_")
        store_block(nc, k, out)


def store_block(nc, k, out):
    with ExitStack() as ctx:
        stored = Memory(nc, ctx, "st_").sem("stored")
        block = ctx.enter_context(nc.Block())

        @block.sync
        def _(sync):
            sync.dma_start(out, k.xT[:, :]).then_inc(stored, 16)
            sync.wait_ge(stored, 16)


_PROJECTIONS = ["L0_attn_Wq", "L0_attn_Wk", "L0_attn_Wv", "L0_attn_Wo",
                "L1_attn_Wq", "L1_attn_Wk", "L1_attn_Wv"]
PHASES = ("moe", "heads", "moe", "ffn", "attention", "ffn")


def kernel(**inputs):
    import ml_dtypes
    import concourse.bacc as bacc
    from concourse.bass_utils import run_bass_kernel_spmd

    given = {name: np.asarray(value) for name, value in inputs.items()}
    gate_up, down = given["L0_ffn_gate_up_proj"], given["L0_ffn_down_proj"]

    def pairs(w):
        return w.transpose(2, 0, 1).reshape(P, ROUTED * INNER)

    def by_chunk(w):
        return w.T.reshape(HCH, P, P).transpose(1, 0, 2).reshape(P, HIDDEN)

    third_row, column_ = np.arange(3 * ROUTED)[:, None], np.arange(ROUTED * INNER)[None, :]
    arrays = {
        "xT": given["L0_attn_x"].reshape(TOKENS, P).T,
        "wg": pairs(gate_up[:ROUTED, :INNER]),
        "wu": pairs(gate_up[:ROUTED, INNER:]),
        "wd": down.transpose(0, 2, 1).reshape(PAIRS, P, P).transpose(1, 0, 2).reshape(P, -1),
        "wc": given["L0_ffn_classifier_weight"].T,
        "bias": given["L0_ffn_e_score_correction_bias"],
        "proj": np.concatenate([given[name].T for name in _PROJECTIONS], axis=1),
        "ffn": np.concatenate([given["L1_ffn_w_gate"].T, given["L1_ffn_w_up"].T,
                               by_chunk(given["L1_ffn_w_down"])], axis=1),
        "biases": np.stack([given[f"L0_attn_b{x}"] for x in "qkvo"], axis=1),
        "wv_full": np.concatenate([given["L0_attn_Wv"].T, given["L1_attn_Wv"].T], axis=1),
        "bv": given["L0_attn_bv"],
        "sel": (third_row % ROUTED == column_ // INNER).astype(ml_dtypes.bfloat16),
        "ident": np.eye(P, dtype=np.float32),
        "identb": np.eye(P, dtype=ml_dtypes.bfloat16),
    }
    arrays = {name: np.ascontiguousarray(a) for name, a in arrays.items()}

    nc = bacc.Bacc("TRN2", target_bir_lowering=False, num_devices=1)
    ins = {name: nc.dram_tensor("in_" + name, a.shape, mybir.dt.from_np(a.dtype),
                                kind="ExternalInput").ap() for name, a in arrays.items()}
    out = nc.dram_tensor("out_xT", (P, TOKENS), F32, kind="ExternalOutput").ap()
    program(nc, ins, out, PHASES)
    run = run_bass_kernel_spmd(nc, [{"in_" + name: a for name, a in arrays.items()}],
                               core_ids=[0])
    return run.results[0]["out_xT"].T.reshape(BATCH, SEQ, P)
```

```python
from contextlib import ExitStack

import numpy as np

import concourse.bass as bass
from concourse import mybir

F32 = mybir.dt.float32
F32R = mybir.dt.float32r
BF16 = mybir.dt.bfloat16
I32 = mybir.dt.int32
ALU = mybir.AluOpType
ACT = mybir.ActivationFunctionType
AX = mybir.AxisListType

P = 128
BATCH, SEQ = 16, 512
TOKENS = BATCH * SEQ
TILE = 512
TILES = TOKENS // TILE
CH = TILE // P
EPS = 1e-5

ROUTED, ZERO, TOPK = 32, 8, 6
EXPERTS = ROUTED + ZERO
INNER = 64
SLICE = P // ROUTED
SLICES = INNER // SLICE
ROUTE_SCALE = 2.5 * 0.5
HIDDEN = 384
HCH = HIDDEN // P
DEQUANT = 1.0 / 127.0
SENTINEL = -3.0e38

HEADS, DK = 16, 8
TERMS = 8
STACK = TERMS * DK
NORM = 1.0 / float(np.sqrt(128.0))


def wait(eng, sem, value):
    if isinstance(value, int) and value <= 0:
        return
    eng.wait_ge(sem, value)


def wait_first(eng, sem, value):
    if isinstance(value, int):
        return wait(eng, sem, value)
    value = eng.snap(value)
    eng.wait_ge(sem, 1)
    eng.wait_ge(sem, value)


class Chain:

    def __init__(self, eng, sem, per):
        self.eng, self.sem, self.per, self.at = eng, sem, per, 0

    def tile(self, t):
        self.base, self.at = t * self.per, 0

    def link(self, ins):
        self.at += 1
        ins.then_inc(self.sem, 1)
        self.eng.wait_ge(self.sem, self.base + self.at)

    def end(self):
        assert self.at == self.per, self.at


def column(ap, t, width=TILE):
    if isinstance(t, int):
        return ap[:, t * width:(t + 1) * width]
    return ap[:, bass.ds(t * width, width)]


def chunks(ap):
    return ap.rearrange("p (c n) -> p c n", c=CH)


def over(ap, n):
    return ap.unsqueeze(2).broadcast_to([ap.shape[0], ap.shape[1], n])


class Memory:

    def __init__(self, nc, ctx, prefix):
        self.nc, self.ctx, self.prefix, self.semaphores = nc, ctx, prefix, []

    def sb(self, name, shape, dtype):
        return self.ctx.enter_context(self.nc.sbuf_tensor(self.prefix + name, shape, dtype))

    def ps(self, name, shape=(P, 512), dtype=F32):
        return self.ctx.enter_context(self.nc.psum_tensor(self.prefix + name, list(shape), dtype))

    def sem(self, name):
        semaphore = self.ctx.enter_context(self.nc.semaphore(self.prefix + name))
        self.semaphores.append(semaphore)
        return semaphore

    def sems(self, names):
        return [self.sem(name) for name in names.split()]

    def block(self):
        self.ctx.callback(self.clear)
        return self.ctx.enter_context(self.nc.Block())

    def clear(self):
        with self.nc.Block() as clearing:
            @clearing.gpsimd
            def _(pool):
                for semaphore in self.semaphores:
                    pool.sem_clear(semaphore)


def over_tiles(eng, body):
    body(0, 0)
    body(1, 1)
    with eng.Fori(1, TILES // 2 - 1) as i:
        body(i * 2, 0)
        body(i * 2 + 1, 1)
    body(TILES - 2, 0)
    body(TILES - 1, 1)


def is_last(t):
    return isinstance(t, int) and t == TILES - 1


def is_first(t):
    return isinstance(t, int) and t == 0


class Kept:

    def __init__(self, m):
        def parts(name, width):
            return (m.sb(name + "_high", [P, width], F32R), m.sb(name + "_low", [P, width], F32R))

        self.xT = m.sb("xT", [P, TOKENS], F32)
        self.wg, self.wu = parts("wg", SLICES * P), parts("wu", SLICES * P)
        self.wd = parts("wd", SLICES * P)
        self.ffn = parts("ffn", 3 * HIDDEN)
        self.proj = parts("proj", PROJECTIONS * P)
        self.wc = m.sb("wc", [P, EXPERTS], F32)
        self.bias = m.sb("bias", [P, CH, EXPERTS], F32)
        self.sel = m.sb("sel", [3 * ROUTED, P], BF16)
        self.ident = m.sb("ident", [P, P], F32)
        self.identb = m.sb("identb", [P, P], BF16)
        self.biases = m.sb("biases", [P, 4], F32)
        self.minus_half = m.sb("minus_half", [P, CH], F32)
        self.eps = m.sb("eps", [P, CH], F32)
        self.wv_full = m.sb("wv_full", [P, 2 * P], F32)
        self.bv_row = m.sb("bv_row", [P, P], F32)
        self.x_dram = m.nc.dram_tensor("x_kept", (P, TOKENS), F32).ap()
        self.heads_dram = m.nc.dram_tensor("heads_kept", (P, TOKENS), F32).ap()
        self.thirds_dram = [m.nc.dram_tensor(f"thirds_{x}", (3, P, CH, BATCH, P), BF16).ap()
                            for x in "qk"]

    def ffn_part(self, n):
        return [part[:, n * HIDDEN:(n + 1) * HIDDEN] for part in self.ffn]

    def proj_part(self, n):
        return [part[:, n * P:(n + 1) * P] for part in self.proj]


PROJECTIONS = 7


def load_block(nc, k, ins):
    with ExitStack() as ctx:
        m = Memory(nc, ctx, "ld_")
        ints = m.sb("ints", [P, 3 * HIDDEN], I32)
        ints_loaded, dequantised, const_loaded, high_done, low_done, half_set = m.sems(
            "ints_loaded dequantised const_loaded high_done low_done half_set")
        todo = [(ins["wg"], k.wg), (ins["wu"], k.wu), (ins["wd"], k.wd), (ins["proj"], k.proj),
                (None, k.ffn)]
        raw = [m.sb(f"raw{n}", parts[0].shape, F32) for n, (_, parts) in enumerate(todo)]
        loaded = [m.sem(f"loaded{n}") for n in range(len(todo) - 1)]
        consts = [("wc", k.wc), ("sel", k.sel), ("ident", k.ident), ("identb", k.identb),
                  ("biases", k.biases), ("wv_full", k.wv_full)]
        block = m.block()

        @block.sync
        def _(sync):
            for n, (src, parts) in enumerate(todo[:-1]):
                sync.dma_start(raw[n][:, :], src).then_inc(loaded[n], 16)
            sync.dma_start(ints[:, :], ins["ffn"]).then_inc(ints_loaded, 16)

        @block.scalar
        def _(act):
            for c in range(CH):
                act.dma_start(k.bias[:, c, :],
                              ins["bias"].partition_broadcast(P)).then_inc(const_loaded, 16)
            act.dma_start(k.bv_row[:, :], ins["bv"].partition_broadcast(P)).then_inc(const_loaded,
                                                                                     16)
            for name, tensor in consts:
                act.dma_start(tensor[:, :], ins[name]).then_inc(const_loaded, 16)
            for n, (src, (high, _)) in enumerate(todo):
                if src is None:
                    act.wait_ge(dequantised, 1)
                else:
                    act.wait_ge(loaded[n], 16)
                nc.scalar.activation(high[:, :], raw[n][:, :], ACT.Copy).then_inc(high_done, 1)
            act.wait_ge(const_loaded, 16 * (CH + 1 + len(consts)))

        @block.vector
        def _(dve):
            nc.vector.memset(k.minus_half[:, :], -0.5).then_inc(half_set, 1)
            nc.vector.memset(k.eps[:, :], EPS).then_inc(half_set, 1)
            for n, (src, (high, low)) in enumerate(todo):
                if src is None:
                    dve.wait_ge(ints_loaded, 16)
                    nc.vector.tensor_scalar(raw[n][:, :], ints[:, :], DEQUANT, None,
                                            ALU.mult).then_inc(dequantised, 1)
                dve.wait_ge(high_done, n + 1)
                nc.vector.tensor_tensor(low[:, :], raw[n][:, :], high[:, :],
                                        ALU.subtract).then_inc(low_done, 1)


def three_passes(nc, out, w, x, start=True, stop=True):
    (wh, wl), (xh, xl) = w, x
    nc.tensor.matmul(out, wl, xh, start=start, stop=False, skip_group_check=True)
    nc.tensor.matmul(out, wh, xl, start=False, stop=False, skip_group_check=True)
    return nc.tensor.matmul(out, wh, xh, start=False, stop=stop, skip_group_check=True)


class Norm:

    def __init__(self, nc, k, m, bank, back=None, fulls=1):
        self.nc, self.k, self.bank, self.own_back = nc, k, bank, back is not None
        self.back = back if self.own_back else bank
        self.xs = m.sb("xs", [P, TILE], F32)
        self.stats = m.sb("stats", [P, CH, 6], F32)
        self.mv = m.sb("mv", [P, CH, 2], F32)
        self.var = m.sb("var", [P, CH], F32)
        self.rstd = m.sb("rstd", [P, CH], F32)
        self.rows = [m.sb(f"rows{i}", [P, TILE], F32) for i in range(2)]
        self.full = [m.sb(f"full{i}", [P, TILE], F32) for i in range(fulls)]
        self.high = [m.sb(f"high{i}", [P, TILE], F32R) for i in range(2)]
        self.low = [m.sb(f"low{i}", [P, TILE], F32R) for i in range(2)]
        (self.x_copied, self.x_turned, self.stats_done, self.aggregated, self.var_done,
         self.rstd_done, self.normed, self.n_turned, self.n_copied, self.n_high,
         self.n_low) = m.sems("x_copied x_turned stats_done aggregated var_done rstd_done "
                              "normed n_turned n_copied n_high n_low")

    def copy_in(self, act, t):
        wait(act, self.x_turned, t)
        self.nc.scalar.activation(self.xs[:, :], column(self.k.xT, t),
                                  ACT.Copy).then_inc(self.x_copied, 1)

    def turn(self, pe, t):
        pe.wait_ge(self.x_copied, t + 1)
        if self.own_back:
            wait(pe, self.normed, t)
        else:
            self.wait_back(pe, t)
        for c in range(CH):
            part = self.nc.tensor.transpose(self.bank[:, c * P:(c + 1) * P],
                                            self.xs[:, c * P:(c + 1) * P], self.k.ident[:, :])
        part.then_inc(self.x_turned, 1)

    def wait_back(self, pe, t):
        wait(pe, self.n_copied, t)
        wait(pe, self.n_high, t)

    def moments(self, dve, t):
        dve.wait_ge(self.x_turned, t + 1)
        wait(dve, self.aggregated, t)
        for c in range(CH):
            part = self.nc.vector.bn_stats(self.stats[:, c, :], self.bank[:, c * P:(c + 1) * P])
        part.then_inc(self.stats_done, 1)

    def aggregate(self, dve, t):
        dve.wait_ge(self.stats_done, 1)
        dve.wait_ge(self.stats_done, t + 1)
        for c in range(CH):
            part = self.nc.vector.bn_aggr(self.mv[:, c, :], self.stats[:, c, :])
        part.then_inc(self.aggregated, 1)

    def deviation(self, pool, t):
        pool.wait_ge(self.aggregated, t + 1)
        self.nc.gpsimd.tensor_tensor(self.var[:, :], self.mv[:, :, 1], self.k.eps[:, :],
                                     ALU.add).then_inc(self.var_done, 1)
        pool.wait_ge(self.var_done, t + 1)
        self.nc.gpsimd.tensor_tensor(self.rstd[:, :], self.var[:, :], self.k.minus_half[:, :],
                                     ALU.pow).then_inc(self.rstd_done, 1)

    def norm_rows(self, dve, t, parity, which=range(CH)):
        dve.wait_ge(self.rstd_done, t + 1)
        wait(dve, self.n_turned, t - 1)
        for c in which:
            part = self.nc.vector.tensor_scalar(
                self.rows[parity][:, c * P:(c + 1) * P], self.bank[:, c * P:(c + 1) * P],
                self.mv[:, c, 0:1], self.rstd[:, c:c + 1], ALU.subtract, ALU.mult)
        if CH - 1 in which:
            part.then_inc(self.normed, 1)

    def turn_back(self, pe, t, parity):
        pe.wait_ge(self.normed, t + 1)
        if self.own_back:
            self.wait_back(pe, t)
        for c in range(CH):
            part = self.nc.tensor.transpose(self.back[:, c * P:(c + 1) * P],
                                            self.rows[parity][:, c * P:(c + 1) * P],
                                            self.k.ident[:, :])
        part.then_inc(self.n_turned, 1)

    def cut_high(self, act, t, parity):
        act.wait_ge(self.n_turned, t + 1)
        wait(act, self.n_low, t)
        self.nc.scalar.activation(self.full[parity % len(self.full)][:, :], self.back[:, :],
                                  ACT.Copy).then_inc(self.n_copied, 1)
        self.nc.scalar.activation(self.high[parity][:, :], self.back[:, :],
                                  ACT.Copy).then_inc(self.n_high, 1)

    def cut_low(self, dve, t, parity):
        dve.wait_ge(self.n_copied, t + 1)
        dve.wait_ge(self.n_high, t + 1)
        self.nc.vector.tensor_tensor(self.low[parity][:, :],
                                     self.full[parity % len(self.full)][:, :],
                                     self.high[parity][:, :], ALU.subtract).then_inc(self.n_low, 1)


class Router:

    LINKS = 12

    def __init__(self, nc, k, m, norm):
        self.nc, self.k, self.norm, self.bank = nc, k, norm, norm.bank
        self.top = m.sb("top", [P, CH], F32)
        self.z = m.sb("z", [P, CH, EXPERTS], F32)
        self.e = m.sb("e", [P, CH, EXPERTS], F32)
        self.total = m.sb("total", [P, CH], F32)
        self.inverse = m.sb("inverse", [P, CH], F32)
        self.score = m.sb("score", [P, CH, EXPERTS], F32)
        self.biased = m.sb("biased", [P, CH, EXPERTS + 2], F32)
        self.best = m.sb("best", [P, CH, 8], F32)
        self.marked = m.sb("marked", [P, CH, EXPERTS + 2], F32)
        self.mask = m.sb("mask", [P, CH, EXPERTS], F32)
        self.weight = m.sb("weight", [P, CH, EXPERTS], F32)
        self.rest = m.sb("rest", [P, CH, ROUTED], F32)
        self.rest2 = m.sb("rest2", [P, CH, ROUTED], F32)
        self.thirds = m.sb("thirds", [P, CH, 3 * ROUTED], BF16)
        self.zero_weight = m.sb("zero_weight", [P, CH], F32)
        self.diagonal = [m.sb(f"diagonal{i}", [P, CH, P], F32) for i in range(2)]
        self.turned = [m.sb(f"turned{i}", [3 * ROUTED, TILE], BF16) for i in range(2)]
        (self.sentinels, self.logits_done, self.shifted, self.e_done, self.thirds_done,
         self.w_turned, self.w_copied, self.diagonal_done,
         self.biased_done, self.best_done, self.own) = m.sems(
             "sentinels logits_done shifted e_done thirds_done w_turned w_copied diagonal_done "
             "biased_done best_done route_own")

    def chain(self, dve):
        self.steps = Chain(dve, self.own, self.LINKS)

    def logits(self, pe, t):
        norm = self.norm
        pe.wait_ge(norm.n_copied, t + 1)
        pe.wait_ge(norm.n_high, t + 1)
        for c in range(CH):
            part = self.nc.tensor.matmul(self.bank[:, c * EXPERTS:(c + 1) * EXPERTS],
                                         norm.full[0][:, c * P:(c + 1) * P], self.k.wc[:, :],
                                         start=True, stop=True)
        part.then_inc(self.logits_done, 1)

    def shift(self, dve, t):
        logits = self.bank[:, 0:CH * EXPERTS].rearrange("p (c n) -> p c n", c=CH)
        self.steps.tile(t)
        dve.wait_ge(self.logits_done, t + 1)
        self.steps.link(self.nc.vector.tensor_reduce(self.top[:, :], logits, AX.X, ALU.max))
        wait(dve, self.e_done, t)
        self.nc.vector.tensor_tensor(self.z[:, :, :], logits, over(self.top[:, :], EXPERTS),
                                     ALU.subtract).then_inc(self.shifted, 1)

    def exponentials(self, act, t):
        act.wait_ge(self.shifted, t + 1)
        wait(act, self.thirds_done, t)
        self.nc.scalar.activation(self.e[:, :, :], self.z[:, :, :],
                                  ACT.Exp).then_inc(self.e_done, 1)

    def choose(self, dve, t):
        vector, link = self.nc.vector, self.steps.link
        real = self.biased[:, :, 0:EXPERTS]
        dve.wait_ge(self.e_done, t + 1)
        link(vector.tensor_reduce(self.total[:, :], self.e[:, :, :], AX.X, ALU.add))
        link(vector.reciprocal(self.inverse[:, :], self.total[:, :]))
        link(vector.tensor_tensor(self.score[:, :, :], self.e[:, :, :],
                                  over(self.inverse[:, :], EXPERTS), ALU.mult))
        vector.tensor_tensor(real, self.score[:, :, :], self.k.bias[:, :, :],
                             ALU.add).then_inc(self.biased_done, 1)

    def search(self, dve, t):
        vector, link = self.nc.vector, self.steps.link
        dve.wait_ge(self.biased_done, 1)
        dve.wait_ge(self.biased_done, t + 1)
        for c in range(CH):
            part = vector.max(self.best[:, c, :], self.biased[:, c, 0:EXPERTS])
        link(part)
        vector.memset(self.best[:, :, TOPK:8], SENTINEL).then_inc(self.best_done, 1)

    def mark(self, dve, t):
        vector, link = self.nc.vector, self.steps.link
        real = self.biased[:, :, 0:EXPERTS]
        dve.wait_ge(self.best_done, 1)
        dve.wait_ge(self.best_done, t + 1)
        for c in range(CH):
            part = vector.match_replace(self.marked[:, c, :], self.best[:, c, :],
                                        self.biased[:, c, :], -SENTINEL)
        link(part)
        link(vector.tensor_tensor(self.mask[:, :, :], self.marked[:, :, 0:EXPERTS], real,
                                  ALU.not_equal))
        link(vector.scalar_tensor_tensor(self.weight[:, :, :], self.mask[:, :, :], ROUTE_SCALE,
                                         self.score[:, :, :], ALU.mult, ALU.mult))

    def cut(self, dve, t):
        vector, link = self.nc.vector, self.steps.link
        routed = self.weight[:, :, 0:ROUTED]
        third = [self.thirds[:, :, i * ROUTED:(i + 1) * ROUTED] for i in range(3)]
        wait(dve, self.w_turned, t)
        wait(dve, self.diagonal_done, t)
        vector.tensor_reduce(self.zero_weight[:, :], self.weight[:, :, ROUTED:EXPERTS], AX.X,
                             ALU.add)
        link(vector.tensor_copy(third[0], routed))

    def cut_rest(self, dve, t):
        vector, link = self.nc.vector, self.steps.link
        routed = self.weight[:, :, 0:ROUTED]
        third = [self.thirds[:, :, i * ROUTED:(i + 1) * ROUTED] for i in range(3)]
        link(vector.tensor_tensor(self.rest[:, :, :], routed, third[0], ALU.subtract))
        link(vector.tensor_copy(third[1], self.rest[:, :, :]))
        link(vector.tensor_tensor(self.rest2[:, :, :], self.rest[:, :, :], third[1],
                                  ALU.subtract))
        vector.tensor_copy(third[2], self.rest2[:, :, :]).then_inc(self.thirds_done, 1)
        self.steps.end()

    def diagonals(self, pool, t, parity):
        pool.wait_ge(self.thirds_done, t + 1)
        for c in range(CH):
            part = self.nc.gpsimd.tensor_tensor(
                self.diagonal[parity][:, c, :], self.k.ident[:, :],
                self.zero_weight[:, c:c + 1].broadcast_to([P, P]), ALU.mult)
        part.then_inc(self.diagonal_done, 1)

    def turn(self, pe, t):
        bank = self.bank[:, :].bitcast(BF16)
        pe.wait_ge(self.thirds_done, t + 1)
        for c in range(CH):
            part = self.nc.tensor.transpose(bank[0:3 * ROUTED, c * P:(c + 1) * P],
                                            self.thirds[:, c, :], self.k.identb[:, :])
        part.then_inc(self.w_turned, 1)

    def copy_turned(self, act, t, parity):
        act.wait_ge(self.w_turned, t + 1)
        self.nc.scalar.activation(self.turned[parity][:, :],
                                  self.bank[:, :].bitcast(BF16)[0:3 * ROUTED, 0:TILE],
                                  ACT.Copy).then_inc(self.w_copied, 1)


def gated_block(nc, k, prefix, units, w_gate, w_up, w_down, routed, source=None, sink=None):
    LAG = 3
    hold = 4 if routed else 3
    with ExitStack() as ctx:
        m = Memory(nc, ctx, prefix)
        gate = [m.ps(f"gate{i}") for i in range(2)]
        up = [m.ps(f"up{i}") for i in range(2)]
        y, bank = m.ps("y"), m.ps("bank")
        norm = Norm(nc, k, m, bank, None if routed else m.ps("back"))
        gated = [m.sb(f"gated{i}", [P, TILE], F32) for i in range(2)]
        h = [m.sb(f"h{i}", [P, TILE], F32) for i in range(2)]
        h_high = [m.sb(f"h_high{i}", [P, TILE], F32R) for i in range(hold)]
        h_low = [m.sb(f"h_low{i}", [P, TILE], F32R) for i in range(hold)]
        (gate_done, up_done, silu_done, h_done, high_done, low_done, down_done, y_done,
         y_added) = m.sems("gate_done up_done silu_done h_done high_done low_done down_done "
                           "y_done y_added")
        x_loaded, stored = m.sems("x_loaded stored")
        if routed:
            share = [m.ps(f"share{i}") for i in range(2)]
            product = m.sb("product", [P, TILE], F32)
            share_done, product_done = m.sems("share_done product_done")
            router = Router(nc, k, m, norm)
            at = dict(copy=0, turn=1, moments=1, aggregate=2, deviation=2, rows_a=3, rows_b=4,
                      back=5, high=6, low=6, logits=7, shift=8, exp=9, choose=10, search=11,
                      mark=12, cut=13, cut_rest=13, diagonals=14, w_turn=15, w_copy=15)
        else:
            at = dict(copy=0, turn=1, moments=1, aggregate=1, deviation=1, rows_a=2, rows_b=2,
                      back=1, high=1, low=1)
        far = () if routed else ("copy", "turn", "moments", "aggregate", "deviation", "rows_a",
                                 "rows_b")
        block = m.block()

        def prepare_first(steps, prepare):
            for t in range(2 if far else 1):
                for s in steps:
                    if t == 0 or s in far:
                        prepare(s, t, t)

        def prepare_next(steps, prepare, t, parity, u):
            for s in steps:
                if at[s] != u:
                    continue
                if s in far and not (isinstance(t, int) and t >= TILES - 2):
                    prepare(s, t + 2, parity)
                elif s not in far and not is_last(t):
                    prepare(s, t + 1, 1 - parity)

        @block.sync
        def _(sync):
            def load(t, parity):
                wait_first(sync, x_loaded, t * 16)
                sync.dma_start(column(k.xT, t), column(source, t)).then_inc(x_loaded, 16)

            def store(t, parity):
                wait_first(sync, y_added, t + 1)
                sync.dma_start(column(sink, t), column(k.xT, t)).then_inc(stored, 16)

            if source is not None:
                over_tiles(sync, load)
            if sink is not None:
                over_tiles(sync, store)
                sync.wait_ge(stored, 16 * TILES)

        @block.scalar
        def _(act):
            def high(n, u, slot):
                act.wait_ge(h_done, n + 1)
                wait(act, down_done, n - hold + 1)
                nc.scalar.activation(h_high[u % hold][:, :], h[slot][:, :],
                                     ACT.Copy).then_inc(high_done, 1)

            def prepare(s, t, parity):
                if s == "copy":
                    if source is not None:
                        act.wait_ge(x_loaded, (t + 1) * 16)
                    norm.copy_in(act, t)
                elif s == "high":
                    wait(act, up_done, units * (t - 1))
                    if routed:
                        wait(act, router.logits_done, t)
                    norm.cut_high(act, t, parity)
                elif s == "exp":
                    router.exponentials(act, t)
                elif s == "w_copy":
                    router.copy_turned(act, t, parity)

            steps = [s for s in ("copy", "high", "exp", "w_copy") if s in at]
            prepare_first(steps, prepare)

            def tile(t, parity):
                for u in range(units):
                    n = t * units + u
                    slot = (parity * units + u) % 2
                    act.wait_ge(gate_done, n + 1)
                    wait(act, h_done, n - 1)
                    nc.scalar.activation(gated[slot][:, :], gate[slot][:, :],
                                         ACT.Silu).then_inc(silu_done, 1)
                    if u:
                        high(n - 1, u - 1, 1 - slot)
                    prepare_next(steps, prepare, t, parity, u)
                high(n, u, slot)

            over_tiles(act, tile)

        @block.gpsimd
        def _(pool):
            def prepare(s, t, parity):
                if s == "deviation":
                    norm.deviation(pool, t)
                elif s == "diagonals":
                    wait(pool, y_done, t - 1)
                    router.diagonals(pool, t, parity)

            steps = [s for s in ("deviation", "diagonals") if s in at]
            prepare_first(steps, prepare)

            def tile(t, parity):
                for u in range(units):
                    n = t * units + u
                    slot = (parity * units + u) % 2
                    prepare_next(steps, prepare, t, parity, u)
                    pool.wait_ge(high_done, n + 1)
                    nc.gpsimd.tensor_tensor(h_low[u % hold][:, :], h[slot][:, :],
                                            h_high[u % hold][:, :],
                                            ALU.subtract).then_inc(low_done, 1)

            over_tiles(pool, tile)

        @block.vector
        def _(dve):
            if routed:
                router.chain(dve)
                nc.vector.memset(router.biased[:, :, EXPERTS:EXPERTS + 2],
                                 SENTINEL).then_inc(router.sentinels, 1)
                dve.wait_ge(router.sentinels, 1)

            def prepare(s, t, parity):
                if s == "moments":
                    norm.moments(dve, t)
                elif s == "aggregate":
                    norm.aggregate(dve, t)
                elif s == "rows_a":
                    if routed:
                        wait(dve, y_done, t - 1)
                    norm.norm_rows(dve, t, parity, range(CH // 2))
                elif s == "rows_b":
                    norm.norm_rows(dve, t, parity, range(CH // 2, CH))
                elif s == "low":
                    norm.cut_low(dve, t, parity)
                elif s == "shift":
                    router.shift(dve, t)
                elif s == "choose":
                    router.choose(dve, t)
                elif s == "search":
                    router.search(dve, t)
                elif s == "mark":
                    router.mark(dve, t)
                elif s == "cut":
                    router.cut(dve, t)
                elif s == "cut_rest":
                    router.cut_rest(dve, t)

            steps = [s for s in ("moments", "aggregate", "rows_a", "rows_b", "low", "shift",
                                 "choose", "search", "mark", "cut", "cut_rest") if s in at]
            prepare_first(steps, prepare)

            def add(t):
                if routed:
                    dve.wait_ge(y_done, t + 1)
                else:
                    dve.wait_ge(down_done, (t + 1) * units)
                nc.vector.scalar_tensor_tensor(column(k.xT, t), y[:, :], 1.0 if routed else 0.5,
                                               column(k.xT, t), ALU.mult,
                                               ALU.add).then_inc(y_added, 1)

            def tile(t, parity):
                for u in range(units):
                    n = t * units + u
                    slot = (parity * units + u) % 2
                    dve.wait_ge(silu_done, n + 1)
                    if routed:
                        if u == 0:
                            dve.wait_ge(share_done, t + 1)
                        wait(dve, h_done, n)
                        nc.vector.tensor_tensor(product[:, :], gated[slot][:, :], share[parity][:, :],
                                                ALU.mult).then_inc(product_done, 1)
                        dve.wait_ge(product_done, n + 1)
                        dve.wait_ge(up_done, n + 1)
                        wait(dve, low_done, n - 1)
                        nc.vector.tensor_tensor(h[slot][:, :], product[:, :], up[slot][:, :],
                                                ALU.mult).then_inc(h_done, 1)
                    else:
                        dve.wait_ge(up_done, n + 1)
                        wait(dve, low_done, n - 1)
                        nc.vector.tensor_tensor(h[slot][:, :], gated[slot][:, :], up[slot][:, :],
                                                ALU.mult).then_inc(h_done, 1)
                    if u == LAG - 1 and not is_first(t):
                        add(t - 1)
                    prepare_next(steps, prepare, t, parity, u)

            over_tiles(dve, tile)
            add(TILES - 1)

        @block.tensor
        def _(pe):
            def prepare(s, t, parity):
                if s == "turn":
                    if routed:
                        wait(pe, router.w_copied, t)
                    norm.turn(pe, t)
                elif s == "back":
                    norm.turn_back(pe, t, parity)
                elif s == "logits":
                    router.logits(pe, t)
                elif s == "w_turn":
                    router.turn(pe, t)

            def rows_of(w, u):
                return w[0][:, u * P:(u + 1) * P], w[1][:, u * P:(u + 1) * P]

            def down(t, u, parity):
                n = t * units + u
                if u == 0:
                    wait(pe, y_added, t)
                pe.wait_ge(high_done, n + 1)
                pe.wait_ge(low_done, n + 1)
                last = u == units - 1
                ins = three_passes(nc, y[:, :], rows_of(w_down, u),
                                   (h_high[u % hold][:, :], h_low[u % hold][:, :]),
                                   start=(u == 0), stop=(last and not routed))
                ins.then_inc(down_done, 1)
                if last:
                    if routed:
                        pe.wait_ge(router.diagonal_done, t + 1)
                        for c in range(CH):
                            ins = nc.tensor.matmul(y[:, c * P:(c + 1) * P],
                                                   norm.rows[parity][:, c * P:(c + 1) * P],
                                                   router.diagonal[parity][:, c, :],
                                                   start=False, stop=True, skip_group_check=True)
                        ins.then_inc(y_done, 1)

            steps = [s for s in ("turn", "back", "logits", "w_turn") if s in at]
            prepare_first(steps, prepare)

            def tile(t, parity):
                x = (norm.high[parity][:, :], norm.low[parity][:, :])
                pe.wait_ge(norm.n_low, t + 1)
                pe.wait_ge(norm.n_high, t + 1)
                for u in range(units):
                    n = t * units + u
                    slot = (parity * units + u) % 2
                    wait(pe, silu_done, n - 1)
                    three_passes(nc, gate[slot][:, :], rows_of(w_gate, u),
                                 x).then_inc(gate_done, 1)
                    wait(pe, h_done, n - 1)
                    three_passes(nc, up[slot][:, :], rows_of(w_up, u), x).then_inc(up_done, 1)
                    if routed and u == 0:
                        pe.wait_ge(router.w_copied, t + 1)
                        nc.tensor.matmul(share[parity][:, :], k.sel[:, :],
                                         router.turned[parity][:, :],
                                         start=True, stop=True).then_inc(share_done, 1)
                    if u >= LAG:
                        down(t, u - LAG, parity)
                    elif not is_first(t):
                        down(t - 1, units - LAG + u, 1 - parity)
                    prepare_next(steps, prepare, t, parity, u)

            over_tiles(pe, tile)
            for u in range(units - LAG, units):
                down(TILES - 1, u, (TILES - 1) % 2)


THIRDS_Q = ((0, 3), (1, 3), (2, 2))
PIECES = SEQ // P
HALF = P // 2
UNITS = 2 * PIECES
STEPS = HEADS * PIECES


def head_projection(nc, k, prefix):
    with ExitStack() as ctx:
        m = Memory(nc, ctx, prefix)
        norm = Norm(nc, k, m, m.ps("bank"), m.ps("back"), 2)
        product = [[m.ps(f"{x}{i}") for i in range(2)] for x in "qk"]
        v_bank = m.ps("v")
        biased = [m.sb(f"biased{x}", [P, TILE], F32) for x in "qk"]
        rest = [m.sb(f"rest{x}", [P, TILE], F32) for x in "qk"]
        thirds = [[m.sb(f"thirds{x}{i}", [P, 3, TILE], BF16) for i in range(2)] for x in "qk"]
        x_saved, v_done, v_added = m.sems("x_saved v_done v_added")
        qk_done, full_done, first_done, rest_done, second_done, third_done = [
            [m.sem(f"{name}_{x}") for x in "qk"] for name in
            ("qk_done", "full_done", "first_done", "rest_done", "second_done", "third_done")]
        stored = [[m.sem(f"stored_{x}{i}") for i in range(2)] for x in "qk"]
        block = m.block()

        def in_tiles(t, ahead):
            return t + ahead < TILES if isinstance(t, int) else True

        @block.sync
        def _(sync):
            sync.dma_start(k.x_dram, k.xT[:, :]).then_inc(x_saved, 16)

            def tile(t, parity):
                for x in range(2):
                    wait_first(sync, third_done[x], t + 1)
                    for n in range(3):
                        out = k.thirds_dram[x][n]
                        at = out[:, :, t, :] if isinstance(t, int) else out[:, :, bass.ds(t, 1), :]
                        sync.dma_start(at, thirds[x][parity][:, n, :].rearrange(
                            "p (c q) -> p c q", c=PIECES)).then_inc(stored[x][parity], 16)

            over_tiles(sync, tile)
            for x in range(2):
                for parity in range(2):
                    sync.wait_ge(stored[x][parity], 16 * 3 * TILES // 2)

        @block.scalar
        def _(act):
            def tile(t, parity):
                if in_tiles(t, 2):
                    norm.copy_in(act, t + 2)
                for x in range(2):
                    act.wait_ge(qk_done[x], t + 1)
                    wait(act, rest_done[x], t)
                    nc.scalar.activation(biased[x][:, :], product[x][parity][:, :], ACT.Identity,
                                         bias=k.biases[:, x:x + 1]).then_inc(full_done[x], 1)
                    if isinstance(t, int):
                        wait(act, stored[x][parity], 48 * (t // 2))
                    else:
                        act.wait_ge(stored[x][parity], (t - parity) * 24)
                    nc.scalar.activation(thirds[x][parity][:, 0, :], product[x][parity][:, :],
                                         ACT.Identity,
                                         bias=k.biases[:, x:x + 1]).then_inc(first_done[x], 1)
                    if x == 0 and not is_last(t):
                        wait(act, v_done, t)
                        norm.cut_high(act, t + 1, 1 - parity)

            norm.copy_in(act, 0)
            norm.copy_in(act, 1)
            norm.cut_high(act, 0, 0)
            over_tiles(act, tile)

        @block.gpsimd
        def _(pool):
            def tile(t, parity):
                if in_tiles(t, 2):
                    norm.deviation(pool, t + 2)
                for x in range(2):
                    pool.wait_ge(second_done[x], t + 1)
                    nc.gpsimd.tensor_tensor(thirds[x][parity][:, 2, :], rest[x][:, :],
                                            thirds[x][parity][:, 1, :],
                                            ALU.subtract).then_inc(third_done[x], 1)

            norm.deviation(pool, 0)
            norm.deviation(pool, 1)
            over_tiles(pool, tile)

        @block.vector
        def _(dve):
            def tile(t, parity):
                if in_tiles(t, 2):
                    norm.moments(dve, t + 2)
                    norm.aggregate(dve, t + 2)
                for x in range(2):
                    dve.wait_ge(full_done[x], t + 1)
                    dve.wait_ge(first_done[x], t + 1)
                    wait(dve, third_done[x], t)
                    nc.vector.tensor_tensor(rest[x][:, :], biased[x][:, :],
                                            thirds[x][parity][:, 0, :],
                                            ALU.subtract).then_inc(rest_done[x], 1)
                    dve.wait_ge(rest_done[x], t + 1)
                    nc.vector.tensor_copy(thirds[x][parity][:, 1, :],
                                          rest[x][:, :]).then_inc(second_done[x], 1)
                    if x == 0 and not is_last(t):
                        norm.cut_low(dve, t + 1, 1 - parity)
                    if x == 0 and in_tiles(t, 2):
                        norm.norm_rows(dve, t + 2, parity)
                dve.wait_ge(v_done, t + 1)
                dve.wait_ge(x_saved, 16)
                dve.wait_ge(norm.x_copied, t + 1)
                nc.vector.tensor_tensor(chunks(column(k.xT, t)), chunks(v_bank[:, :]),
                                        k.bv_row[:, :].unsqueeze(1).broadcast_to([P, CH, P]),
                                        ALU.add).then_inc(v_added, 1)

            for t in range(2):
                norm.moments(dve, t)
                norm.aggregate(dve, t)
                norm.norm_rows(dve, t, t)
            norm.cut_low(dve, 0, 0)
            over_tiles(dve, tile)

        @block.tensor
        def _(pe):
            def tile(t, parity):
                pe.wait_ge(norm.n_copied, t + 1)
                pe.wait_ge(norm.n_high, t + 1)
                pe.wait_ge(norm.n_low, t + 1)
                for x in range(2):
                    wait(pe, first_done[x], t - 1)
                    wait(pe, full_done[x], t - 1)
                    three_passes(nc, product[x][parity][:, :], k.proj_part(x),
                                 (norm.high[parity][:, :], norm.low[parity][:, :])
                                 ).then_inc(qk_done[x], 1)
                    if x == 0 and in_tiles(t, 2):
                        norm.turn(pe, t + 2)
                    if x == 0 and not is_last(t):
                        norm.turn_back(pe, t + 1, 1 - parity)
                wait(pe, v_added, t)
                for c in range(CH):
                    part = nc.tensor.matmul(v_bank[:, c * P:(c + 1) * P],
                                            norm.full[parity][:, c * P:(c + 1) * P],
                                            k.wv_full[:, 0:P], start=True, stop=True)
                part.then_inc(v_done, 1)

            norm.turn(pe, 0)
            norm.turn(pe, 1)
            norm.turn_back(pe, 0, 0)
            over_tiles(pe, tile)


def batch_attention(nc, k, prefix):
    BUFS = 4
    LAG = 3
    with ExitStack() as ctx:
        m = Memory(nc, ctx, prefix)
        score = [m.ps(f"score{i}", (P, BATCH * HALF)) for i in range(3)]
        heads_bank = m.ps("heads")
        keys = m.sb("keys", [P, PIECES, BATCH * P], BF16)
        queries = m.sb("queries", [P, 3, BATCH * P], BF16)
        e = [m.sb(f"e{i}", [P, BATCH, P], F32) for i in range(BUFS)]
        top = [m.sb(f"top{i}", [P, HALF], F32R) for i in range(2)]
        total = [m.sb(f"total{i}", [P, P], F32) for i in range(2)]
        log = m.sb("log", [P, P], F32)
        inverse = [m.sb(f"inverse{i}", [P, P], F32) for i in range(2)]
        values = m.sb("values", [P, PIECES, BATCH, 32], F32)
        heads_out = m.sb("heads_out", [P, 3, TILE], F32)
        minus = m.sb("minus", [P, P], F32R)
        (keys_padded, queries_padded, zeroed, minus_set, queries_loaded, stored, scored, top_done,
         shifted, e_done, summed, log_done, inverse_done, normed, v_copied, weighted,
         copied) = m.sems("keys_padded queries_padded zeroed minus_set queries_loaded stored "
                          "scored top_done shifted e_done summed log_done inverse_done normed "
                          "v_copied weighted copied")
        keys_loaded = [m.sem(f"keys_loaded{i}") for i in range(PIECES)]
        v = k.xT[:, :].rearrange("p (b c n) -> p b c n", b=BATCH, c=PIECES)
        block = m.block()

        def rows(head):
            return slice(head * DK, (head + 1) * DK) if isinstance(head, int) else \
                bass.ds(head * DK, DK)

        @block.sync
        def _(sync):
            def load_keys(head, c):
                first = 0
                for count in (3, 3, 2):
                    for n in range(count):
                        sync.dma_start(keys[first:first + DK, c, :],
                                       k.thirds_dram[1][n, rows(head), c, :, :].rearrange(
                                           "d b q -> d (b q)")).then_inc(keys_loaded[c], 16)
                        first += DK

            def place(tensor, rows_, step):
                if isinstance(step, int):
                    return tensor[rows_, step % 3, :]
                return tensor[rows_, bass.ds(step % 3, 1), :].squeeze(1)

            def load_queries(step, head, c):
                wait_first(sync, queries_loaded, step * (16 * TERMS))
                first = 0
                for n, count in THIRDS_Q:
                    for _ in range(count):
                        sync.dma_start(place(queries, slice(first, first + DK), step),
                                       k.thirds_dram[0][n, rows(head), c, :, :].rearrange(
                                           "d b q -> d (b q)")).then_inc(queries_loaded, 16)
                        first += DK

            def store(step, head, c):
                wait_first(sync, copied, step + 1)
                wait_first(sync, stored, step * 64)
                out = k.heads_dram[rows(head), :].rearrange("d (j g c q) -> d g j c q",
                                                            g=4, c=PIECES, q=P)
                for g in range(4):
                    sync.dma_start(out[:, g, :, c, :],
                                   place(heads_out, slice(32 * g, 32 * g + DK), step).rearrange(
                                       "d (j q) -> d j q", j=4)).then_inc(stored, 16)

            def head_steps(head, first, last):
                for c in range(PIECES):
                    step = head * PIECES + c
                    if c == PIECES - 1 and not last:
                        for piece in range(PIECES):
                            wait_first(sync, scored, step * UNITS + 2 * piece + 2)
                            load_keys(head + 1, piece)
                    if not (last and c >= PIECES - 2):
                        wait_first(sync, scored, step * UNITS)
                        load_queries(step + 2, head + (c + 2) // PIECES, (c + 2) % PIECES)
                    if c:
                        store(step - 1, head, c - 1)
                    elif not first:
                        store(step - 1, head - 1, PIECES - 1)

            for c in range(PIECES):
                load_keys(0, c)
                if c < 2:
                    load_queries(c, 0, c)
            head_steps(0, True, False)
            with sync.Fori(1, HEADS - 1) as head:
                head_steps(head, False, False)
            head_steps(HEADS - 1, False, True)
            store(STEPS - 1, HEADS - 1, PIECES - 1)
            sync.wait_ge(stored, 16 * 4 * STEPS)

        def over_steps(eng, body):
            for r in range(3):
                body(r, r)
            with eng.Fori(1, STEPS // 3) as i:
                for r in range(3):
                    body(i * 3 + r, r)
            body(STEPS - 1, 0)

        def begins(s):
            return isinstance(s, int) and s == 0

        def ends(s):
            return isinstance(s, int) and s == STEPS - 1

        @block.tensor
        def _(pe):
            def scores(n, r, u):
                c, half, slot = u // 2, u % 2, (2 * r + u) % 3
                wait(pe, e_done, n - 2)
                for b in range(BATCH):
                    part = nc.tensor.matmul(
                        score[slot][:, b * HALF:(b + 1) * HALF], keys[:, c, b * P:(b + 1) * P],
                        queries[:, r, b * P + half * HALF:b * P + (half + 1) * HALF],
                        start=(b % 8 == 0), stop=False, skip_group_check=True)
                part.then_inc(scored, 1)

            def shift(n, slot, half):
                pe.wait_ge(top_done, n + 1)
                for bank in range(2):
                    part = nc.tensor.matmul(
                        score[slot][:, bank * 512:(bank + 1) * 512], minus[:, :],
                        top[half][:, :].unsqueeze(1).broadcast_to([P, 8, HALF]),
                        start=False, stop=True, skip_group_check=True)
                part.then_inc(shifted, 1)

            def values_of(pair, c, step, head):
                pe.wait_ge(normed, pair + 1)
                pe.wait_ge(v_copied, head * PIECES + c + 1)
                if c == 0:
                    wait(pe, copied, step)
                for b in range(BATCH):
                    g, j = b % 4, b // 4
                    part = nc.tensor.matmul(
                        heads_bank[32 * g:32 * g + 32, j * P:(j + 1) * P], values[:, c, b, :],
                        e[c][:, b, :], start=(c == 0 and j == 0), stop=(c == PIECES - 1),
                        skip_group_check=True)
                part.then_inc(weighted, 1)

            def score_unit(s, r, u):
                if u % 2 == 0:
                    pe.wait_ge(queries_loaded, (s + 1) * (16 * TERMS))
                    pe.wait_ge(keys_loaded[u // 2], (s // PIECES + 1) * (16 * TERMS))
                scores(s * UNITS + u, r, u)

            def step(s, r):
                for c in range(PIECES):
                    for u in (2 * c, 2 * c + 1):
                        shift(s * UNITS + u, (2 * r + u) % 3, u % 2)
                    for u in (2 * c + 2, 2 * c + 3):
                        if u < UNITS:
                            score_unit(s, r, u)
                        elif not ends(s):
                            score_unit(s + 1, (r + 1) % 3, u - UNITS)
                    if c == LAG:
                        values_of(s * PIECES, 0, s, s // PIECES)
                    elif not begins(s):
                        values_of(s * PIECES + c - LAG, c + PIECES - LAG, s - 1,
                                  (s - 1) // PIECES)

            pe.wait_ge(minus_set, 1)
            pe.wait_ge(keys_padded, 1)
            pe.wait_ge(queries_padded, 1)
            for u in range(2):
                score_unit(0, 0, u)
            over_steps(pe, step)
            for c in range(PIECES - LAG, PIECES):
                values_of((STEPS - 1) * PIECES + c, c, STEPS - 1, HEADS - 1)

        @block.vector
        def _(dve):
            def largest(n, slot, half):
                dve.wait_ge(scored, n + 1)
                wait(dve, shifted, n - 1)
                nc.vector.tensor_reduce(
                    top[half][:, :], score[slot][:, :].rearrange("p (b q) -> p q b", b=BATCH),
                    AX.X, ALU.max).then_inc(top_done, 1)

            def add_up(pair, slot):
                dve.wait_ge(e_done, (pair + 1) * 2)
                wait(dve, log_done, pair - 1)
                nc.vector.tensor_reduce(total[slot % 2][:, :], e[slot][:, :, :].rearrange("p b q -> p q b"),
                                        AX.X, ALU.add).then_inc(summed, 1)

            def step(s, r):
                for c in range(PIECES):
                    pair = s * PIECES + c
                    for u in (2 * c, 2 * c + 1):
                        largest(s * UNITS + u, (2 * r + u) % 3, u % 2)
                    if c or not begins(s):
                        add_up(pair - 1, (c - 1) % PIECES)

            nc.vector.memset(keys[STACK:P, :, :], 0.0).then_inc(keys_padded, 1)
            nc.vector.tensor_scalar(minus[:, :], k.ident[:, :], -1.0, None,
                                    ALU.mult).then_inc(minus_set, 1)
            over_steps(dve, step)
            add_up(STEPS * PIECES - 1, PIECES - 1)

        @block.scalar
        def _(act):
            def copy_heads(s, r):
                act.wait_ge(weighted, (s + 1) * PIECES)
                wait(act, stored, (s - 2) * 64)
                nc.scalar.activation(heads_out[:, r, :], heads_bank[:, :],
                                     ACT.Copy).then_inc(copied, 1)

            def invert(pair, slot):
                act.wait_ge(summed, pair + 1)
                wait(act, inverse_done, pair)
                nc.scalar.activation(log[:, :], total[slot % 2][:, :], ACT.Ln).then_inc(log_done, 1)
                act.wait_ge(log_done, pair + 1)
                wait(act, normed, pair - 1)
                nc.scalar.activation(inverse[slot % 2][:, :], log[:, :], ACT.Exp,
                                     scale=-1.0).then_inc(inverse_done, 1)

            def step(s, r):
                for u in range(UNITS):
                    c, half, slot = u // 2, u % 2, (2 * r + u) % 3
                    act.wait_ge(shifted, s * UNITS + u + 1)
                    wait(act, weighted, s * PIECES + c - BUFS + 1)
                    nc.scalar.activation(
                        e[c][:, :, half * HALF:(half + 1) * HALF],
                        score[slot][:, :].rearrange("p (b q) -> p b q", b=BATCH),
                        ACT.Exp).then_inc(e_done, 1)
                    if half and (c or not begins(s)):
                        invert(s * PIECES + c - 1, (c - 1) % PIECES)
                    if u == UNITS - 1 and not begins(s):
                        copy_heads(s - 1, (r - 1) % 3)

            nc.scalar.preload_act_table_set("natural_log_exp_and_others")
            over_steps(act, step)
            invert(STEPS * PIECES - 1, PIECES - 1)
            copy_heads(STEPS - 1, 0)

        @block.gpsimd
        def _(pool):
            def head_steps(head):
                for c in range(PIECES):
                    for piece in range(PIECES):
                        pair = (head * PIECES + c) * PIECES + piece
                        if c == 0:
                            wait(pool, weighted, pair - PIECES + 1)
                            at = rows(head)
                            nc.gpsimd.tensor_copy(values[:, piece, :, 0:DK],
                                                  v[:, :, piece, at]).then_inc(v_copied, 1)
                        pool.wait_ge(inverse_done, pair + 1)
                        nc.gpsimd.tensor_tensor(
                            e[piece][:, :, :], e[piece][:, :, :],
                            inverse[piece % 2][:, :].unsqueeze(1).broadcast_to([P, BATCH, P]),
                            ALU.mult).then_inc(normed, 1)

            nc.gpsimd.memset(queries[STACK:P, :, :], 0.0).then_inc(queries_padded, 1)
            pool.wait_ge(queries_padded, 1)
            nc.gpsimd.memset(values[:, :, :, :], 0.0).then_inc(zeroed, 1)
            pool.wait_ge(zeroed, 1)
            head_steps(0)
            with pool.Fori(1, HEADS) as head:
                head_steps(head)


def head_output(nc, k, prefix):
    PART = TILES // 4
    with ExitStack() as ctx:
        m = Memory(nc, ctx, prefix)
        heads = m.sb("heads", [P, TOKENS], F32)
        high = [m.sb(f"high{i}", [P, TILE], F32R) for i in range(2)]
        low = [m.sb(f"low{i}", [P, TILE], F32R) for i in range(2)]
        y = [m.ps(f"y{i}") for i in range(2)]
        high_done, low_done, y_done, added = m.sems("high_done low_done y_done added")
        heads_loaded, x_loaded = [[m.sem(f"{n}_loaded{i}") for i in range(TILES // PART)]
                                  for n in ("heads", "x")]
        block = m.block()

        def over_parts(eng, loaded, body):
            for part, sem in enumerate(loaded):
                eng.wait_ge(sem, 16)
                if part == 0:
                    for t in range(PART):
                        body(t, t % 2)
                else:
                    with eng.Fori(part * PART // 2, (part + 1) * PART // 2) as i:
                        body(i * 2, 0)
                        body(i * 2 + 1, 1)

        @block.sync
        def _(sync):
            for part in range(TILES // PART):
                sync.dma_start(column(heads, part, PART * TILE),
                               column(k.heads_dram, part, PART * TILE)
                               ).then_inc(heads_loaded[part], 16)

        @block.scalar
        def _(act):
            def tile(t, parity):
                wait(act, y_done, t - 1)
                nc.scalar.activation(high[parity][:, :], column(heads, t),
                                     ACT.Copy).then_inc(high_done, 1)

            for part in range(TILES // PART):
                act.dma_start(column(k.xT, part, PART * TILE),
                              column(k.x_dram, part, PART * TILE)).then_inc(x_loaded[part], 16)
            over_parts(act, heads_loaded, tile)

        @block.gpsimd
        def _(pool):
            def tile(t, parity):
                pool.wait_ge(high_done, t + 1)
                wait(pool, y_done, t - 1)
                nc.gpsimd.tensor_tensor(low[parity][:, :], column(heads, t), high[parity][:, :],
                                        ALU.subtract).then_inc(low_done, 1)

            over_parts(pool, heads_loaded, tile)

        @block.vector
        def _(dve):
            def tile(t, parity):
                dve.wait_ge(y_done, t + 1)
                nc.vector.scalar_tensor_tensor(column(k.xT, t), y[parity][:, :], k.biases[:, 3:4],
                                               column(k.xT, t), ALU.add,
                                               ALU.add).then_inc(added, 1)

            over_parts(dve, x_loaded, tile)

        @block.tensor
        def _(pe):
            def tile(t, parity):
                pe.wait_ge(low_done, t + 1)
                pe.wait_ge(high_done, t + 1)
                wait(pe, added, t - 1)
                three_passes(nc, y[parity][:, :], k.proj_part(3),
                             (high[parity][:, :], low[parity][:, :])).then_inc(y_done, 1)

            over_tiles(pe, tile)


def sequence_attention(nc, k, prefix):
    with ExitStack() as ctx:
        m = Memory(nc, ctx, prefix)
        norm = Norm(nc, k, m, m.ps("bank"))
        project = [m.ps(f"project{i}") for i in range(2)]
        score = [m.ps(f"score{i}") for i in range(2)]
        turned_bank = [m.ps(f"turned_bank{i}") for i in range(2)]
        y = m.ps("y")
        full = [m.sb(f"full_{x}", [P, TILE], F32) for x in "qk"]
        high = [[m.sb(f"high_{x}{i}", [P, TILE], F32R) for i in range(2)] for x in "qk"]
        low = [[m.sb(f"low_{x}{i}", [P, TILE], F32R) for i in range(2)] for x in "qk"]
        v = [m.sb(f"v{i}", [P, TILE], F32) for i in range(2)]
        top = [m.sb(f"top{i}", [P, 1], F32) for i in range(2)]
        e = [m.sb(f"e{i}", [P, SEQ], F32) for i in range(2)]
        total = [m.sb(f"total{i}", [P, 1], F32) for i in range(2)]
        inverse = [m.sb(f"inverse{i}", [P, 1], F32) for i in range(2)]
        weight = [m.sb(f"weight{i}", [P, SEQ], F32) for i in range(2)]
        turned = [m.sb(f"turned{i}", [P, SEQ], F32) for i in range(2)]
        (v_done, v_copied, scored, top_done, e_done, inverse_done, scaled, w_turned, w_copied,
         weighted, added) = m.sems("v_done v_copied scored top_done e_done inverse_done scaled "
                                   "w_turned w_copied weighted added")
        qk_done, full_done, high_done, low_done = [
            [m.sem(f"{name}_{x}") for x in "qk"] for name in
            ("qk_done", "full_done", "high_done", "low_done")]
        block = m.block()

        def has_second_next(t):
            return not isinstance(t, int) or t < TILES - 2

        @block.scalar
        def _(act):
            def cut(t, parity):
                for x in range(2):
                    act.wait_ge(qk_done[x], t + 1)
                    wait(act, low_done[x], t)
                    nc.scalar.activation(full[x][:, :], project[x][:, :],
                                         ACT.Copy).then_inc(full_done[x], 1)
                    wait(act, scored, (t - 1) * PIECES)
                    nc.scalar.activation(high[x][parity][:, :], project[x][:, :],
                                         ACT.Copy).then_inc(high_done[x], 1)

            def copy_v(t, parity):
                act.wait_ge(v_done, t + 1)
                wait(act, weighted, (t - 1) * PIECES)
                nc.scalar.activation(v[parity][:, :], project[0][:, :],
                                     ACT.Copy).then_inc(v_copied, 1)

            def copy_turned(n, slot):
                act.wait_ge(w_turned, n + 1)
                wait(act, weighted, n - 1)
                nc.scalar.activation(turned[slot][:, :], turned_bank[slot][:, :],
                                     ACT.Copy).then_inc(w_copied, 1)

            def tile(t, parity):
                for c in range(PIECES):
                    n, slot = t * PIECES + c, c % 2
                    act.wait_ge(top_done, n + 1)
                    wait(act, inverse_done, n - 1)
                    wait(act, scaled, n - 1)
                    nc.scalar.activation(e[slot][:, :], score[slot][:, :], ACT.Exp,
                                         bias=top[slot][:, 0:1],
                                         accum_out=total[slot][:, 0:1]).then_inc(e_done, 1)
                    if c >= 2 or not is_first(t):
                        copy_turned(n - 2, slot)
                    if not is_last(t):
                        if c == 1:
                            wait(act, v_done, t + 1)
                            norm.cut_high(act, t + 1, 1 - parity)
                        elif c == 2:
                            cut(t + 1, 1 - parity)
                        elif c == 3:
                            copy_v(t + 1, 1 - parity)
                    if c == 1 and has_second_next(t):
                        norm.copy_in(act, t + 2)

            norm.copy_in(act, 0)
            norm.cut_high(act, 0, 0)
            cut(0, 0)
            copy_v(0, 0)
            norm.copy_in(act, 1)
            over_tiles(act, tile)
            copy_turned(TILES * PIECES - 2, 0)
            copy_turned(TILES * PIECES - 1, 1)

        @block.gpsimd
        def _(pool):
            def cut_q(t, parity):
                pool.wait_ge(full_done[0], t + 1)
                pool.wait_ge(high_done[0], t + 1)
                nc.gpsimd.tensor_tensor(low[0][parity][:, :], full[0][:, :],
                                        high[0][parity][:, :],
                                        ALU.subtract).then_inc(low_done[0], 1)

            def tile(t, parity):
                if not is_last(t):
                    cut_q(t + 1, 1 - parity)
                if has_second_next(t):
                    norm.deviation(pool, t + 2)

            norm.deviation(pool, 0)
            cut_q(0, 0)
            norm.deviation(pool, 1)
            over_tiles(pool, tile)

        @block.vector
        def _(dve):
            def largest(n, slot):
                dve.wait_ge(scored, n + 1)
                wait(dve, e_done, n - 1)
                nc.vector.tensor_reduce(top[slot][:, 0:1], score[slot][:, :], AX.X, ALU.max,
                                        negate=True).then_inc(top_done, 1)

            def scale(n, slot):
                dve.wait_ge(e_done, n + 1)
                nc.vector.reciprocal(inverse[slot][:, 0:1],
                                     total[slot][:, 0:1]).then_inc(inverse_done, 1)
                dve.wait_ge(inverse_done, n + 1)
                wait(dve, w_turned, n - 1)
                nc.vector.tensor_scalar(weight[slot][:, :], e[slot][:, :], inverse[slot][:, 0:1],
                                        NORM, ALU.mult, ALU.mult).then_inc(scaled, 1)

            def cut_k(t, parity):
                dve.wait_ge(full_done[1], t + 1)
                dve.wait_ge(high_done[1], t + 1)
                nc.vector.tensor_tensor(low[1][parity][:, :], full[1][:, :],
                                        high[1][parity][:, :],
                                        ALU.subtract).then_inc(low_done[1], 1)

            def add(t):
                dve.wait_ge(weighted, (t + 1) * PIECES)
                nc.vector.tensor_tensor(column(k.xT, t), y[:, :], column(k.xT, t),
                                        ALU.add).then_inc(added, 1)

            def tile(t, parity):
                for c in range(PIECES):
                    n, slot = t * PIECES + c, c % 2
                    largest(n, slot)
                    if c or not is_first(t):
                        scale(n - 1, 1 - slot)
                    if c == 2 and not is_first(t):
                        add(t - 1)
                    if not is_last(t):
                        if c == 0:
                            norm.norm_rows(dve, t + 1, 1 - parity)
                        elif c == 1:
                            norm.cut_low(dve, t + 1, 1 - parity)
                        elif c == 3:
                            cut_k(t + 1, 1 - parity)
                    if c == 3 and has_second_next(t):
                        norm.moments(dve, t + 2)
                        norm.aggregate(dve, t + 2)

            norm.moments(dve, 0)
            norm.aggregate(dve, 0)
            norm.norm_rows(dve, 0, 0)
            norm.cut_low(dve, 0, 0)
            cut_k(0, 0)
            norm.moments(dve, 1)
            norm.aggregate(dve, 1)
            over_tiles(dve, tile)
            scale(TILES * PIECES - 1, 1)
            add(TILES - 1)

        @block.tensor
        def _(pe):
            def projections(t, parity):
                pe.wait_ge(norm.n_copied, t + 1)
                pe.wait_ge(norm.n_high, t + 1)
                pe.wait_ge(norm.n_low, t + 1)
                for x in range(2):
                    if x == 0:
                        wait(pe, v_copied, t)
                    else:
                        wait(pe, high_done[x], t)
                    three_passes(nc, project[x][:, :], k.proj_part(4 + x),
                                 (norm.high[parity][:, :], norm.low[parity][:, :])
                                 ).then_inc(qk_done[x], 1)

            def project_v(t):
                pe.wait_ge(high_done[0], t + 1)
                pe.wait_ge(full_done[0], t + 1)
                for c in range(CH):
                    part = nc.tensor.matmul(project[0][:, c * P:(c + 1) * P],
                                            norm.full[0][:, c * P:(c + 1) * P],
                                            k.wv_full[:, P:2 * P], start=True, stop=True)
                part.then_inc(v_done, 1)

            def scores(n, c, parity):
                wait(pe, e_done, n - 1)
                (qh, ql), (kh, kl) = [(high[x][parity], low[x][parity]) for x in range(2)]
                three_passes(nc, score[c % 2][:, :],
                             (qh[:, c * P:(c + 1) * P], ql[:, c * P:(c + 1) * P]),
                             (kh[:, :], kl[:, :])).then_inc(scored, 1)

            def turn_weights(n, slot):
                pe.wait_ge(scaled, n + 1)
                wait(pe, w_copied, n - 1)
                for c in range(PIECES):
                    part = nc.tensor.transpose(turned_bank[slot][:, c * P:(c + 1) * P],
                                               weight[slot][:, c * P:(c + 1) * P], k.ident[:, :])
                part.then_inc(w_turned, 1)

            def weigh(t, c, parity):
                pe.wait_ge(w_copied, t * PIECES + c + 1)
                if c == 0:
                    pe.wait_ge(v_copied, t + 1)
                    wait(pe, added, t)
                for piece in range(PIECES):
                    part = nc.tensor.matmul(y[:, c * P:(c + 1) * P],
                                            v[parity][:, piece * P:(piece + 1) * P],
                                            turned[c % 2][:, piece * P:(piece + 1) * P],
                                            start=(piece == 0), stop=(piece == PIECES - 1))
                part.then_inc(weighted, 1)

            def tile(t, parity):
                for x in range(2):
                    pe.wait_ge(high_done[x], t + 1)
                    pe.wait_ge(low_done[x], t + 1)
                for c in range(PIECES):
                    n = t * PIECES + c
                    scores(n, c, parity)
                    if c == 3 and has_second_next(t):
                        norm.turn(pe, t + 2)
                    if c >= 2 or not is_first(t):
                        turn_weights(n - 2, c % 2)
                    if c == 1 and not is_last(t):
                        norm.turn_back(pe, t + 1, 1 - parity)
                    if c >= 3:
                        weigh(t, c - 3, parity)
                    elif not is_first(t):
                        weigh(t - 1, c + 1, 1 - parity)
                    if not is_last(t):
                        if c == 2:
                            projections(t + 1, 1 - parity)
                        elif c == 3:
                            project_v(t + 1)

            norm.turn(pe, 0)
            norm.turn_back(pe, 0, 0)
            projections(0, 0)
            project_v(0)
            norm.turn(pe, 1)
            over_tiles(pe, tile)
            turn_weights(TILES * PIECES - 2, 0)
            weigh(TILES - 1, 1, 1)
            turn_weights(TILES * PIECES - 1, 1)
            weigh(TILES - 1, 2, 1)
            weigh(TILES - 1, 3, 1)


def program(nc, ins, out, phases):
    with ExitStack() as ctx:
        m = Memory(nc, ctx, "")
        k = Kept(m)
        load_block(nc, k, ins)
        for n, phase in enumerate(phases):
            ends = dict(source=ins["xT"] if n == 0 else None,
                        sink=out if n == len(phases) - 1 else None)
            if phase == "moe":
                gated_block(nc, k, f"b{n}_", SLICES, k.wg, k.wu, k.wd, True, **ends)
            elif phase == "ffn":
                gated_block(nc, k, f"b{n}_", HCH, k.ffn_part(0), k.ffn_part(1), k.ffn_part(2),
                            False, **ends)
            elif phase == "heads":
                head_projection(nc, k, f"b{n}_")
                batch_attention(nc, k, f"b{n}c_")
                head_output(nc, k, f"b{n}d_")
            elif phase == "attention":
                sequence_attention(nc, k, f"b{n}_")


_PROJECTIONS = ["L0_attn_Wq", "L0_attn_Wk", "L0_attn_Wv", "L0_attn_Wo",
                "L1_attn_Wq", "L1_attn_Wk", "L1_attn_Wv"]
PHASES = ("moe", "heads", "moe", "ffn", "attention", "ffn")


def kernel(**inputs):
    import ml_dtypes
    import concourse.bacc as bacc
    from concourse.bass_utils import run_bass_kernel_spmd

    given = {name: np.asarray(value) for name, value in inputs.items()}
    gate_up, down = given["L0_ffn_gate_up_proj"], given["L0_ffn_down_proj"]

    def slices(w):
        return w.transpose(2, 0, 1).reshape(P, ROUTED, SLICES, SLICE).transpose(
            0, 2, 1, 3).reshape(P, -1)

    def by_chunk(w):
        return w.T.reshape(HCH, P, P).transpose(1, 0, 2).reshape(P, HIDDEN)

    third_row, inner_row = np.arange(3 * ROUTED)[:, None], np.arange(P)[None, :]
    arrays = {
        "xT": given["L0_attn_x"].reshape(TOKENS, P).T,
        "wg": slices(gate_up[:ROUTED, :INNER]),
        "wu": slices(gate_up[:ROUTED, INNER:]),
        "wd": down.transpose(0, 2, 1).reshape(ROUTED, SLICES, SLICE, P).transpose(
            0, 2, 1, 3).reshape(P, -1),
        "wc": given["L0_ffn_classifier_weight"].T,
        "bias": given["L0_ffn_e_score_correction_bias"],
        "proj": np.concatenate([given[name].T for name in _PROJECTIONS], axis=1),
        "ffn": np.concatenate([given["L1_ffn_w_gate"].T, given["L1_ffn_w_up"].T,
                               by_chunk(given["L1_ffn_w_down"])], axis=1),
        "biases": np.stack([given[f"L0_attn_b{x}"] for x in "qkvo"], axis=1),
        "wv_full": np.concatenate([given["L0_attn_Wv"].T, given["L1_attn_Wv"].T], axis=1),
        "bv": given["L0_attn_bv"],
        "sel": (third_row % ROUTED == inner_row // SLICE).astype(ml_dtypes.bfloat16),
        "ident": np.eye(P, dtype=np.float32),
        "identb": np.eye(P, dtype=ml_dtypes.bfloat16),
    }
    arrays = {name: np.ascontiguousarray(a) for name, a in arrays.items()}

    nc = bacc.Bacc("TRN2", target_bir_lowering=False, num_devices=1)
    ins = {name: nc.dram_tensor("in_" + name, a.shape, mybir.dt.from_np(a.dtype),
                                kind="ExternalInput").ap() for name, a in arrays.items()}
    out = nc.dram_tensor("out_xT", (P, TOKENS), F32, kind="ExternalOutput").ap()
    program(nc, ins, out, PHASES)
    run = run_bass_kernel_spmd(nc, [{"in_" + name: a for name, a in arrays.items()}],
                               core_ids=[0])
    return run.results[0]["out_xT"].T.reshape(BATCH, SEQ, P)
```
